# Optimizing a Trainium2 kernel written in Bass

```python
import numpy as np
import jax
import jax.numpy as jnp

def _softmax(x, axis=-1):
    return jax.nn.softmax(x, axis=axis)

def _gelu(x):
    return jax.nn.gelu(x, approximate=True)

def _silu(x):
    return jax.nn.silu(x)

def _sigmoid(x):
    return jax.nn.sigmoid(x)

def _layernorm(x, axis=-1, eps=1e-05):
    m = jnp.mean(x, axis=axis, keepdims=True)
    v = jnp.var(x, axis=axis, keepdims=True)
    return (x - m) / jnp.sqrt(v + eps)

def _scatter_add(tgt, idx, src, axis=0):
    return tgt.at[idx].add(src)

def _segment_sum(src, seg, n):
    return jax.ops.segment_sum(src, seg, n)
kernel_name = 'mk_hybrid_d1_jaxref_r8_bfbb0b'

def setup_inputs(seed: int=0):
    np.random.seed(seed)
    _w = jnp.asarray

    def _L0_attn_a_setup():
        import jax, jax.numpy as jnp
        import numpy as np
        L, B, S, D, N, H = (4, 4, 128, 128, 64, 16)
        DI = 2 * D
        DH = D // H
        DF = 4 * D
        SCALE = 1.0 / np.sqrt(DH)

        def _ln(x, g, b, eps=1e-05):
            mu = x.mean(-1, keepdims=True)
            var = ((x - mu) ** 2).mean(-1, keepdims=True)
            return (x - mu) * jax.lax.rsqrt(var + eps) * g + b

        def _mamba(x, A_log, Dp, W_in, b_in, W_xp, b_xp, W_dt, b_dt, W_out, b_out):
            xr = jnp.einsum('bsd,od->bso', x, W_in) + b_in
            xi, res = jnp.split(xr, 2, axis=-1)
            xi = jax.nn.silu(xi)
            A = -jnp.exp(A_log)
            delta = jax.nn.softplus(jnp.einsum('bsi,di->bsd', xi, W_dt) + b_dt)
            m = delta.mean(-1)
            A_disc = jnp.exp(A[None, None, :] * m[:, :, None])
            u = jnp.einsum('bsi,ni->bsn', xi, W_xp) + b_xp

            def step(state, inp):
                a_t, u_t = inp
                state = a_t * state + u_t
                return (state, state.sum(-1))
            init = jnp.zeros((x.shape[0], A_log.shape[0]), x.dtype)
            _, ssum = jax.lax.scan(step, init, (A_disc.swapaxes(0, 1), u.swapaxes(0, 1)))
            ssum = ssum.swapaxes(0, 1)
            y = ssum[..., None] * xi
            y = y * jax.nn.silu(res)
            y = jnp.einsum('bsi,di->bsd', y, W_out) + b_out
            return y + x * Dp

        def _attn(x, W_qkv, b_qkv, W_ao, b_ao):
            b, s, d = x.shape
            qkv = jnp.einsum('bsd,od->bso', x, W_qkv) + b_qkv
            qkv = qkv.reshape(b, s, 3, H, DH)
            q = jnp.moveaxis(qkv[:, :, 0], 2, 1)
            k = jnp.moveaxis(qkv[:, :, 1], 2, 1)
            v = jnp.moveaxis(qkv[:, :, 2], 2, 1)
            scores = jnp.einsum('bhqd,bhkd->bhqk', q, k) * SCALE
            wts = jax.nn.softmax(scores, axis=-1)
            o = jnp.einsum('bhqk,bhkd->bhqd', wts, v)
            o = jnp.moveaxis(o, 1, 2).reshape(b, s, d)
            return jnp.einsum('bsd,od->bso', o, W_ao) + b_ao

        def _forward(x, A_log, Dp, W_in, b_in, W_xp, b_xp, W_dt, b_dt, W_out, b_out, W_qkv, b_qkv, W_ao, b_ao, g1, be1, g2, be2, W_f1, b_f1, W_f2, b_f2):
            for l in range(L):
                m = _mamba(x, A_log[l], Dp[l], W_in[l], b_in[l], W_xp[l], b_xp[l], W_dt[l], b_dt[l], W_out[l], b_out[l])
                x = _ln(x + m, g1[l], be1[l])
                a = _attn(x, W_qkv[l], b_qkv[l], W_ao[l], b_ao[l])
                x = _ln(x + a, g2[l], be2[l])
                h = jax.nn.gelu(jnp.einsum('bsd,fd->bsf', x, W_f1[l]) + b_f1[l], approximate=False)
                x = x + jnp.einsum('bsf,df->bsd', h, W_f2[l]) + b_f2[l]
            return x
        key = jax.random.key(seed)
        ks = jax.random.split(key, 12)
        w = lambda k, sh: jax.random.normal(k, sh, jnp.float32) * 0.02
        return {'x': jax.random.normal(ks[0], (B, S, D), jnp.float32), 'A_log': jax.random.normal(ks[1], (L, N), jnp.float32), 'Dp': jax.random.normal(ks[2], (L, D), jnp.float32), 'W_in': w(ks[3], (L, 2 * DI, D)), 'b_in': jnp.zeros((L, 2 * DI), jnp.float32), 'W_xp': w(ks[4], (L, N, DI)), 'b_xp': jnp.zeros((L, N), jnp.float32), 'W_dt': w(ks[5], (L, D, DI)), 'b_dt': jnp.zeros((L, D), jnp.float32), 'W_out': w(ks[6], (L, D, DI)), 'b_out': jnp.zeros((L, D), jnp.float32), 'W_qkv': w(ks[7], (L, 3 * D, D)), 'b_qkv': jnp.zeros((L, 3 * D), jnp.float32), 'W_ao': w(ks[8], (L, D, D)), 'b_ao': jnp.zeros((L, D), jnp.float32), 'g1': jnp.ones((L, D), jnp.float32), 'be1': jnp.zeros((L, D), jnp.float32), 'g2': jnp.ones((L, D), jnp.float32), 'be2': jnp.zeros((L, D), jnp.float32), 'W_f1': w(ks[9], (L, DF, D)), 'b_f1': jnp.zeros((L, DF), jnp.float32), 'W_f2': w(ks[10], (L, D, DF)), 'b_f2': jnp.zeros((L, D), jnp.float32)}
    _L0_attn_a_in = _L0_attn_a_setup()

    def _L0_attn_b_setup():
        import math
        import jax, jax.numpy as jnp
        import numpy as np
        B, L, D_MODEL, NHEAD, FACTOR = (8, 512, 128, 16, 5)
        D_HEAD = D_MODEL // NHEAD
        SAMPLE_K = min(L, max(1, FACTOR * int(math.ceil(math.log(max(L, 2))))))
        TOP_U = min(L, max(1, FACTOR * int(math.ceil(math.log(max(L, 2))))))

        def _split_heads(t):
            b, l, _ = t.shape
            return t.reshape(b, l, NHEAD, D_HEAD).transpose(0, 2, 1, 3)
        key = jax.random.key(seed)
        ks = jax.random.split(key, 10)
        x = jax.random.normal(ks[0], (B, L, D_MODEL), dtype=jnp.float32)
        sample_idx = jax.random.randint(ks[1], (SAMPLE_K,), 0, L)
        s = 0.02
        Wq = jax.random.normal(ks[2], (D_MODEL, D_MODEL), dtype=jnp.float32) * s
        Wk = jax.random.normal(ks[3], (D_MODEL, D_MODEL), dtype=jnp.float32) * s
        Wv = jax.random.normal(ks[4], (D_MODEL, D_MODEL), dtype=jnp.float32) * s
        Wo = jax.random.normal(ks[5], (D_MODEL, D_MODEL), dtype=jnp.float32) * s
        bq = jnp.zeros((D_MODEL,), dtype=jnp.float32)
        bk = jnp.zeros((D_MODEL,), dtype=jnp.float32)
        bv = jnp.zeros((D_MODEL,), dtype=jnp.float32)
        bo = jnp.zeros((D_MODEL,), dtype=jnp.float32)
        return {'x': x, 'Wq': Wq, 'bq': bq, 'Wk': Wk, 'bk': bk, 'Wv': Wv, 'bv': bv, 'Wo': Wo, 'bo': bo, 'sample_idx': sample_idx}
    _L0_attn_b_in = _L0_attn_b_setup()

    def _L0_ffn_setup():
        import jax, jax.numpy as jnp
        import numpy as np
        B, S, D = (4, 512, 128)
        H = 512
        RH = 128
        E = 16
        K = 2
        NS = 1

        def _swiglu(x, w1, w2, w3):
            return jax.nn.silu(x @ w1) * (x @ w2) @ w3
        key = jax.random.key(seed)
        ks = jax.random.split(key, 9)
        s = 0.02
        return {'x': jax.random.normal(ks[0], (B, S, D), dtype=jnp.float32), 'router_w': jax.random.normal(ks[1], (D, E), dtype=jnp.float32) * s, 'expert_bias': jnp.zeros((E,), dtype=jnp.float32), 'shared_w1': jax.random.normal(ks[2], (NS, D, H), dtype=jnp.float32) * s, 'shared_w2': jax.random.normal(ks[3], (NS, D, H), dtype=jnp.float32) * s, 'shared_w3': jax.random.normal(ks[4], (NS, H, D), dtype=jnp.float32) * s, 'routed_w1': jax.random.normal(ks[5], (E, D, RH), dtype=jnp.float32) * s, 'routed_w2': jax.random.normal(ks[6], (E, D, RH), dtype=jnp.float32) * s, 'routed_w3': jax.random.normal(ks[7], (E, RH, D), dtype=jnp.float32) * s}
    _L0_ffn_in = _L0_ffn_setup()
    _d = {'L0_attn_a_x': _L0_attn_a_in['x'], 'L0_attn_a_A_log': _L0_attn_a_in['A_log'], 'L0_attn_a_Dp': _L0_attn_a_in['Dp'], 'L0_attn_a_W_in': _L0_attn_a_in['W_in'], 'L0_attn_a_b_in': _L0_attn_a_in['b_in'], 'L0_attn_a_W_xp': _L0_attn_a_in['W_xp'], 'L0_attn_a_b_xp': _L0_attn_a_in['b_xp'], 'L0_attn_a_W_dt': _L0_attn_a_in['W_dt'], 'L0_attn_a_b_dt': _L0_attn_a_in['b_dt'], 'L0_attn_a_W_out': _L0_attn_a_in['W_out'], 'L0_attn_a_b_out': _L0_attn_a_in['b_out'], 'L0_attn_a_W_qkv': _L0_attn_a_in['W_qkv'], 'L0_attn_a_b_qkv': _L0_attn_a_in['b_qkv'], 'L0_attn_a_W_ao': _L0_attn_a_in['W_ao'], 'L0_attn_a_b_ao': _L0_attn_a_in['b_ao'], 'L0_attn_a_g1': _L0_attn_a_in['g1'], 'L0_attn_a_be1': _L0_attn_a_in['be1'], 'L0_attn_a_g2': _L0_attn_a_in['g2'], 'L0_attn_a_be2': _L0_attn_a_in['be2'], 'L0_attn_a_W_f1': _L0_attn_a_in['W_f1'], 'L0_attn_a_b_f1': _L0_attn_a_in['b_f1'], 'L0_attn_a_W_f2': _L0_attn_a_in['W_f2'], 'L0_attn_a_b_f2': _L0_attn_a_in['b_f2'], 'L0_attn_b_Wq': _L0_attn_b_in['Wq'], 'L0_attn_b_bq': _L0_attn_b_in['bq'], 'L0_attn_b_Wk': _L0_attn_b_in['Wk'], 'L0_attn_b_bk': _L0_attn_b_in['bk'], 'L0_attn_b_Wv': _L0_attn_b_in['Wv'], 'L0_attn_b_bv': _L0_attn_b_in['bv'], 'L0_attn_b_Wo': _L0_attn_b_in['Wo'], 'L0_attn_b_bo': _L0_attn_b_in['bo'], 'L0_attn_b_sample_idx': _L0_attn_b_in['sample_idx'], 'L0_ffn_router_w': _L0_ffn_in['router_w'], 'L0_ffn_expert_bias': _L0_ffn_in['expert_bias'], 'L0_ffn_shared_w1': _L0_ffn_in['shared_w1'], 'L0_ffn_shared_w2': _L0_ffn_in['shared_w2'], 'L0_ffn_shared_w3': _L0_ffn_in['shared_w3'], 'L0_ffn_routed_w1': _L0_ffn_in['routed_w1'], 'L0_ffn_routed_w2': _L0_ffn_in['routed_w2'], 'L0_ffn_routed_w3': _L0_ffn_in['routed_w3']}
    _x0 = _d['L0_attn_a_x']
    _d['L0_attn_a_x'] = jax.random.normal(jax.random.fold_in(jax.random.key(seed), 1), (16, 256, 128), dtype=_x0.dtype)
    del _x0
    return _d

def reference(L0_attn_a_x, L0_attn_a_A_log, L0_attn_a_Dp, L0_attn_a_W_in, L0_attn_a_b_in, L0_attn_a_W_xp, L0_attn_a_b_xp, L0_attn_a_W_dt, L0_attn_a_b_dt, L0_attn_a_W_out, L0_attn_a_b_out, L0_attn_a_W_qkv, L0_attn_a_b_qkv, L0_attn_a_W_ao, L0_attn_a_b_ao, L0_attn_a_g1, L0_attn_a_be1, L0_attn_a_g2, L0_attn_a_be2, L0_attn_a_W_f1, L0_attn_a_b_f1, L0_attn_a_W_f2, L0_attn_a_b_f2, L0_attn_b_Wq, L0_attn_b_bq, L0_attn_b_Wk, L0_attn_b_bk, L0_attn_b_Wv, L0_attn_b_bv, L0_attn_b_Wo, L0_attn_b_bo, L0_attn_b_sample_idx, L0_ffn_router_w, L0_ffn_expert_bias, L0_ffn_shared_w1, L0_ffn_shared_w2, L0_ffn_shared_w3, L0_ffn_routed_w1, L0_ffn_routed_w2, L0_ffn_routed_w3):

    def _L0_attn_a_ref(x, A_log, Dp, W_in, b_in, W_xp, b_xp, W_dt, b_dt, W_out, b_out, W_qkv, b_qkv, W_ao, b_ao, g1, be1, g2, be2, W_f1, b_f1, W_f2, b_f2):
        import jax, jax.numpy as jnp
        import numpy as np
        L, B, S, D, N, H = (4, 4, 128, 128, 64, 16)
        DI = 2 * D
        DH = D // H
        DF = 4 * D
        SCALE = 1.0 / np.sqrt(DH)

        def _ln(x, g, b, eps=1e-05):
            mu = x.mean(-1, keepdims=True)
            var = ((x - mu) ** 2).mean(-1, keepdims=True)
            return (x - mu) * jax.lax.rsqrt(var + eps) * g + b

        def _mamba(x, A_log, Dp, W_in, b_in, W_xp, b_xp, W_dt, b_dt, W_out, b_out):
            xr = jnp.einsum('bsd,od->bso', x, W_in) + b_in
            xi, res = jnp.split(xr, 2, axis=-1)
            xi = jax.nn.silu(xi)
            A = -jnp.exp(A_log)
            delta = jax.nn.softplus(jnp.einsum('bsi,di->bsd', xi, W_dt) + b_dt)
            m = delta.mean(-1)
            A_disc = jnp.exp(A[None, None, :] * m[:, :, None])
            u = jnp.einsum('bsi,ni->bsn', xi, W_xp) + b_xp

            def step(state, inp):
                a_t, u_t = inp
                state = a_t * state + u_t
                return (state, state.sum(-1))
            init = jnp.zeros((x.shape[0], A_log.shape[0]), x.dtype)
            _, ssum = jax.lax.scan(step, init, (A_disc.swapaxes(0, 1), u.swapaxes(0, 1)))
            ssum = ssum.swapaxes(0, 1)
            y = ssum[..., None] * xi
            y = y * jax.nn.silu(res)
            y = jnp.einsum('bsi,di->bsd', y, W_out) + b_out
            return y + x * Dp

        def _attn(x, W_qkv, b_qkv, W_ao, b_ao):
            b, s, d = x.shape
            qkv = jnp.einsum('bsd,od->bso', x, W_qkv) + b_qkv
            qkv = qkv.reshape(b, s, 3, H, DH)
            q = jnp.moveaxis(qkv[:, :, 0], 2, 1)
            k = jnp.moveaxis(qkv[:, :, 1], 2, 1)
            v = jnp.moveaxis(qkv[:, :, 2], 2, 1)
            scores = jnp.einsum('bhqd,bhkd->bhqk', q, k) * SCALE
            wts = jax.nn.softmax(scores, axis=-1)
            o = jnp.einsum('bhqk,bhkd->bhqd', wts, v)
            o = jnp.moveaxis(o, 1, 2).reshape(b, s, d)
            return jnp.einsum('bsd,od->bso', o, W_ao) + b_ao

        def _forward(x, A_log, Dp, W_in, b_in, W_xp, b_xp, W_dt, b_dt, W_out, b_out, W_qkv, b_qkv, W_ao, b_ao, g1, be1, g2, be2, W_f1, b_f1, W_f2, b_f2):
            for l in range(L):
                m = _mamba(x, A_log[l], Dp[l], W_in[l], b_in[l], W_xp[l], b_xp[l], W_dt[l], b_dt[l], W_out[l], b_out[l])
                x = _ln(x + m, g1[l], be1[l])
                a = _attn(x, W_qkv[l], b_qkv[l], W_ao[l], b_ao[l])
                x = _ln(x + a, g2[l], be2[l])
                h = jax.nn.gelu(jnp.einsum('bsd,fd->bsf', x, W_f1[l]) + b_f1[l], approximate=False)
                x = x + jnp.einsum('bsf,df->bsd', h, W_f2[l]) + b_f2[l]
            return x
        return _forward(x, A_log, Dp, W_in, b_in, W_xp, b_xp, W_dt, b_dt, W_out, b_out, W_qkv, b_qkv, W_ao, b_ao, g1, be1, g2, be2, W_f1, b_f1, W_f2, b_f2)

    def _L0_attn_b_ref(x, Wq, bq, Wk, bk, Wv, bv, Wo, bo, sample_idx):
        import math
        import jax, jax.numpy as jnp
        import numpy as np
        B, L, D_MODEL, NHEAD, FACTOR = (8, 512, 128, 16, 5)
        D_HEAD = D_MODEL // NHEAD
        SAMPLE_K = min(L, max(1, FACTOR * int(math.ceil(math.log(max(L, 2))))))
        TOP_U = min(L, max(1, FACTOR * int(math.ceil(math.log(max(L, 2))))))

        def _split_heads(t):
            b, l, _ = t.shape
            return t.reshape(b, l, NHEAD, D_HEAD).transpose(0, 2, 1, 3)
        b, l, d = x.shape
        q = _split_heads(x @ Wq.T + bq)
        k = _split_heads(x @ Wk.T + bk)
        v = _split_heads(x @ Wv.T + bv)
        scale = 1.0 / math.sqrt(D_HEAD)
        k_sample = k[:, :, sample_idx, :]
        scores_sample = jnp.einsum('bhqd,bhsd->bhqs', q, k_sample) * scale
        m = scores_sample.max(axis=-1) - scores_sample.mean(axis=-1)
        _, top_idx = jax.lax.top_k(m, TOP_U)
        context = jnp.broadcast_to(v.mean(axis=-2, keepdims=True), (b, NHEAD, l, D_HEAD))
        q_top = jnp.take_along_axis(q, top_idx[..., None], axis=2)
        scores_top = jnp.einsum('bhud,bhkd->bhuk', q_top, k) * scale
        attn = jax.nn.softmax(scores_top, axis=-1)
        out_top = jnp.einsum('bhuk,bhkd->bhud', attn, v)
        bi = jnp.arange(b)[:, None, None]
        hi = jnp.arange(NHEAD)[None, :, None]
        context = context.at[bi, hi, top_idx].set(out_top)
        out = context.transpose(0, 2, 1, 3).reshape(b, l, d)
        return out @ Wo.T + bo

    def _L0_ffn_ref(x, router_w, expert_bias, shared_w1, shared_w2, shared_w3, routed_w1, routed_w2, routed_w3):
        import jax, jax.numpy as jnp
        import numpy as np
        B, S, D = (4, 512, 128)
        H = 512
        RH = 128
        E = 16
        K = 2
        NS = 1

        def _swiglu(x, w1, w2, w3):
            return jax.nn.silu(x @ w1) * (x @ w2) @ w3
        shared_out = jnp.sum(jax.vmap(lambda w1, w2, w3: _swiglu(x, w1, w2, w3))(shared_w1, shared_w2, shared_w3), axis=0)
        scores = jax.nn.sigmoid(x @ router_w)
        sel_scores = scores + expert_bias
        _, top_idx = jax.lax.top_k(sel_scores, K)
        top_scores = jnp.take_along_axis(scores, top_idx, axis=-1)
        gates = jnp.sum(jax.nn.one_hot(top_idx, E, dtype=scores.dtype) * top_scores[..., None], axis=-2)
        xf = x.reshape(-1, D)
        gf = gates.reshape(-1, E).T

        def body(acc, ws):
            w1, w2, w3, g = ws
            return (acc + _swiglu(xf, w1, w2, w3) * g[:, None], None)
        routed_out, _ = jax.lax.scan(body, jnp.zeros_like(xf), (routed_w1, routed_w2, routed_w3, gf))
        return shared_out + routed_out.reshape(x.shape)
    x = L0_attn_a_x
    x = x + _L0_attn_a_ref(_layernorm(x, axis=-1), L0_attn_a_A_log, L0_attn_a_Dp, L0_attn_a_W_in, L0_attn_a_b_in, L0_attn_a_W_xp, L0_attn_a_b_xp, L0_attn_a_W_dt, L0_attn_a_b_dt, L0_attn_a_W_out, L0_attn_a_b_out, L0_attn_a_W_qkv, L0_attn_a_b_qkv, L0_attn_a_W_ao, L0_attn_a_b_ao, L0_attn_a_g1, L0_attn_a_be1, L0_attn_a_g2, L0_attn_a_be2, L0_attn_a_W_f1, L0_attn_a_b_f1, L0_attn_a_W_f2, L0_attn_a_b_f2)
    x = x + _L0_ffn_ref(_layernorm(x, axis=-1), L0_ffn_router_w, L0_ffn_expert_bias, L0_ffn_shared_w1, L0_ffn_shared_w2, L0_ffn_shared_w3, L0_ffn_routed_w1, L0_ffn_routed_w2, L0_ffn_routed_w3)
    x = x + _L0_attn_b_ref(_layernorm(x, axis=-1), L0_attn_b_Wq, L0_attn_b_bq, L0_attn_b_Wk, L0_attn_b_bk, L0_attn_b_Wv, L0_attn_b_bv, L0_attn_b_Wo, L0_attn_b_bo, L0_attn_b_sample_idx)
    x = x + _L0_ffn_ref(_layernorm(x, axis=-1), L0_ffn_router_w, L0_ffn_expert_bias, L0_ffn_shared_w1, L0_ffn_shared_w2, L0_ffn_shared_w3, L0_ffn_routed_w1, L0_ffn_routed_w2, L0_ffn_routed_w3)
    return x

_drawn_inputs = setup_inputs


def setup_inputs(seed=0):
    import zlib

    import numpy as np

    out = dict(_drawn_inputs(seed))
    spreads = {'L0_attn_a_b_in': (0.0, 0.8),
     'L0_attn_a_b_xp': (0.0, 0.726),
     'L0_attn_a_b_dt': (0.0, 0.8),
     'L0_attn_a_b_out': (0.0, 0.1),
     'L0_attn_a_b_qkv': (0.0, 0.321),
     'L0_attn_a_b_ao': (0.0, 0.1),
     'L0_attn_a_g1': (1.0, 0.2),
     'L0_attn_a_be1': (0.0, 0.1),
     'L0_attn_a_g2': (1.0, 0.2),
     'L0_attn_a_be2': (0.0, 0.1),
     'L0_attn_a_b_f1': (0.0, 0.29),
     'L0_attn_a_b_f2': (0.0, 0.1),
     'L0_attn_b_bq': (0.0, 0.8),
     'L0_attn_b_bk': (0.0, 0.8),
     'L0_attn_b_bv': (0.0, 0.547),
     'L0_attn_b_bo': (0.0, 0.1),
     'L0_ffn_expert_bias': (0.0, 0.8)}
    factors = {'L0_attn_a_A_log': 3.13,
     'L0_attn_a_W_in': 4.845,
     'L0_attn_a_W_xp': 7.76,
     'L0_attn_a_W_dt': 8.0,
     'L0_attn_a_W_out': 4.654,
     'L0_attn_b_Wq': 8.0,
     'L0_attn_b_Wk': 8.0,
     'L0_attn_b_Wv': 5.119,
     'L0_attn_b_Wo': 2.944,
     'L0_ffn_router_w': 8.0,
     'L0_ffn_shared_w1': 3.82,
     'L0_ffn_shared_w2': 3.824,
     'L0_ffn_shared_w3': 3.803,
     'L0_ffn_routed_w1': 8.0,
     'L0_ffn_routed_w2': 8.0,
     'L0_ffn_routed_w3': 8.0}
    for name, (base, spread) in spreads.items():
        noise = np.random.default_rng([zlib.crc32(name.encode()), seed]).standard_normal(out[name].shape)
        drawn = base * np.exp(spread * noise) if base else spread * noise
        out[name] = jnp.asarray(drawn.astype(out[name].dtype))
    for name, factor in factors.items():
        out[name] = (out[name] * factor).astype(out[name].dtype)
    return out
```

```python
from contextlib import ExitStack

import concourse.bass as bass
from concourse import mybir

F32 = mybir.dt.float32
F32R = mybir.dt.float32r
I32 = mybir.dt.int32
ALU = mybir.AluOpType
ACT = mybir.ActivationFunctionType
AX = mybir.AxisListType
ds = bass.ds

P = 128
BATCH, SEQ, D = 16, 256, 128
TOK = BATCH * SEQ
CH = 512
NC = TOK // CH
LAYERS, STATES, HEADS, DH = 4, 64, 16, 8
DI, DF = 2 * D, 4 * D
EXPERTS, SHARED = 16, 4
BLOCKS = EXPERTS + SHARED
SAMPLES = TOP = 35
SC = SAMPLES + 1
EPS = 1e-5
QSCALE = 1.0 / DH ** 0.5
CREDIT = 4

MW = {}
for _name, _n in (("win", 2 * DI), ("wdt", 2 * D), ("wout", 2 * D), ("wf1", DF), ("wf2", DF), ("b_in", 4),
                  ("b_dt", 1), ("b_xp", 1), ("b_out", 1), ("Dp", 1), ("A_log", 1), ("g1", 1), ("be1", 1), ("g2", 1),
                  ("be2", 1), ("b_f1", 4), ("b_f2", 1)):
    MW[_name] = (sum(n for _, n in MW.values()), _n)
MCOLS = sum(n for _, n in MW.values())
TW = {}
for _name, _n in (("wq", D), ("wk", D), ("wv", D), ("wo", D), ("bvb", D), ("bq", 1), ("bk", 1), ("bo", 1), ("bv", 1)):
    TW[_name] = (sum(n for _, n in TW.values()), _n)
TCOLS = sum(n for _, n in TW.values())
GW = {}
for _name, _n in (("w3", BLOCKS * D), ("router", EXPERTS), ("ebias", EXPERTS)):
    GW[_name] = (sum(n for _, n in GW.values()), _n)
GCOLS = sum(n for _, n in GW.values())


def build_program(nc, x_d, mw_d, xp_d, tw_d, w12_d, gw_d, idx_d, out_d):
    ctx = ExitStack()
    with ctx:
        def sem(name):
            return ctx.enter_context(nc.semaphore(name))

        base = (nc.sbuf_base + 63) // 64 * 64
        top = [base]

        def at(name, shape, dt=F32, where=None):
            where = top if where is None else where
            n = 4
            for s in shape[1:]:
                n *= s
            t = nc.alloc_sbuf_tensor_at(name, shape, dt, offset=where[0])
            where[0] += (n + 63) // 64 * 64
            return t

        res = at("res", [P, TOK])
        xa = at("xa", [P, TOK])
        mw = at("mw", [P, MCOLS])
        tw = at("tw", [P, TCOLS])
        wxp = at("wxp", [P, 2, 2, P])
        w1h = at("w1h", [P, BLOCKS, D], F32R)
        w1l = at("w1l", [P, BLOCKS, D], F32R)
        w2h = at("w2h", [P, BLOCKS, D], F32R)
        w2l = at("w2l", [P, BLOCKS, D], F32R)
        gw = at("gw", [P, GCOLS])
        ident = at("ident", [P, P])
        center = at("center", [P, P])
        average = at("average", [P, P])
        halfavg = at("halfavg", [P, 2, P])
        halfsum = at("halfsum", [P, 2, P])
        acol = at("acol", [P, 5])
        work = top[0]
        end = nc.sbuf_usable_end

        def M(name, k=0, n=None):
            a, m = MW[name]
            return mw[:, a + k:a + k + (m if n is None else n)]

        def T(name, k=0, n=None):
            a, m = TW[name]
            return tw[:, a + k:a + k + (m if n is None else n)]

        def G(name, k=0, n=None):
            a, m = GW[name]
            return gw[:, a + k:a + k + (m if n is None else n)]

        w = [work + (3 * 16 + 3 * 4 + 3 * 4) * 1024]
        sq = at("sq", [P, 2, CH], where=w)
        logv = at("logv", [P, 2, CH], where=w)
        rstd = at("rstd", [P, 2, CH], where=w)
        unit = at("unit", [P, 2, CH], where=w)
        w = [work]
        xi = at("xi", [P, 2, TOK], where=w)
        zz = at("zz", [P, 2, TOK], where=w)
        st = at("st", [P, NC * SEQ], where=w)
        shared_at = w[0]
        sres = at("sres", [P, 2, 2, CH], where=w)
        w = [shared_at]
        y = at("y", [P, 2, 2, CH], where=w)
        xd = at("xd", [P, 2, CH], where=w)
        absd = at("absd", [P, 2, CH], where=w)
        logd = at("logd", [P, 2, CH], where=w)
        posd = at("posd", [P, 2, CH], where=w)
        delta = at("delta", [P, 2, CH], where=w)
        adisc = at("adisc", [P, 2, SEQ], where=w)
        uin = at("uin", [P, 2, SEQ], where=w)
        assert w[0] <= end
        w = [work]
        hid = at("hid", [P, 2, 2, CH], where=w)
        w = [work]
        w12raw = at("w12raw", [P, 2, BLOCKS * D], where=w)
        w = [work]
        gateT = at("gateT", [64, TOK], F32R, where=w)
        esel = at("esel", [64, EXPERTS, P], F32R, where=w)
        xh = at("xh", [P, 2, CH], F32R, where=w)
        xl = at("xl", [P, 2, CH], F32R, where=w)
        sil = at("sil", [P, 2, CH], where=w)
        su = at("su", [P, 2, CH], where=w)
        hh = at("hh", [P, 2, CH], where=w)
        ntile = TOK // P
        sg = at("sg", [P, ntile, EXPERTS], where=w)
        se = at("se", [P, ntile, EXPERTS], where=w)
        m8 = at("m8", [P, ntile, 8], where=w)
        gt = at("gt", [P, ntile, EXPERTS], where=w)
        eq = at("eq", [P, ntile, EXPERTS], where=w)
        cum = at("cum", [P, ntile, EXPERTS], where=w)
        cnt = at("cnt", [P, ntile], where=w)
        before = at("before", [P, ntile], where=w)
        assert w[0] <= end
        w = [work]
        qv = [at(f"qv{r}", [P, HEADS, SEQ], F32R, where=w) for r in range(3)]
        k4 = [at(f"k4{r}", [P, 4, SEQ], F32R, where=w) for r in range(3)]
        vx = [at(f"vx{r}", [P, 2, HEADS, 32], where=w) for r in range(3)]
        pt = at("pt", [P, 2, 4, 2, SEQ], where=w)
        oraw = at("oraw", [P, 4, SEQ], where=w)
        xs = at("xs", [P, SEQ], where=w)
        qs = at("qs", [P, 2, SEQ], F32R, where=w)
        ks = at("ks", [P, 2, SEQ], F32R, where=w)
        mh = at("mh", [8, 2, SEQ], F32R, where=w)
        ml = at("ml", [8, 2, SEQ], F32R, where=w)
        mxs = at("mxs", [P, 3, HEADS, 2], where=w)
        rec = at("rec", [P, HEADS], where=w)
        ontok = at("ontok", [P, 2, P], where=w)
        onT = at("onT", [P, SEQ], where=w)
        maskb = at("maskb", [P, SEQ], where=w)
        selo = at("selo", [P, SEQ], where=w)
        vmean = at("vmean", [P, 3], where=w)
        xsum = at("xsum", [P, 3], where=w)
        assert w[0] <= end, (w[0], end)
        w = [work + (3 * 16 + 3 * 4 + 3 * 4) * 1024]
        idx_i = at("idx_i", [P, SAMPLES], I32, where=w)
        idx_f = at("idx_f", [P, SAMPLES], where=w)
        idx_n = at("idx_n", [P, SAMPLES], where=w)
        idx_c = at("idx_c", [P, SAMPLES], I32, where=w)
        xg = at("xg", [P, BATCH, SC], where=w)
        ksg = at("ksg", [P, BATCH, SC], where=w)
        headmask = at("headmask", [P, HEADS], where=w)
        kbd = at("kbd", [P, 2, HEADS, SC], where=w)
        qf = at("qf", [P, 2, SEQ], where=w)
        mxq = at("mxq", [P, 2, 2, HEADS], where=w)
        mall = at("mall", [P, 2, BATCH, HEADS], where=w)
        mrow = at("mrow", [P, 2, SEQ], where=w)
        mwork = at("mwork", [P, 2, SEQ], where=w)
        mtop = at("mtop", [P, 2, 8], where=w)
        mgt = at("mgt", [P, 2, SEQ], where=w)
        meq = at("meq", [P, 2, SEQ], where=w)
        mcum = at("mcum", [P, 2, SEQ], where=w)
        mneed = at("mneed", [P, 2], where=w)

        ps = ctx.enter_context(nc.psum_tensor("ps", [P, 8, CH], F32))
        qk_d = nc.dram_tensor("qk_scratch", (2, 2, P, SEQ), F32, kind="Internal").ap()
        mask_d = nc.dram_tensor("mask_scratch", (BATCH * P, SEQ), F32, kind="Internal").ap()

        counted = {}

        def counter(name, n=1):
            s = sem(name)
            counted[s.name] = (s, n)
            return s

        phase_done = sem("phase_done")
        load_x = [sem(f"load_x{c}") for c in range(NC)]
        load_m = sem("load_m")
        load_t = sem("load_t")
        load_g = sem("load_g")
        load_i = sem("load_i")
        stored = sem("stored")
        gates_ready = sem("gates_ready")
        idx_ready = sem("idx_ready")
        column_taken = sem("column_taken")
        taken = sem("taken")
        gathered = sem("gathered")
        sampled = sem("sampled")
        mask_ready = sem("mask_ready")
        mask_stored = sem("mask_stored")
        setup_done = sem("setup_done")
        waited = sem("waited")
        dve_step = sem("dve_step")
        act_step = sem("act_step")
        pool_step = sem("pool_step")
        pe_step = sem("pe_step")

        ln_cen = counter("ln_cen")
        ln_sq = counter("ln_sq")
        ln_var = counter("ln_var")
        ln_log = counter("ln_log")
        ln_rstd = counter("ln_rstd")
        ln_unit = counter("ln_unit")
        ln_aff = counter("ln_aff")
        acol_exp = counter("acol_exp")
        acol_neg = counter("acol_neg")
        acol_skip = counter("acol_skip")
        m1_psum = counter("m1_psum", 4)
        m1_evac = counter("m1_evac", 4)
        m1_gate = counter("m1_gate")
        m2_dt = counter("m2_dt")
        m2_u = counter("m2_u")
        m2_mean = counter("m2_mean")
        m2_abs = counter("m2_abs")
        m2_exp = counter("m2_exp")
        m2_log = counter("m2_log")
        m2_pos = counter("m2_pos")
        m2_delta = counter("m2_delta")
        m2_uin = counter("m2_uin")
        m2_adisc = counter("m2_adisc")
        m2_scan = counter("m2_scan")
        m3_sum = counter("m3_sum")
        m3_y = counter("m3_y")
        m3_out = counter("m3_out")
        m3_skip = counter("m3_skip")
        m3_res = counter("m3_res")
        f_h = counter("f_h", 4)
        f_g = counter("f_g", 4)
        f_acc = counter("f_acc", 2)
        f_out = counter("f_out")
        add_res = counter("add_res")
        e_h = counter("e_h", BLOCKS)
        e_s = counter("e_s", BLOCKS)
        e_t = counter("e_t", EXPERTS)
        e_m = counter("e_m", BLOCKS)
        e_w = counter("e_w", BLOCKS)
        e_xh = counter("e_xh")
        e_xl = counter("e_xl")
        e_out = counter("e_out")
        at_xs = counter("at_xs")
        at_proj = counter("at_proj", 2)
        at_hi = counter("at_hi", 2)
        at_lo = counter("at_lo", 3)
        at_spill = counter("at_spill", 32)
        at_scat = [sem(f"at_scat{r}") for r in range(3)]
        at_am = counter("at_am", 16)
        at_max = counter("at_max", 16)
        at_tp = counter("at_tp", 2)
        at_mh = counter("at_mh", 2)
        at_ml = counter("at_ml", 2)
        at_mx = [counter(f"at_mx{h}", 32) for h in range(2)]
        at_sc = counter("at_sc", 8)
        at_exp = counter("at_exp", 8)
        at_pv = counter("at_pv", 4)
        at_oev = counter("at_oev", 4)
        at_otp = counter("at_otp", 2)
        at_rec = counter("at_rec", 2)
        at_ot = counter("at_ot", 2)
        at_obp = counter("at_obp")
        at_ob = counter("at_ob")
        at_aop = counter("at_aop")
        at_ao = counter("at_ao")
        at_xm = counter("at_xm")
        at_vmp = counter("at_vmp")
        at_vm = counter("at_vm")
        at_sel = counter("at_sel")
        at_mask = counter("at_mask", 16)
        b_kbd = counter("b_kbd")
        b_q = counter("b_q")
        b_qf = counter("b_qf")
        b_s = counter("b_s", 2)
        b_mx = counter("b_mx", 2)
        b_m = counter("b_m", 2)

        def nth(s, c, k=0):
            n = counted[s.name][1]
            return n * c + (n * CREDIT + k + 1)

        def every(s, c):
            n = counted[s.name][1]
            return n * c + n * (CREDIT + 1)

        SETUP, LN0, SPLIT, LAYER0 = 0, 1, 2, 3
        M1, M2, M3, LN1, ATT, LN2, F, PER_LAYER = range(8)
        TAIL = LAYER0 + PER_LAYER * LAYERS
        (LN_F1, GATE_F1, EXP_F1, LN_B, CHOOSE, ATT_B, LN_F2, GATE_F2, EXP_F2) = range(TAIL, TAIL + 9)

        def passed(eng, n):
            eng.wait_ge(phase_done, 4 * n + 4)
            eng.sem_inc(waited, 1)

        def gate(eng, n):
            eng.drain().then_inc(phase_done, 1)
            passed(eng, n)

        def of_layer(l, k):
            return l * PER_LAYER + (LAYER0 + k)

        NR = [(BATCH + 2 - r) // 3 for r in range(3)]

        def scattered(e, third, r):
            return e * (NR[r] * 240) + third * 240 + 240

        def sequences(eng, step, last):
            step(0, 0, 0, first=True)
            with eng.Fori(0, 4) as i:
                for k in range(3):
                    step(i * 3 + (1 + k), i + (1 + k) // 3, (1 + k) % 3)
            step(13, 4, 1)
            step(14, 4, 2, proj=False)
            step(15, 5, 0, nxt=False, proj=False)
            last()

        pe_steps = {0: 1, 1: 5, "samples": 3, "rows": 4}
        act_steps = {0: 3, 1: 4}

        block = ctx.enter_context(nc.Block())

        @block.sync
        def _(sp):
            for s, n in counted.values():
                sp.sem_inc(s, CREDIT * n)
            for c in range(NC):
                sp.dma_start(res[:, c * CH:(c + 1) * CH], x_d[:, c * CH:(c + 1) * CH]).then_inc(load_x[c], 16)

            def load_layer(l):
                sp.dma_start(mw[:], mw_d[ds(l, 1)].rearrange("o p n -> (o p) n")).then_inc(load_m, 16)
                for hb in range(2):
                    sp.dma_start(wxp[:, hb, :, hb * STATES:(hb + 1) * STATES],
                                 xp_d[ds(l, 1)].rearrange("o p k n -> (o p) k n")).then_inc(load_m, 16)

            def load_attention(l):
                sp.dma_start(tw[:], tw_d[ds(l, 1)].rearrange("o p n -> (o p) n")).then_inc(load_t, 16)

            sp.dma_start(w12raw[:], w12_d).then_inc(load_g, 16)
            sp.wait_ge(setup_done, 1)
            load_layer(0)
            load_attention(0)
            sp.dma_start(gw[:], gw_d).then_inc(load_g, 16)

            def attention(e, probsparse):
                def send_max(b, half, r):
                    B = e * BATCH + b
                    sp.wait_ge(at_mh, nth(at_mh, B, half))
                    sp.wait_ge(at_ml, nth(at_ml, B, half))
                    sp.wait_ge(at_sc, nth(at_sc, B - 3, 7))
                    for row, part in ((96, mh), (97, ml)):
                        sp.dma_start(qv[r][row:row + 1, 8 * half:8 * half + 8, :].bitcast(F32),
                                     part[0:8, half, :].bitcast(F32)).then_inc(at_mx[half], 16)

                def send_qk(b, third, r):
                    B = e * BATCH + b
                    for n, t in enumerate((qs, ks)):
                        sp.wait_ge(at_lo, nth(at_lo, B, n))
                        sp.dma_start(qk_d[n].rearrange("a p n -> p a n"), t[:].bitcast(F32)).then_inc(at_spill, 16)
                    sp.wait_ge(at_spill, every(at_spill, B))
                    sp.wait_ge(at_sc, nth(at_sc, B - 3, 7))
                    for term, part in enumerate((0, 1, 0)):
                        sp.dma_start(k4[r][32 * term:32 * term + 32].bitcast(F32),
                                     qk_d[1, part].rearrange("(j p) n -> p j n", j=4)).then_inc(at_scat[r], 16)
                    for term, part in enumerate((0, 0, 1)):
                        for g in range(4):
                            sp.dma_start(qv[r][32 * term + 8 * g:32 * term + 8 * g + 8].bitcast(F32)
                                         .rearrange("p (j g) n -> p j g n", g=4)[:, :, g, :],
                                         qk_d[0, part].rearrange("(j g p) n -> g p j n", j=4, g=4)[g])\
                              .then_inc(at_scat[r], 16)
                    sp.wait_ge(at_scat[r], scattered(e, third, r))

                def send_mask(b):
                    sp.wait_ge(at_sel, nth(at_sel, b - 1))
                    sp.dma_start(maskb[:], mask_d[ds(b * P, P), :]).then_inc(at_mask, 16)

                def step(b, third, r, nxt=True, proj=True, first=False):
                    send_max(b, 1, r)
                    if probsparse and not first:
                        send_mask(b - 1)
                    if proj:
                        send_qk(b + 2, third + (r + 2) // 3, (r + 2) % 3)
                    if nxt:
                        send_max(b + 1, 0, (r + 1) % 3)

                for b in (0, 1):
                    send_qk(b, 0, b)
                send_max(0, 0, 0)
                sequences(sp, step, (lambda: send_mask(15)) if probsparse else (lambda: None))

            with sp.Fori(0, LAYERS) as l:
                passed(sp, of_layer(l, LN1))
                attention(l, False)
                passed(sp, of_layer(l, ATT))
                load_attention(l + 1)
                passed(sp, of_layer(l, F))
                load_layer(l + 1)
            passed(sp, LN_B)
            sp.dma_start(idx_i[:], idx_d).then_inc(load_i, 16)
            sp.wait_ge(mask_ready, 1)
            for h in range(2):
                for d in range(DH):
                    sp.dma_start(mask_d.rearrange("(g r d) n -> g r d n", g=2, d=DH)[h, :, d, :],
                                 mwork[:, h, :]).then_inc(mask_stored, 16)
            sp.wait_ge(mask_stored, 16 * 2 * DH)
            passed(sp, CHOOSE)
            attention(LAYERS, True)
            for c in range(NC):
                sp.wait_ge(e_out, nth(e_out, NC + c))
                sp.dma_start(out_d[:, c * CH:(c + 1) * CH], res[:, c * CH:(c + 1) * CH]).then_inc(stored, 16)
            sp.wait_ge(load_m, 48 * (LAYERS + 1))
            sp.wait_ge(stored, 16 * NC)

        @block.tensor
        def _(pe):
            mm = nc.tensor.matmul

            def norm(n, src, added=False, loaded=False):
                def centered(c, u, C):
                    pe.wait_ge(ln_unit, nth(ln_unit, C - 2))
                    mm(ps[:, u, :], center[:], src[:, ds(c * CH, CH)], start=True, stop=True).then_inc(ln_cen, 1)

                with pe.Fori(0, NC // 2) as i:
                    for u in range(2):
                        if added:
                            pe.wait_ge(add_res, nth(add_res, i * 2 + u))
                        centered(i * 2 + u, u, n * NC + i * 2 + u)
                    for u in range(2):
                        C = n * NC + i * 2 + u
                        pe.wait_ge(ln_sq, nth(ln_sq, C))
                        pe.wait_ge(ln_log, nth(ln_log, C - 2))
                        mm(ps[:, 2 + u, :], average[:], sq[:, u, :], start=True, stop=True).then_inc(ln_var, 1)

            def m1(l):
                with pe.Fori(0, NC // 2) as i:
                    for u in range(2):
                        C = l * NC + i * 2 + u
                        for o in range(4):
                            pe.wait_ge(m1_evac, nth(m1_evac, C - 2, o))
                            mm(ps[:, 4 * u + o, :], M("win", o * P, P), xa[:, ds((i * 2 + u) * CH, CH)],
                               start=True, stop=True).then_inc(m1_psum, 1)

            def m2(l):
                with pe.Fori(0, NC // 2) as i:
                    for u in range(2):
                        C = l * NC + i * 2 + u
                        pe.wait_ge(m2_abs, nth(m2_abs, C - 2))
                        pe.wait_ge(m2_pos, nth(m2_pos, C - 2))
                        for kb in range(2):
                            last = mm(ps[:, u, :], M("wdt", kb * P, P), xi[:, kb, ds((i * 2 + u) * CH, CH)],
                                      start=kb == 0, stop=kb == 1)
                        last.then_inc(m2_dt, 1)
                        pe.wait_ge(m2_uin, nth(m2_uin, C - 2))
                        for hb in range(2):
                            for kb in range(2):
                                last = mm(ps[:, 4 + u, 0:SEQ], wxp[:, hb, kb, :],
                                          xi[:, kb, ds((i * 2 + u) * CH + hb * SEQ, SEQ)],
                                          start=hb + kb == 0, stop=hb + kb == 2)
                        last.then_inc(m2_u, 1)
                    for u in range(2):
                        C = l * NC + i * 2 + u
                        pe.wait_ge(m2_delta, nth(m2_delta, C))
                        pe.wait_ge(m2_adisc, nth(m2_adisc, C - 2))
                        for hb in range(2):
                            last = mm(ps[:, 2 + u, 0:SEQ], halfavg[:, hb, :], delta[:, u, hb * SEQ:(hb + 1) * SEQ],
                                      start=hb == 0, stop=hb == 1)
                        last.then_inc(m2_mean, 1)

            def m3(l):
                with pe.Fori(0, NC // 2) as i:
                    for u in range(2):
                        C = l * NC + i * 2 + u
                        pe.wait_ge(m3_y, nth(m3_y, C - 2))
                        for hb in range(2):
                            last = mm(ps[:, u, hb * SEQ:(hb + 1) * SEQ], halfsum[:, hb, :],
                                      st[:, ds((i * 2 + u) * SEQ, SEQ)], start=True, stop=True)
                        last.then_inc(m3_sum, 1)
                    for u in range(2):
                        C = l * NC + i * 2 + u
                        pe.wait_ge(m3_y, nth(m3_y, C))
                        pe.wait_ge(m3_res, nth(m3_res, C - 2))
                        for kb in range(2):
                            last = mm(ps[:, 2 + u, :], M("wout", kb * P, P), y[:, u, kb, :], start=kb == 0, stop=kb == 1)
                        last.then_inc(m3_out, 1)

            def f(l):
                with pe.Fori(0, NC // 2) as i:
                    def up(u, half):
                        C = l * NC + i * 2 + u
                        pe.wait_ge(f_g, nth(f_g, C - 1, 2 * half + 1))
                        for q in range(2):
                            mm(ps[:, 2 * half + q, :], M("wf1", (2 * half + q) * P, P),
                               xa[:, ds((i * 2 + u) * CH, CH)], start=True, stop=True).then_inc(f_h, 1)

                    def down(u, half):
                        C = l * NC + i * 2 + u
                        pe.wait_ge(f_g, nth(f_g, C, 2 * half + 1))
                        if half == 0:
                            pe.wait_ge(f_out, nth(f_out, C - 2))
                        for q in range(2):
                            last = mm(ps[:, 4 + u, :], M("wf2", (2 * half + q) * P, P), hid[:, half, q, :],
                                      start=half + q == 0, stop=half + q == 2)
                        last.then_inc(f_acc, 1)

                    up(0, 0)
                    up(0, 1)
                    down(0, 0)
                    up(1, 0)
                    down(0, 1)
                    up(1, 1)
                    down(1, 0)
                    down(1, 1)

            def attention(e, probsparse):
                def project_qk(b):
                    B = e * BATCH + b
                    pe.wait_ge(at_xs, nth(at_xs, B))
                    pe.wait_ge(at_lo, nth(at_lo, B - 1, 2))
                    pe.wait_ge(at_ml, nth(at_ml, B - 2, 1))
                    mm(ps[:, 7, 0:SEQ], T("wq"), xs[:], start=True, stop=True)
                    mm(ps[:, 7, SEQ:CH], T("wk"), xs[:], start=True, stop=True).then_inc(at_proj, 1)

                def project_v(b):
                    B = e * BATCH + b
                    pe.wait_ge(at_lo, nth(at_lo, B, 1))
                    pe.wait_ge(at_ot, nth(at_ot, B - 3, 1))
                    if probsparse:
                        pe.wait_ge(at_xm, nth(at_xm, b))
                    for t in range(2):
                        last = mm(ps[:, 7, t * P:(t + 1) * P], xs[:, t * P:(t + 1) * P], T("wv"),
                                  start=True, stop=True)
                    last.then_inc(at_proj, 1)

                def rows(b, h, r):
                    B = e * BATCH + b
                    pe.wait_ge(at_max, nth(at_max, B, h - 2))
                    for qt in range(2):
                        last = mm(ps[:, h % 2, qt * SEQ:(qt + 1) * SEQ], qv[r][0:96, h, qt * P:(qt + 1) * P],
                                  k4[r][0:96, h // 4, :], start=True, stop=True)
                    last.then_inc(at_am, 1)

                def maxima(b, half, r):
                    B = e * BATCH + b
                    pe.wait_ge(at_max, nth(at_max, B, 8 * half + 7))
                    for qt in range(2):
                        last = nc.tensor.transpose(ps[0:8, 7, qt * P:(qt + 1) * P],
                                                   mxs[:, r, 8 * half:8 * half + 8, qt], ident[:])
                    last.then_inc(at_tp, 1)

                def scores(b, p, r):
                    B = e * BATCH + b
                    if p % 4 == 0:
                        pe.wait_ge(at_mx[p // 4], every(at_mx[p // 4], B))
                    pe.wait_ge(at_exp, nth(at_exp, B, p - 2))
                    for hh_ in range(2):
                        h = 2 * p + hh_
                        for kt in range(2):
                            last = mm(ps[:, 2 + 2 * (p % 2) + hh_, kt * SEQ:(kt + 1) * SEQ],
                                      k4[r][0:98, h // 4, kt * P:(kt + 1) * P], qv[r][0:98, h, :],
                                      start=True, stop=True)
                    last.then_inc(at_sc, 1)

                def values(b, j, r):
                    B = e * BATCH + b
                    pe.wait_ge(at_exp, nth(at_exp, B, 2 * j + 1))
                    pe.wait_ge(at_oev, nth(at_oev, B, j - 1))
                    if j == 0:
                        pe.wait_ge(at_lo, nth(at_lo, B, 2))
                    for kt in range(2):
                        for g in range(4):
                            last = mm(ps[32 * g:32 * g + 32, 6, (j % 2) * SEQ:(j % 2 + 1) * SEQ],
                                      vx[r][:, kt, 4 * j + g, :], pt[:, j % 2, g, kt, :], start=kt == 0, stop=kt == 1)
                    last.then_inc(at_pv, 1)

                def to_rows(b, qt):
                    B = e * BATCH + b
                    if qt == 0:
                        pe.wait_ge(at_oev, nth(at_oev, B, 3))
                    else:
                        pe.wait_ge(at_ot, nth(at_ot, B, 0))
                    for j in range(4):
                        last = nc.tensor.transpose(ps[:, 7, j * P:(j + 1) * P], oraw[:, j, qt * P:(qt + 1) * P],
                                                   ident[:])
                    last.then_inc(at_otp, 1)

                def to_columns(b):
                    pe.wait_ge(at_ot, nth(at_ot, e * BATCH + b, 1))
                    for qt in range(2):
                        last = nc.tensor.transpose(ps[:, 7, qt * P:(qt + 1) * P], ontok[:, qt, :], ident[:])
                    last.then_inc(at_obp, 1)

                def out(b):
                    pe.wait_ge(at_ob, nth(at_ob, e * BATCH + b))
                    mm(ps[:, 7, 0:SEQ], T("wo"), onT[:], start=True, stop=True).then_inc(at_aop, 1)

                def mean_v(b, r):
                    mm(ps[:, 7, SEQ:SEQ + 1], T("wv"), xsum[:, r:r + 1], start=True, stop=True).then_inc(at_vmp, 1)

                def step(b, third, r, nxt=True, proj=True, first=False):
                    B = e * BATCH + b
                    t, rn = third + (r + 1) // 3, (r + 1) % 3
                    for p in range(8):
                        if p == 0:
                            pe.wait_ge(at_ml, nth(at_ml, B, 0))
                            pe.wait_ge(at_ao, nth(at_ao, B - 2))
                            maxima(b, 1, r)
                        scores(b, p, r)
                        if nxt:
                            if p == 0:
                                pe.wait_ge(at_scat[rn], scattered(e, t, rn))
                            rows(b + 1, 2 * p, rn)
                            rows(b + 1, 2 * p + 1, rn)
                        if p == 0 and not first:
                            values(b - 1, 3, (r + 2) % 3)
                        if p == 1 and proj:
                            project_qk(b + 2)
                        if p == 2:
                            values(b, 0, r)
                            if not first:
                                if proj:
                                    pe.wait_ge(at_lo, nth(at_lo, B + 2, 1))
                                else:
                                    pe.wait_ge(at_ml, nth(at_ml, B, 1))
                                to_rows(b - 1, 0)
                        if p == 3 and not first:
                            to_rows(b - 1, 1)
                        if p == 4:
                            values(b, 1, r)
                            if proj:
                                project_v(b + 2)
                        if p == 5:
                            if proj:
                                pe.wait_ge(at_lo, nth(at_lo, B + 2, 2))
                            else:
                                pe.wait_ge(at_ot, nth(at_ot, B - 1, 1))
                            if probsparse:
                                mean_v(b, r)
                            if nxt:
                                maxima(b + 1, 0, rn)
                        if p == 6:
                            values(b, 2, r)
                            if not first:
                                if nxt:
                                    pe.wait_ge(at_ml, nth(at_ml, B + 1, 0))
                                if probsparse:
                                    pe.wait_ge(at_vm, nth(at_vm, b))
                                to_columns(b - 1)
                        if p == 7 and not first:
                            out(b - 1)

                def last():
                    values(15, 3, 0)
                    pe.wait_ge(at_ao, nth(at_ao, e * BATCH + 14))
                    to_rows(15, 0)
                    to_rows(15, 1)
                    to_columns(15)
                    out(15)

                for b in (0, 1):
                    project_qk(b)
                    project_v(b)
                pe.wait_ge(at_scat[0], scattered(e, 0, 0))
                for h in range(HEADS):
                    rows(0, h, 0)
                pe.wait_ge(at_lo, nth(at_lo, e * BATCH + 1, 2))
                maxima(0, 0, 0)
                sequences(pe, step, last)

            def gates(n):
                for t in range(ntile):
                    last = mm(ps[:, 0, t * EXPERTS:(t + 1) * EXPERTS], xa[:, t * P:(t + 1) * P], G("router"),
                              start=True, stop=True)
                last.then_inc(pe_step, 1)
                pe.wait_ge(gates_ready, n + 1)
                for t in range(ntile):
                    last = nc.tensor.transpose(ps[0:EXPERTS, t // 4, (t % 4) * P:(t % 4 + 1) * P], sg[:, t, :],
                                               ident[:])
                last.then_inc(pe_step, 1)

            def experts(n):
                with pe.Fori(0, NC // 2) as i:
                    def up(u, k):
                        C = n * NC + i * 2 + u
                        if k == 0:
                            pe.wait_ge(e_xh, nth(e_xh, C))
                            pe.wait_ge(e_xl, nth(e_xl, C))
                        s = k % 2
                        if k == 0:
                            pe.wait_ge(e_m, nth(e_m, C - 1, BLOCKS - 2))
                        elif k == 1:
                            pe.wait_ge(e_m, nth(e_m, C - 1, BLOCKS - 1))
                        if k >= SHARED:
                            mm(ps[:, 4 + s, :], esel[:, k - SHARED, :], gateT[:, ds((i * 2 + u) * CH, CH)],
                               start=True, stop=True)
                        for bank, wh, wl in ((0, w1h, w1l), (2, w2h, w2l)):
                            o = ps[:, bank + s, :]
                            mm(o, wh[:, k, :], xh[:, u, :], start=True, stop=False)
                            mm(o, wh[:, k, :], xl[:, u, :], start=False, stop=False)
                            last = mm(o, wl[:, k, :], xh[:, u, :], start=False, stop=True)
                        last.then_inc(e_h, 1)

                    def down(u, k):
                        C = n * NC + i * 2 + u
                        pe.wait_ge(e_m, nth(e_m, C, k))
                        if k == 0:
                            pe.wait_ge(e_out, nth(e_out, C - 2))
                        mm(ps[:, 6 + u, :], G("w3", k * P, P), hh[:, k % 2, :], start=k == 0, stop=k == BLOCKS - 1)\
                            .then_inc(e_w, 1)

                    todo = [(u, k) for u in range(2) for k in range(BLOCKS)]
                    up(*todo[0])
                    for before_, now in zip(todo, todo[1:]):
                        up(*now)
                        down(*before_)
                    down(*todo[-1])

            def choose():
                pe.wait_ge(gathered, 1)
                for g in range(2):
                    last = mm(ps[:, g, 0:8 * SC], T("wk"), xg[:, 8 * g:8 * g + 8, :], start=True, stop=True)
                last.then_inc(pe_step, 1)
                pe.wait_ge(sampled, 2)
                with pe.Fori(0, BATCH // 2) as i:
                    for u in range(2):
                        b = i * 2 + u
                        pe.wait_ge(b_qf, nth(b_qf, b - 2))
                        mm(ps[:, u, 0:SEQ], T("wq"), xa[:, ds(b * SEQ, SEQ)], start=True, stop=True).then_inc(b_q, 1)
                    for u in range(2):
                        b = i * 2 + u
                        pe.wait_ge(b_qf, nth(b_qf, b))
                        pe.wait_ge(b_kbd, nth(b_kbd, b))
                        for qt in range(2):
                            pe.wait_ge(b_m, nth(b_m, b - 1, qt))
                            for g in range(2):
                                last = mm(ps[:, 2 + 2 * qt + g, 0:8 * SC], qf[:, u, qt * P:(qt + 1) * P],
                                          kbd[:, u, 8 * g:8 * g + 8, :], start=True, stop=True)
                            last.then_inc(b_s, 1)
                pe.wait_ge(b_m, every(b_m, BATCH - 1))
                for g in range(2):
                    for qt in range(2):
                        last = nc.tensor.transpose(ps[:, 6, (2 * g + qt) * P:(2 * g + qt + 1) * P],
                                                   mall[:, qt, 8 * g:8 * g + 8, :], ident[:])
                last.then_inc(pe_step, 1)

            gate(pe, SETUP)
            for c in range(NC):
                pe.wait_ge(load_x[c], 16)
            norm(0, res)
            gate(pe, LN0)
            gate(pe, SPLIT)
            with pe.Fori(0, LAYERS) as l:
                pe.wait_ge(load_m, l * 48 + 48)
                pe.sem_inc(waited, 1)
                m1(l)
                gate(pe, of_layer(l, M1))
                m2(l)
                gate(pe, of_layer(l, M2))
                m3(l)
                gate(pe, of_layer(l, M3))
                norm(l * 2 + 1, xa)
                gate(pe, of_layer(l, LN1))
                pe.wait_ge(load_t, l * 16 + 16)
                pe.sem_inc(waited, 1)
                attention(l, False)
                gate(pe, of_layer(l, ATT))
                norm(l * 2 + 2, xa)
                gate(pe, of_layer(l, LN2))
                f(l)
                gate(pe, of_layer(l, F))
            norm(9, res, added=True)
            gate(pe, LN_F1)
            pe.wait_ge(load_g, 32)
            gates(0)
            gate(pe, GATE_F1)
            experts(0)
            gate(pe, EXP_F1)
            norm(10, res)
            gate(pe, LN_B)
            pe.wait_ge(load_t, (LAYERS + 1) * 16)
            choose()
            gate(pe, CHOOSE)
            attention(LAYERS, True)
            gate(pe, ATT_B)
            norm(11, res)
            gate(pe, LN_F2)
            gates(1)
            gate(pe, GATE_F2)
            experts(1)
            gate(pe, EXP_F2)

        @block.scalar
        def _(act):
            A = nc.scalar.activation

            def norm(n):
                with act.Fori(0, NC // 2) as i:
                    for u in range(2):
                        C = n * NC + i * 2 + u
                        act.wait_ge(ln_cen, nth(ln_cen, C))
                        act.wait_ge(ln_var, nth(ln_var, C - 2))
                        A(sq[:, u, :], ps[:, u, :], ACT.Square).then_inc(ln_sq, 1)
                    for u in range(2):
                        C = n * NC + i * 2 + u
                        act.wait_ge(ln_var, nth(ln_var, C))
                        act.wait_ge(ln_rstd, nth(ln_rstd, C - 2))
                        A(logv[:, u, :], ps[:, 2 + u, :], ACT.Ln, bias=acol[:, 3:4]).then_inc(ln_log, 1)
                        act.wait_ge(ln_log, nth(ln_log, C))
                        act.wait_ge(ln_unit, nth(ln_unit, C - 2))
                        A(rstd[:, u, :], logv[:, u, :], ACT.Exp, scale=-0.5).then_inc(ln_rstd, 1)

            def m1(l):
                act.preload_act_table(ACT.Silu)
                with act.Fori(0, NC // 2) as i:
                    for u in range(2):
                        C = l * NC + i * 2 + u
                        for o in range(4):
                            act.wait_ge(m1_psum, nth(m1_psum, C, o))
                            if o == 2:
                                act.wait_ge(m1_gate, nth(m1_gate, C - 2))
                            dst = xi[:, o, ds((i * 2 + u) * CH, CH)] if o < 2 else sres[:, u, o - 2, :]
                            A(dst, ps[:, 4 * u + o, :], ACT.Silu, bias=M("b_in", o, 1)).then_inc(m1_evac, 1)

            def m2(l):
                A(acol[:, 0:1], M("A_log"), ACT.Exp).then_inc(acol_exp, 1)
                act.wait_ge(acol_neg, l + CREDIT + 1)
                act.sem_inc(waited, 1)
                with act.Fori(0, NC // 2) as i:
                    for u in range(2):
                        C = l * NC + i * 2 + u
                        act.wait_ge(m2_dt, nth(m2_dt, C))
                        act.wait_ge(m2_log, nth(m2_log, C - 2))
                        A(absd[:, u, :], ps[:, u, :], ACT.Abs, bias=M("b_dt")).then_inc(m2_abs, 1)
                        act.wait_ge(m2_abs, nth(m2_abs, C))
                        A(absd[:, u, :], absd[:, u, :], ACT.Exp, scale=-1.0).then_inc(m2_exp, 1)
                        act.wait_ge(m2_exp, nth(m2_exp, C))
                        act.wait_ge(m2_delta, nth(m2_delta, C - 2))
                        A(logd[:, u, :], absd[:, u, :], ACT.Ln, bias=1.0).then_inc(m2_log, 1)
                    for u in range(2):
                        C = l * NC + i * 2 + u
                        act.wait_ge(m2_mean, nth(m2_mean, C))
                        act.wait_ge(m2_scan, nth(m2_scan, C - 2))
                        A(adisc[:, u, :], ps[:, 2 + u, 0:SEQ], ACT.Exp, scale=acol[:, 1:2]).then_inc(m2_adisc, 1)

            def m3(l):
                A(acol[:, 2:3], M("Dp"), ACT.Identity, bias=1.0).then_inc(acol_skip, 1)
                act.wait_ge(acol_skip, l + CREDIT + 1)
                act.sem_inc(waited, 1)
                with act.Fori(0, NC // 2) as i:
                    for u in range(2):
                        act.wait_ge(m3_res, nth(m3_res, l * NC + i * 2 + u - 2))
                        A(xd[:, u, :], xa[:, ds((i * 2 + u) * CH, CH)], ACT.Identity, scale=acol[:, 2:3],
                          bias=M("b_out")).then_inc(m3_skip, 1)

            def f(l):
                act.preload_act_table(ACT.Gelu)
                with act.Fori(0, NC // 2) as i:
                    for u in range(2):
                        C = l * NC + i * 2 + u
                        for o in range(4):
                            act.wait_ge(f_h, nth(f_h, C, o))
                            if o % 2 == 0:
                                act.wait_ge(f_acc, nth(f_acc, C - 1, o // 2))
                            A(hid[:, o // 2, o % 2, :], ps[:, o, :], ACT.Gelu, bias=M("b_f1", o, 1)).then_inc(f_g, 1)

            def attention(e, probsparse):
                def high(b):
                    B = e * BATCH + b
                    act.wait_ge(at_proj, nth(at_proj, B, 0))
                    act.wait_ge(at_spill, every(at_spill, B - 1))
                    for n, (t, bias, at_) in enumerate(((qs, "bq", 0), (ks, "bk", SEQ))):
                        A(t[:, 0, :], ps[:, 7, at_:at_ + SEQ], ACT.Identity, bias=T(bias)).then_inc(at_hi, 1)

                def minus_max(b, half):
                    B = e * BATCH + b
                    act.wait_ge(at_tp, nth(at_tp, B, half))
                    act.wait_ge(at_mx[half], every(at_mx[half], B - 1))
                    A(mh[:, half, :], ps[0:8, 7, 0:SEQ], ACT.Identity, scale=-1.0).then_inc(at_mh, 1)

                def exps(b, p):
                    B = e * BATCH + b
                    j = p // 2
                    act.wait_ge(at_sc, nth(at_sc, B, p))
                    act.wait_ge(at_pv, nth(at_pv, B, j - 2))
                    A(pt[:, j % 2, 2 * (p % 2):2 * (p % 2) + 2, :, :],
                      ps[:, 2 + 2 * (p % 2):4 + 2 * (p % 2), :], ACT.Exp, scale=QSCALE).then_inc(at_exp, 1)

                def evac(b, j):
                    B = e * BATCH + b
                    act.wait_ge(at_pv, nth(at_pv, B, j))
                    act.wait_ge(at_otp, nth(at_otp, B - 1, 1))
                    A(oraw[:, j, :], ps[:, 6, (j % 2) * SEQ:(j % 2 + 1) * SEQ], ACT.Copy).then_inc(at_oev, 1)

                def columns(b, r):
                    B = e * BATCH + b
                    act.wait_ge(at_aop, nth(at_aop, B - 1))
                    if probsparse:
                        act.wait_ge(at_sel, nth(at_sel, b))
                        A(onT[:], selo[:], ACT.Identity, bias=vmean[:, r:r + 1]).then_inc(at_ob, 1)
                    else:
                        act.wait_ge(at_obp, nth(at_obp, B))
                        A(onT[:], ps[:, 7, 0:SEQ], ACT.Copy).then_inc(at_ob, 1)

                def step(b, third, r, nxt=True, proj=True, first=False):
                    for p in range(8):
                        if p == 0:
                            minus_max(b, 1)
                        if p == 7 and not first:
                            columns(b - 1, (r + 2) % 3)
                        exps(b, p)
                        if p == 1:
                            if not first:
                                evac(b - 1, 3)
                            if proj:
                                high(b + 2)
                        if p in (3, 5, 7):
                            evac(b, p // 2 - 1)
                        if p == 5 and nxt:
                            minus_max(b + 1, 0)

                def last():
                    evac(15, 3)
                    columns(15, 0)

                for b in (0, 1):
                    high(b)
                minus_max(0, 0)
                sequences(act, step, last)

            def gates(n):
                act.wait_ge(pe_step, pe_steps[n])
                A(sg[:].rearrange("p t e -> p (t e)"), ps[:, 0, :], ACT.Sigmoid).then_inc(act_step, 1)

            def experts(n):
                act.preload_act_table(ACT.Silu)
                with act.Fori(0, NC // 2) as i:
                    def split(u):
                        C = n * NC + i * 2 + u
                        act.wait_ge(e_w, nth(e_w, C - 2, BLOCKS - 1))
                        A(xh[:, u, :], xa[:, ds((i * 2 + u) * CH, CH)], ACT.Copy).then_inc(e_xh, 1)
                    split(0)
                    for u in range(2):
                        C = n * NC + i * 2 + u
                        for k in range(BLOCKS):
                            if u == 0 and k == BLOCKS // 2:
                                split(1)
                            act.wait_ge(e_h, nth(e_h, C, k))
                            act.wait_ge(e_m, nth(e_m, C, k - 2))
                            A(sil[:, k % 2, :], ps[:, k % 2, :], ACT.Silu).then_inc(e_s, 1)

            gate(act, SETUP)
            act.preload_act_table_set("natural_log_exp_and_others")
            norm(0)
            gate(act, LN0)
            act.wait_ge(load_g, 32)
            for n, (h_, l_) in enumerate(((w1h, w1l), (w2h, w2l))):
                A(h_[:].rearrange("p k n -> p (k n)"), w12raw[:, n, :], ACT.Copy).then_inc(act_step, 1)
            gate(act, SPLIT)
            with act.Fori(0, LAYERS) as l:
                act.wait_ge(load_m, l * 48 + 48)
                act.sem_inc(waited, 1)
                m1(l)
                gate(act, of_layer(l, M1))
                act.preload_act_table_set("natural_log_exp_and_others")
                m2(l)
                gate(act, of_layer(l, M2))
                m3(l)
                gate(act, of_layer(l, M3))
                norm(l * 2 + 1)
                A(qv[0][:].rearrange("p h n -> p (h n)"), acol[:, 4:5].broadcast_to([P, HEADS * SEQ]), ACT.Copy)
                gate(act, of_layer(l, LN1))
                act.wait_ge(load_t, l * 16 + 16)
                act.sem_inc(waited, 1)
                attention(l, False)
                gate(act, of_layer(l, ATT))
                norm(l * 2 + 2)
                gate(act, of_layer(l, LN2))
                f(l)
                gate(act, of_layer(l, F))
            act.preload_act_table_set("natural_log_exp_and_others")
            norm(9)
            gate(act, LN_F1)
            gates(0)
            gate(act, GATE_F1)
            experts(0)
            gate(act, EXP_F1)
            act.preload_act_table_set("natural_log_exp_and_others")
            norm(10)
            A(qv[0][:].rearrange("p h n -> p (h n)"), acol[:, 4:5].broadcast_to([P, HEADS * SEQ]), ACT.Copy)
            gate(act, LN_B)
            act.wait_ge(load_t, (LAYERS + 1) * 16)
            act.wait_ge(pe_step, pe_steps["samples"])
            for g in range(2):
                A(ksg[:, 8 * g:8 * g + 8, :], ps[:, g, 0:8 * SC].rearrange("p (b s) -> p b s", s=SC), ACT.Identity,
                  bias=T("bk")).then_inc(sampled, 1)
            with act.Fori(0, BATCH // 2) as i:
                for u in range(2):
                    b = i * 2 + u
                    act.wait_ge(b_q, nth(b_q, b))
                    act.wait_ge(b_s, nth(b_s, b - 2, 1))
                    A(qf[:, u, :], ps[:, u, 0:SEQ], ACT.Identity, bias=T("bq")).then_inc(b_qf, 1)
            gate(act, CHOOSE)
            attention(LAYERS, True)
            gate(act, ATT_B)
            norm(11)
            gate(act, LN_F2)
            gates(1)
            gate(act, GATE_F2)
            experts(1)
            gate(act, EXP_F2)

        @block.vector
        def _(dve):
            V = nc.vector
            chain = [0]

            def link(ins):
                chain[0] += 1
                ins.then_inc(dve_step, 1)
                dve.wait_ge(dve_step, chain[0])

            def norm(n, dst=None, added=False, gain=None):
                if added:
                    with dve.Fori(0, NC) as c:
                        V.tensor_tensor(res[:, ds(c * CH, CH)], res[:, ds(c * CH, CH)], xa[:, ds(c * CH, CH)],
                                        ALU.add).then_inc(add_res, 1)
                with dve.Fori(0, NC // 2) as i:
                    for u in range(2):
                        C = n * NC + i * 2 + u
                        dve.wait_ge(ln_rstd, nth(ln_rstd, C))
                        if dst is None:
                            dve.wait_ge(ln_aff, nth(ln_aff, C - NC - 2))
                            o = unit[:, u, :]
                        else:
                            o = dst[:, ds((i * 2 + u) * CH, CH)]
                        V.tensor_tensor(o, ps[:, u, :], rstd[:, u, :], ALU.mult).then_inc(ln_unit, 1)
                    for u in range(2 if dst is None else 0):
                        dve.wait_ge(ln_unit, nth(ln_unit, n * NC + i * 2 + u))
                        V.tensor_scalar(xa[:, ds((i * 2 + u) * CH, CH)], unit[:, u, :], M(gain[0]), M(gain[1]),
                                        ALU.mult, ALU.add).then_inc(ln_aff, 1)

            def m1(l):
                with dve.Fori(0, NC // 2) as i:
                    for u in range(2):
                        C = l * NC + i * 2 + u
                        dve.wait_ge(m1_evac, nth(m1_evac, C, 3))
                        c = i * 2 + u
                        V.tensor_tensor(zz[:, :, ds(c * CH, CH)], xi[:, :, ds(c * CH, CH)], sres[:, u, :, :],
                                        ALU.mult).then_inc(m1_gate, 1)

            def m2(l):
                dve.wait_ge(acol_exp, nth(acol_exp, l))
                V.tensor_scalar(acol[:, 1:2], acol[:, 0:1], -1.0, None, ALU.mult).then_inc(acol_neg, 1)
                with dve.Fori(0, NC // 2) as i:
                    for u in range(2):
                        C = l * NC + i * 2 + u
                        dve.wait_ge(m2_abs, nth(m2_abs, C))
                        dve.wait_ge(m2_delta, nth(m2_delta, C - 2))
                        V.tensor_scalar(posd[:, u, :], ps[:, u, :], M("b_dt"), 0.0, ALU.add, ALU.max)\
                            .then_inc(m2_pos, 1)
                        dve.wait_ge(m2_u, nth(m2_u, C))
                        dve.wait_ge(m2_scan, nth(m2_scan, C - 2))
                        V.tensor_scalar(uin[:, u, :], ps[:, 4 + u, 0:SEQ], M("b_xp"), None, ALU.add)\
                            .then_inc(m2_uin, 1)
                        dve.wait_ge(m2_pos, nth(m2_pos, C))
                        dve.wait_ge(m2_log, nth(m2_log, C))
                        dve.wait_ge(m2_mean, nth(m2_mean, C - 2))
                        V.tensor_tensor(delta[:, u, :], posd[:, u, :], logd[:, u, :], ALU.add).then_inc(m2_delta, 1)
                    for u in range(2):
                        C = l * NC + i * 2 + u
                        dve.wait_ge(m2_adisc, nth(m2_adisc, C))
                        dve.wait_ge(m2_uin, nth(m2_uin, C))
                        V.tensor_tensor_scan(st[:, ds((i * 2 + u) * SEQ, SEQ)], adisc[:, u, :], uin[:, u, :], 0.0,
                                             ALU.mult, ALU.add).then_inc(m2_scan, 1)

            def m3(l):
                with dve.Fori(0, NC // 2) as i:
                    for u in range(2):
                        C = l * NC + i * 2 + u
                        c = i * 2 + u
                        dve.wait_ge(m3_sum, nth(m3_sum, C))
                        dve.wait_ge(m3_out, nth(m3_out, C - 2))
                        V.tensor_tensor(y[:, u, :, :], zz[:, :, ds(c * CH, CH)],
                                        ps[:, u, :].unsqueeze(1).broadcast_to([P, 2, CH]), ALU.mult)\
                            .then_inc(m3_y, 1)
                    for u in range(2):
                        C = l * NC + i * 2 + u
                        dve.wait_ge(m3_out, nth(m3_out, C))
                        dve.wait_ge(m3_skip, nth(m3_skip, C))
                        V.tensor_tensor(xa[:, ds((i * 2 + u) * CH, CH)], ps[:, 2 + u, :], xd[:, u, :], ALU.add)\
                            .then_inc(m3_res, 1)

            def f(l):
                with dve.Fori(0, NC // 2) as i:
                    for u in range(2):
                        C = l * NC + i * 2 + u
                        c = i * 2 + u
                        dve.wait_ge(f_acc, nth(f_acc, C, 1))
                        V.scalar_tensor_tensor(xa[:, ds(c * CH, CH)], ps[:, 4 + u, :], M("b_f2"),
                                               xa[:, ds(c * CH, CH)], ALU.add, ALU.add).then_inc(f_out, 1)

            def attention(e, probsparse):
                stream = res if probsparse else xa

                def low(b, n):
                    B = e * BATCH + b
                    t, bias, at_ = ((qs, "bq", 0), (ks, "bk", SEQ))[n]
                    dve.wait_ge(at_hi, nth(at_hi, B, 1))
                    V.scalar_tensor_tensor(t[:, 1, :], ps[:, 7, at_:at_ + SEQ], T(bias), t[:, 0, :].bitcast(F32),
                                           ALU.add, ALU.subtract).then_inc(at_lo, 1)

                def lay_v(b, r):
                    B = e * BATCH + b
                    dve.wait_ge(at_proj, nth(at_proj, B, 1))
                    dve.wait_ge(at_pv, nth(at_pv, B - 3, 3))
                    V.tensor_tensor(vx[r][:, :, :, 0:DH],
                                    ps[:, 7, 0:SEQ].rearrange("p (t h d) -> p t h d", t=2, d=DH),
                                    T("bvb").rearrange("p (h d) -> p h d", d=DH).unsqueeze(1)
                                    .broadcast_to([P, 2, HEADS, DH]), ALU.add).then_inc(at_lo, 1)

                def minus_max_low(b, half):
                    B = e * BATCH + b
                    dve.wait_ge(at_mh, nth(at_mh, B, half))
                    V.scalar_tensor_tensor(ml[:, half, :], ps[0:8, 7, 0:SEQ], -1.0, mh[:, half, :].bitcast(F32),
                                           ALU.mult, ALU.subtract).then_inc(at_ml, 1)

                def maxima(b, h, r):
                    B = e * BATCH + b
                    dve.wait_ge(at_am, nth(at_am, B, h))
                    V.tensor_reduce(mxs[:, r, h, :], ps[:, h % 2, :].rearrange("p (t k) -> p t k", t=2), AX.X, ALU.max)\
                        .then_inc(at_max, 1)

                def divide(b, qt):
                    B = e * BATCH + b
                    o = ps[:, 7, :].rearrange("p (h c) -> p h c", c=32)
                    dve.wait_ge(at_otp, nth(at_otp, B, qt))
                    dve.wait_ge(at_ot, nth(at_ot, B, qt - 1))
                    V.reciprocal(rec[:].unsqueeze(2), o[:, :, DH:DH + 1]).then_inc(at_rec, 1)
                    dve.wait_ge(at_rec, nth(at_rec, B, qt))
                    dve.wait_ge(at_obp, nth(at_obp, B - 1))
                    V.tensor_tensor(ontok[:, qt, :].rearrange("p (h d) -> p h d", d=DH), o[:, :, 0:DH],
                                    rec[:].unsqueeze(2).broadcast_to([P, HEADS, DH]), ALU.mult)\
                        .then_inc(at_ot, 1)

                def select(b, r):
                    dve.wait_ge(at_obp, nth(at_obp, e * BATCH + b))
                    dve.wait_ge(at_mask, every(at_mask, b))
                    dve.wait_ge(at_ob, nth(at_ob, e * BATCH + b - 1))
                    V.scalar_tensor_tensor(selo[:], ps[:, 7, 0:SEQ], vmean[:, r:r + 1], maskb[:],
                                           ALU.subtract, ALU.mult).then_inc(at_sel, 1)

                def add_out(b):
                    B = e * BATCH + b
                    dve.wait_ge(at_aop, nth(at_aop, B))
                    V.scalar_tensor_tensor(stream[:, ds(b * SEQ, SEQ)], ps[:, 7, 0:SEQ], T("bo"),
                                           stream[:, ds(b * SEQ, SEQ)], ALU.add, ALU.add).then_inc(at_ao, 1)

                def step(b, third, r, nxt=True, proj=True, first=False):
                    rn = (r + 1) % 3
                    for p in range(8):
                        if p == 0:
                            minus_max_low(b, 1)
                            if probsparse and proj:
                                sum_x(b + 2, (r + 2) % 3)
                        if nxt:
                            maxima(b + 1, 2 * p, rn)
                            maxima(b + 1, 2 * p + 1, rn)
                        if p == 1 and proj:
                            low(b + 2, 0)
                            low(b + 2, 1)
                        if p in (2, 3) and not first:
                            divide(b - 1, p - 2)
                        if p == 4 and proj:
                            lay_v(b + 2, (r + 2) % 3)
                        if p == 5:
                            if nxt:
                                minus_max_low(b + 1, 0)
                            if probsparse:
                                dve.wait_ge(at_vmp, nth(at_vmp, b))
                                dve.wait_ge(at_ob, nth(at_ob, e * BATCH + b - 3))
                                V.tensor_scalar(vmean[:, r:r + 1], ps[:, 7, SEQ:SEQ + 1], 1.0 / SEQ, T("bv"),
                                                ALU.mult, ALU.add).then_inc(at_vm, 1)
                        if p == 6 and probsparse and not first:
                            select(b - 1, (r + 2) % 3)
                        if p == 7 and not first:
                            add_out(b - 1)

                def last():
                    divide(15, 0)
                    divide(15, 1)
                    if probsparse:
                        select(15, 0)
                    add_out(15)

                def sum_x(b, r):
                    dve.wait_ge(at_xs, nth(at_xs, e * BATCH + b))
                    V.tensor_reduce(xsum[:, r:r + 1], xs[:], AX.X, ALU.add).then_inc(at_xm, 1)

                for b in (0, 1):
                    if probsparse:
                        sum_x(b, b)
                    low(b, 0)
                    low(b, 1)
                    lay_v(b, b)
                for h in range(HEADS):
                    maxima(0, h, 0)
                minus_max_low(0, 0)
                sequences(dve, step, last)

            def gates(n):
                dve.wait_ge(act_step, act_steps[n])
                link(V.tensor_tensor(se[:], sg[:], G("ebias").unsqueeze(1).broadcast_to([P, ntile, EXPERTS]), ALU.add))
                for t in range(ntile):
                    last = V.max(m8[:, t, :], se[:, t, :])
                link(last)
                second = m8[:, :, 1:2].broadcast_to([P, ntile, EXPERTS])
                V.tensor_tensor(gt[:], se[:], second, ALU.is_gt)
                link(V.tensor_tensor(eq[:], se[:], second, ALU.is_equal))
                flat = "p t e -> p (t e)"
                link(V.tensor_tensor_scan(cum[:].rearrange(flat), eq[:].rearrange(flat), eq[:].rearrange(flat), 0.0,
                                          ALU.add, ALU.max))
                V.memset(before[:, 0:1], 0.0)
                V.tensor_copy(before[:, 1:ntile], cum[:, 0:ntile - 1, EXPERTS - 1])
                link(V.tensor_reduce(cnt[:], gt[:], AX.X, ALU.add))
                link(V.tensor_tensor(before[:], before[:], cnt[:], ALU.subtract))
                link(V.tensor_tensor(cum[:], cum[:], before[:].unsqueeze(2).broadcast_to([P, ntile, EXPERTS]),
                                     ALU.subtract))
                link(V.scalar_tensor_tensor(eq[:], cum[:], 2.0, eq[:], ALU.is_le, ALU.mult))
                link(V.tensor_tensor(gt[:], gt[:], eq[:], ALU.add))
                V.tensor_tensor(sg[:], sg[:], gt[:], ALU.mult).then_inc(gates_ready, 1)
                dve.wait_ge(pe_step, pe_steps[n] + 1)
                for c in range(NC):
                    last = V.tensor_copy(gateT[0:EXPERTS, c * CH:(c + 1) * CH], ps[0:EXPERTS, c, :])
                link(last)
                for c in range(NC):
                    V.tensor_tensor(gateT[32:32 + EXPERTS, c * CH:(c + 1) * CH], ps[0:EXPERTS, c, :],
                                    gateT[0:EXPERTS, c * CH:(c + 1) * CH].bitcast(F32), ALU.subtract)
                for row in (0, 32):
                    V.tensor_copy(esel[row:row + EXPERTS], ident[0:EXPERTS, 0:EXPERTS].unsqueeze(2)
                                  .broadcast_to([EXPERTS, EXPERTS, P]))

            def experts(n):
                with dve.Fori(0, NC // 2) as i:
                    def split(u):
                        dve.wait_ge(e_xh, nth(e_xh, n * NC + i * 2 + u))
                        V.tensor_tensor(xl[:, u, :], xa[:, ds((i * 2 + u) * CH, CH)], xh[:, u, :].bitcast(F32),
                                        ALU.subtract).then_inc(e_xl, 1)
                    split(0)
                    for u in range(2):
                        C = n * NC + i * 2 + u
                        c = i * 2 + u
                        for k in range(BLOCKS):
                            if u == 0 and k == BLOCKS // 2:
                                split(1)
                            s = k % 2
                            dve.wait_ge(e_s, nth(e_s, C, k))
                            dve.wait_ge(e_w, nth(e_w, C, k - 2))
                            if k < SHARED:
                                V.tensor_tensor(hh[:, s, :], ps[:, 2 + s, :], sil[:, s, :], ALU.mult)\
                                    .then_inc(e_m, 1)
                            else:
                                dve.wait_ge(e_m, nth(e_m, C, k - 2))
                                V.tensor_tensor(su[:, s, :], ps[:, 2 + s, :], sil[:, s, :], ALU.mult)\
                                    .then_inc(e_t, 1)
                                dve.wait_ge(e_t, nth(e_t, C, k - SHARED))
                                V.tensor_tensor(hh[:, s, :], ps[:, 4 + s, :], su[:, s, :], ALU.mult)\
                                    .then_inc(e_m, 1)
                        dve.wait_ge(e_w, nth(e_w, C, BLOCKS - 1))
                        V.tensor_tensor(res[:, ds(c * CH, CH)], ps[:, 6 + u, :], res[:, ds(c * CH, CH)], ALU.add)\
                            .then_inc(e_out, 1)

            def choose():
                dve.wait_ge(load_i, 16)
                link(V.tensor_copy(idx_f[:], idx_i[:]))
                link(V.tensor_scalar(idx_n[:], idx_f[:], 0.0, float(SEQ), ALU.is_lt, ALU.mult))
                link(V.tensor_tensor(idx_f[:], idx_f[:], idx_n[:], ALU.add))
                link(V.tensor_scalar(idx_n[:], idx_f[:], 0.0, float(SEQ - 1), ALU.max, ALU.min))
                V.tensor_copy(idx_c[:], idx_n[:]).then_inc(idx_ready, 1)
                dve.wait_ge(taken, 1)
                link(V.tensor_reduce(mxq[:, 0, 0, :].rearrange("p (b o) -> p b o", o=1), xg[:, :, 0:SAMPLES], AX.X,
                                     ALU.add))
                V.tensor_scalar(xg[:, :, SAMPLES], mxq[:, 0, 0, :], 1.0 / SAMPLES, None, ALU.mult)\
                    .then_inc(gathered, 1)
                dve.wait_ge(sampled, 2)
                with dve.Fori(0, BATCH // 2) as i:
                    for u in range(2):
                        b = i * 2 + u
                        dve.wait_ge(b_s, nth(b_s, b - 2, 1))
                        V.tensor_tensor(kbd[:, u], ksg[:, ds(b, 1), :].broadcast_to([P, HEADS, SC]),
                                        headmask[:].unsqueeze(2).broadcast_to([P, HEADS, SC]), ALU.mult)\
                            .then_inc(b_kbd, 1)
                    for u in range(2):
                        b = i * 2 + u
                        for qt in range(2):
                            s = ps[:, 2 + 2 * qt:4 + 2 * qt, 0:8 * SC].rearrange("p g (h s) -> p g h s", s=SC)
                            dve.wait_ge(b_s, nth(b_s, b, qt))
                            dve.wait_ge(b_m, nth(b_m, b - 1, qt))
                            V.tensor_reduce(mxq[:, u, qt, :].rearrange("p (g h) -> p g h", g=2), s[:, :, :, 0:SAMPLES],
                                            AX.X, ALU.max).then_inc(b_mx, 1)
                            dve.wait_ge(b_mx, nth(b_mx, b, qt))
                            V.tensor_tensor(mall[:, qt, ds(b, 1), :].rearrange("p o (g h) -> p (o g) h", g=2),
                                            mxq[:, u, qt, :].rearrange("p (g h) -> p g h", g=2),
                                            s[:, :, :, SAMPLES], ALU.subtract).then_inc(b_m, 1)
                dve.wait_ge(pe_step, pe_steps["rows"])
                V.tensor_copy(mwork[:], ps[:, 6, :].rearrange("p (g q) -> p g q", g=2))
                link(V.tensor_copy(mrow[:], ps[:, 6, :].rearrange("p (g q) -> p g q", g=2)))
                for rnd in range((TOP + 7) // 8):
                    for g in range(2):
                        last = V.max(mtop[:, g, :], mwork[:, g, :])
                    link(last)
                    if 8 * rnd + 8 < TOP:
                        for g in range(2):
                            last = V.match_replace(mwork[:, g, :], mtop[:, g, :], mwork[:, g, :], -3.0e38)
                        link(last)
                least = (TOP - 1) % 8
                for g in range(2):
                    V.tensor_scalar(mgt[:, g, :], mrow[:, g, :], mtop[:, g, least:least + 1], None, ALU.is_gt)
                    last = V.tensor_scalar(meq[:, g, :], mrow[:, g, :], mtop[:, g, least:least + 1], None, ALU.is_equal)
                link(last)
                V.tensor_reduce(mneed[:].unsqueeze(2), mgt[:], AX.X, ALU.add)
                for g in range(2):
                    last = V.tensor_tensor_scan(mcum[:, g, :], meq[:, g, :], meq[:, g, :], 0.0, ALU.add, ALU.max)
                link(last)
                link(V.tensor_scalar(mneed[:], mneed[:], -1.0, float(TOP), ALU.mult, ALU.add))
                for g in range(2):
                    last = V.scalar_tensor_tensor(mcum[:, g, :], mcum[:, g, :], mneed[:, g:g + 1], meq[:, g, :],
                                                  ALU.is_le, ALU.mult)
                link(last)
                V.tensor_tensor(mwork[:], mgt[:], mcum[:], ALU.add).then_inc(mask_ready, 1)

            V.memset(acol[:, 3:4], EPS)
            V.memset(acol[:, 4:5], 0.0)
            gate(dve, SETUP)
            norm(0, xa)
            gate(dve, LN0)
            for n, (h_, l_) in enumerate(((w1h, w1l), (w2h, w2l))):
                dve.wait_ge(act_step, n + 1)
                V.tensor_tensor(l_[:].rearrange("p k n -> p (k n)"), w12raw[:, n, :],
                                h_[:].rearrange("p k n -> p (k n)").bitcast(F32), ALU.subtract)
            gate(dve, SPLIT)
            with dve.Fori(0, LAYERS) as l:
                dve.wait_ge(load_m, l * 48 + 48)
                dve.sem_inc(waited, 1)
                m1(l)
                gate(dve, of_layer(l, M1))
                m2(l)
                gate(dve, of_layer(l, M2))
                m3(l)
                gate(dve, of_layer(l, M3))
                V.memset(qv[1][:].bitcast(F32), 0.0)
                norm(l * 2 + 1, gain=("g1", "be1"))
                gate(dve, of_layer(l, LN1))
                dve.wait_ge(load_t, l * 16 + 16)
                dve.sem_inc(waited, 1)
                attention(l, False)
                gate(dve, of_layer(l, ATT))
                norm(l * 2 + 2, gain=("g2", "be2"))
                gate(dve, of_layer(l, LN2))
                f(l)
                gate(dve, of_layer(l, F))
            norm(9, xa, added=True)
            gate(dve, LN_F1)
            dve.wait_ge(load_g, 32)
            gates(0)
            gate(dve, GATE_F1)
            experts(0)
            gate(dve, EXP_F1)
            V.memset(qv[1][:].bitcast(F32), 0.0)
            norm(10, xa)
            gate(dve, LN_B)
            dve.wait_ge(load_t, (LAYERS + 1) * 16)
            choose()
            gate(dve, CHOOSE)
            attention(LAYERS, True)
            gate(dve, ATT_B)
            norm(11, xa)
            gate(dve, LN_F2)
            gates(1)
            gate(dve, GATE_F2)
            experts(1)
            gate(dve, EXP_F2)

        @block.gpsimd
        def _(pool):
            G_ = nc.gpsimd

            def clear_operands(n):
                for r in range(3):
                    G_.memset(vx[r][:], 0.0)
                G_.memset(qv[2][:].bitcast(F32), 0.0).then_inc(pool_step, 1)
                pool.wait_ge(pool_step, n * 3 + 3)
                pool.sem_inc(waited, 1)
                for r in range(3):
                    last = G_.memset(vx[r][:, :, :, DH:DH + 1], 1.0)
                last.then_inc(pool_step, 1)
                pool.wait_ge(pool_step, n * 3 + 4)
                pool.sem_inc(waited, 1)
                for r in range(3):
                    last = G_.memset(k4[r][96:P].bitcast(F32), 1.0)
                last.then_inc(pool_step, 1)
                pool.wait_ge(pool_step, n * 3 + 5)
                pool.sem_inc(waited, 1)

            def attention(e):
                with pool.Fori(0, BATCH) as b:
                    pool.wait_ge(at_proj, nth(at_proj, e * BATCH + b - 1, 1))
                    G_.tensor_copy(xs[:], xa[:, ds(b * SEQ, SEQ)]).then_inc(at_xs, 1)

            def clear_gates():
                G_.memset(gateT[:].bitcast(F32), 0.0)
                G_.memset(esel[:].bitcast(F32), 0.0)

            def diagonal(t, value):
                G_.affine_select(out=t, in_=t, compare_op=ALU.not_equal, fill=value, base=0, pattern=[[-1, P]],
                                 channel_multiplier=1)

            G_.memset(wxp[:], 0.0)
            G_.memset(ident[:], 0.0)
            G_.memset(center[:], -1.0 / P)
            G_.memset(average[:], 1.0 / P)
            G_.memset(halfavg[:], 0.0)
            G_.memset(halfsum[:], 0.0).then_inc(setup_done, 1)
            pool.wait_ge(setup_done, 1)
            diagonal(ident[:], 1.0)
            diagonal(center[:], 1.0 - 1.0 / P)
            for hb in range(2):
                G_.memset(halfavg[:, hb, hb * STATES:(hb + 1) * STATES], 1.0 / P)
            for hb in range(2):
                pool.drain().then_inc(pool_step, 1)
                pool.wait_ge(pool_step, hb + 1)
                G_.memset(halfsum[hb * STATES:(hb + 1) * STATES, hb, :], 1.0)
            gate(pool, SETUP)
            gate(pool, LN0)
            gate(pool, SPLIT)
            with pool.Fori(0, LAYERS) as l:
                pool.wait_ge(load_m, l * 48 + 48)
                pool.sem_inc(waited, 1)
                gate(pool, of_layer(l, M1))
                gate(pool, of_layer(l, M2))
                gate(pool, of_layer(l, M3))
                clear_operands(l)
                gate(pool, of_layer(l, LN1))
                attention(l)
                gate(pool, of_layer(l, ATT))
                gate(pool, of_layer(l, LN2))
                gate(pool, of_layer(l, F))
            clear_gates()
            gate(pool, LN_F1)
            gate(pool, GATE_F1)
            gate(pool, EXP_F1)
            clear_operands(LAYERS)
            gate(pool, LN_B)
            G_.memset(headmask[:], 1.0).then_inc(pool_step, 1)
            pool.wait_ge(pool_step, 3 * LAYERS + 6)
            G_.affine_select(out=headmask[:], in_=headmask[:], compare_op=ALU.is_ge, fill=0.0, base=0,
                             pattern=[[-DH, HEADS]], channel_multiplier=1).then_inc(pool_step, 1)
            pool.wait_ge(pool_step, 3 * LAYERS + 7)
            G_.affine_select(out=headmask[:], in_=headmask[:], compare_op=ALU.is_ge, fill=0.0, base=DH - 1,
                             pattern=[[DH, HEADS]], channel_multiplier=-1)
            pool.wait_ge(idx_ready, 1)
            xn = xa[:].rearrange("p (b s) -> p b s", s=SEQ)
            with pool.Fori(0, SAMPLES) as s:
                at_ = pool.value_load(idx_c[0:1, ds(s, 1)], min_val=0, max_val=SEQ - 1)
                G_.tensor_copy(xg[:, :, ds(s, 1)], xn[:, :, ds(at_, 1)]).then_inc(column_taken, 1)
            pool.wait_ge(column_taken, SAMPLES)
            pool.sem_inc(taken, 1)
            gate(pool, CHOOSE)
            attention(LAYERS)
            gate(pool, ATT_B)
            clear_gates()
            gate(pool, LN_F2)
            gate(pool, GATE_F2)
            gate(pool, EXP_F2)


def kernel(**inputs):
    import numpy as np
    import concourse.bacc as bacc
    from concourse.bass_utils import run_bass_kernel_spmd

    a = {k[len("L0_"):]: np.asarray(v) for k, v in inputs.items()}
    m = {k[len("attn_a_"):]: v for k, v in a.items() if k.startswith("attn_a_")}
    b = {k[len("attn_b_"):]: v for k, v in a.items() if k.startswith("attn_b_")}
    g = {k[len("ffn_"):]: v for k, v in a.items() if k.startswith("ffn_")}

    def fill(out, table, **parts):
        for name, part in parts.items():
            at, n = table[name]
            out[:, at:at + n] = np.asarray(part).reshape(P, n)

    def blocks(w):
        return w.T.reshape(-1, P, w.shape[0]).transpose(1, 0, 2)

    def columns(v):
        return v.reshape(-1, P).T

    mws = np.zeros((LAYERS + 1, P, MCOLS), np.float32)
    xps = np.zeros((LAYERS + 1, P, 2, STATES), np.float32)
    tws = np.zeros((LAYERS + 1, P, TCOLS), np.float32)
    for l in range(LAYERS):
        fill(mws[l], MW, win=m["W_in"][l].T, wdt=blocks(m["W_dt"][l]), wout=blocks(m["W_out"][l]), wf1=m["W_f1"][l].T,
             wf2=blocks(m["W_f2"][l]), b_in=columns(m["b_in"][l]), b_dt=m["b_dt"][l], b_xp=np.tile(m["b_xp"][l], 2),
             b_out=m["b_out"][l], Dp=m["Dp"][l], A_log=np.tile(m["A_log"][l], 2), g1=m["g1"][l], be1=m["be1"][l],
             g2=m["g2"][l], be2=m["be2"][l], b_f1=columns(m["b_f1"][l]), b_f2=m["b_f2"][l])
        xps[l] = blocks(m["W_xp"][l])
        wq, wk, wv = (m["W_qkv"][l][k * D:(k + 1) * D].T for k in range(3))
        bq, bk, bv = (m["b_qkv"][l][k * D:(k + 1) * D] for k in range(3))
        fill(tws[l], TW, wq=wq, wk=wk, wv=wv, wo=m["W_ao"][l].T, bq=bq, bk=bk, bo=m["b_ao"][l], bv=bv,
             bvb=np.broadcast_to(bv, (P, D)))
    mws[LAYERS], xps[LAYERS] = mws[LAYERS - 1], xps[LAYERS - 1]
    fill(tws[LAYERS], TW, wq=b["Wq"].T, wk=b["Wk"].T, wv=b["Wv"].T, wo=b["Wo"].T, bq=b["bq"], bk=b["bk"], bo=b["bo"], bv=b["bv"],
         bvb=np.broadcast_to(b["bv"], (P, D)))
    w12 = np.stack([np.concatenate([g[f"shared_w{k}"][0], g[f"routed_w{k}"].transpose(1, 0, 2).reshape(P, -1)], 1)
                    for k in (1, 2)], 1)
    gws = np.zeros((P, GCOLS), np.float32)
    w3 = np.concatenate([g["shared_w3"][0].reshape(SHARED, P, D), g["routed_w3"]], 0).transpose(1, 0, 2)
    fill(gws, GW, w3=w3, router=g["router_w"], ebias=np.broadcast_to(g["expert_bias"], (P, EXPERTS)))
    arrays = {
        "x_in": np.ascontiguousarray(m["x"].reshape(TOK, D).T), "mw_in": mws, "xp_in": xps, "tw_in": tws,
        "w12_in": np.ascontiguousarray(w12), "gw_in": gws,
        "idx_in": np.ascontiguousarray(np.broadcast_to(b["sample_idx"], (P, SAMPLES))),
    }
    nc = bacc.Bacc("TRN2", target_bir_lowering=False, num_devices=1)
    args = [nc.dram_tensor(n, v.shape, mybir.dt.from_np(v.dtype), kind="ExternalInput").ap() for n, v in arrays.items()]
    args.append(nc.dram_tensor("out", (P, TOK), F32, kind="ExternalOutput").ap())
    build_program(nc, *args)
    r = run_bass_kernel_spmd(nc, [arrays], core_ids=[0])
    return r.results[0]["out"].T.reshape(BATCH, SEQ, D)
```

```python
from contextlib import ExitStack

import concourse.bass as bass
from concourse import mybir

F32 = mybir.dt.float32
F32R = mybir.dt.float32r
I32 = mybir.dt.int32
ALU = mybir.AluOpType
ACT = mybir.ActivationFunctionType
AX = mybir.AxisListType
ds = bass.ds

P = 128
BATCH, SEQ, D = 16, 256, 128
TOK = BATCH * SEQ
CH = 512
NC = TOK // CH
LAYERS, STATES, HEADS, DH = 4, 64, 16, 8
DI, DF = 2 * D, 4 * D
EXPERTS, SHARED = 16, 4
BLOCKS = EXPERTS + SHARED
SAMPLES = TOP = 35
SC = SAMPLES + 1
EPS = 1e-5
QSCALE = 1.0 / DH ** 0.5
CREDIT = 4

MW = {}
for _name, _n in (("win", 2 * DI), ("wdt", 2 * D), ("wout", 2 * D), ("b_in", 4), ("b_dt", 1), ("b_xp", 1),
                  ("b_out", 1), ("Dp", 1), ("A_log", 1), ("wf1", DF), ("wf2", DF), ("g1", 1), ("be1", 1), ("g2", 1),
                  ("be2", 1), ("b_f1", 4), ("b_f2", 1)):
    MW[_name] = (sum(n for _, n in MW.values()), _n)
MCOLS = sum(n for _, n in MW.values())
MSPLIT = MW["wf1"][0]
TW = {}
for _name, _n in (("wq", D), ("wk", D), ("wv", D), ("wo", D), ("bvb", D), ("bq", 1), ("bk", 1), ("bo", 1), ("bv", 1)):
    TW[_name] = (sum(n for _, n in TW.values()), _n)
TCOLS = sum(n for _, n in TW.values())
GW = {}
for _name, _n in (("w3", BLOCKS * D), ("router", EXPERTS), ("ebias", EXPERTS)):
    GW[_name] = (sum(n for _, n in GW.values()), _n)
GCOLS = sum(n for _, n in GW.values())


def build_program(nc, x_d, mw_d, xp_d, tw_d, w12_d, gw_d, idx_d, out_d):
    ctx = ExitStack()
    with ctx:
        def sem(name):
            return ctx.enter_context(nc.semaphore(name))

        base = (nc.sbuf_base + 63) // 64 * 64
        top = [base]

        def at(name, shape, dt=F32, where=None):
            where = top if where is None else where
            n = 4
            for s in shape[1:]:
                n *= s
            t = nc.alloc_sbuf_tensor_at(name, shape, dt, offset=where[0])
            where[0] += (n + 63) // 64 * 64
            return t

        res = at("res", [P, TOK])
        xa = at("xa", [P, TOK])
        mw = at("mw", [P, MCOLS])
        tw = at("tw", [P, TCOLS])
        wxp = at("wxp", [P, 2, 2, P])
        w1h = at("w1h", [P, BLOCKS, D], F32R)
        w1l = at("w1l", [P, BLOCKS, D], F32R)
        w2h = at("w2h", [P, BLOCKS, D], F32R)
        w2l = at("w2l", [P, BLOCKS, D], F32R)
        gw = at("gw", [P, GCOLS])
        ident = at("ident", [P, P])
        center = at("center", [P, P])
        average = at("average", [P, P])
        halfavg = at("halfavg", [P, 2, P])
        halfsum = at("halfsum", [P, 2, P])
        acol = at("acol", [P, 5])
        work = top[0]
        end = nc.sbuf_usable_end

        def M(name, k=0, n=None):
            a, m = MW[name]
            return mw[:, a + k:a + k + (m if n is None else n)]

        def T(name, k=0, n=None):
            a, m = TW[name]
            return tw[:, a + k:a + k + (m if n is None else n)]

        def G(name, k=0, n=None):
            a, m = GW[name]
            return gw[:, a + k:a + k + (m if n is None else n)]

        w = [work + (3 * 16 + 3 * 4 + 3 * 4) * 1024]
        sq = at("sq", [P, 2, CH], where=w)
        logv = at("logv", [P, 2, CH], where=w)
        rstd = at("rstd", [P, 2, CH], where=w)
        unit = at("unit", [P, 2, CH], where=w)
        w = [work]
        xi = at("xi", [P, 2, TOK], where=w)
        zz = at("zz", [P, 2, TOK], where=w)
        st = at("st", [P, NC * SEQ], where=w)
        absd = at("absd", [P, 2, CH], where=w)
        logd = at("logd", [P, 2, CH], where=w)
        posd = at("posd", [P, 2, CH], where=w)
        delta = at("delta", [P, 2, CH], where=w)
        shared_at = w[0]
        sres = at("sres", [P, 2, 2, CH], where=w)
        w = [shared_at]
        y = at("y", [P, 2, 2, CH], where=w)
        xd = at("xd", [P, 2, CH], where=w)
        adisc = at("adisc", [P, 2, SEQ], where=w)
        uin = at("uin", [P, 2, SEQ], where=w)
        assert w[0] <= end
        w = [work]
        hid = at("hid", [P, 2, 2, CH], where=w)
        w = [work]
        w12raw = at("w12raw", [P, 2, BLOCKS * D], where=w)
        w = [work]
        gateT = at("gateT", [64, TOK], F32R, where=w)
        esel = at("esel", [64, EXPERTS, P], F32R, where=w)
        xh = at("xh", [P, 2, CH], F32R, where=w)
        xl = at("xl", [P, 2, CH], F32R, where=w)
        sil = at("sil", [P, 2, CH], where=w)
        su = at("su", [P, 2, CH], where=w)
        hh = at("hh", [P, 2, CH], where=w)
        ntile = TOK // P
        sg = at("sg", [P, ntile, EXPERTS], where=w)
        se = at("se", [P, ntile, EXPERTS], where=w)
        m8 = at("m8", [P, ntile, 8], where=w)
        gt = at("gt", [P, ntile, EXPERTS], where=w)
        eq = at("eq", [P, ntile, EXPERTS], where=w)
        cum = at("cum", [P, ntile, EXPERTS], where=w)
        cnt = at("cnt", [P, ntile], where=w)
        before = at("before", [P, ntile], where=w)
        assert w[0] <= end
        w = [work]
        qv = [at(f"qv{r}", [P, HEADS, SEQ], F32R, where=w) for r in range(3)]
        k4 = [at(f"k4{r}", [P, 4, SEQ], F32R, where=w) for r in range(3)]
        vx = [at(f"vx{r}", [P, 2, HEADS, 32], where=w) for r in range(3)]
        pt = at("pt", [P, 2, 4, 2, SEQ], where=w)
        oraw = at("oraw", [P, 4, SEQ], where=w)
        xs = at("xs", [P, SEQ], where=w)
        qks = at("qks", [P, 2, 3, SEQ], F32R, where=w)
        mh = at("mh", [8, 2, SEQ], F32R, where=w)
        ml = at("ml", [8, 2, SEQ], F32R, where=w)
        mxs = at("mxs", [P, 3, HEADS, 2], where=w)
        rec = at("rec", [P, HEADS], where=w)
        ontok = at("ontok", [P, 2, P], where=w)
        onT = at("onT", [P, SEQ], where=w)
        maskb = at("maskb", [P, SEQ], where=w)
        selo = at("selo", [P, SEQ], where=w)
        vmean = at("vmean", [P, 3], where=w)
        xsum = at("xsum", [P, 3], where=w)
        assert w[0] <= end, (w[0], end)
        w = [work + (3 * 16 + 3 * 4 + 3 * 4) * 1024]
        idx_i = at("idx_i", [P, SAMPLES], I32, where=w)
        idx_f = at("idx_f", [P, SAMPLES], where=w)
        idx_n = at("idx_n", [P, SAMPLES], where=w)
        idx_c = at("idx_c", [P, SAMPLES], I32, where=w)
        xg = at("xg", [P, BATCH, SC], where=w)
        ksg = at("ksg", [P, BATCH, SC], where=w)
        headmask = at("headmask", [P, HEADS], where=w)
        kbd = at("kbd", [P, 2, HEADS, SC], where=w)
        qf = at("qf", [P, 2, SEQ], where=w)
        mxq = at("mxq", [P, 2, 2, HEADS], where=w)
        mall = at("mall", [P, 2, BATCH, HEADS], where=w)
        mrow = at("mrow", [P, 2, SEQ], where=w)
        mwork = at("mwork", [P, 2, SEQ], where=w)
        mtop = at("mtop", [P, 2, 8], where=w)
        mgt = at("mgt", [P, 2, SEQ], where=w)
        meq = at("meq", [P, 2, SEQ], where=w)
        mcum = at("mcum", [P, 2, SEQ], where=w)
        mneed = at("mneed", [P, 2], where=w)

        ps = ctx.enter_context(nc.psum_tensor("ps", [P, 8, CH], F32))
        qk_d = nc.dram_tensor("qk_scratch", (2, P, 3, SEQ), F32, kind="Internal").ap()
        mask_d = nc.dram_tensor("mask_scratch", (BATCH * P, SEQ), F32, kind="Internal").ap()

        counted = {}

        def counter(name, n=1):
            s = sem(name)
            counted[s.name] = (s, n)
            return s

        phase_done = sem("phase_done")
        load_x = [sem(f"load_x{c}") for c in range(NC)]
        load_m = sem("load_m")
        load_f = sem("load_f")
        load_t = sem("load_t")
        load_g = sem("load_g")
        load_i = sem("load_i")
        stored = sem("stored")
        gates_ready = sem("gates_ready")
        idx_ready = sem("idx_ready")
        column_taken = sem("column_taken")
        taken = sem("taken")
        gathered = sem("gathered")
        sampled = sem("sampled")
        mask_ready = sem("mask_ready")
        mask_stored = sem("mask_stored")
        setup_done = sem("setup_done")
        waited = sem("waited")
        dve_step = sem("dve_step")
        act_step = sem("act_step")
        pool_step = sem("pool_step")
        pe_step = sem("pe_step")

        ln_cen = counter("ln_cen")
        ln_sq = counter("ln_sq")
        ln_var = counter("ln_var")
        ln_log = counter("ln_log")
        ln_rstd = counter("ln_rstd")
        ln_unit = counter("ln_unit")
        ln_aff = counter("ln_aff")
        acol_exp = counter("acol_exp")
        acol_neg = counter("acol_neg")
        acol_skip = counter("acol_skip")
        m1_psum = counter("m1_psum", 4)
        m1_evac = counter("m1_evac", 4)
        m1_gate = counter("m1_gate")
        m2_dt = counter("m2_dt")
        m2_u = counter("m2_u")
        m2_mean = counter("m2_mean")
        m2_abs = counter("m2_abs")
        m2_exp = counter("m2_exp")
        m2_log = counter("m2_log")
        m2_pos = counter("m2_pos")
        m2_delta = counter("m2_delta")
        m2_uin = counter("m2_uin")
        m2_adisc = counter("m2_adisc")
        m2_scan = counter("m2_scan")
        m3_sum = counter("m3_sum")
        m3_y = counter("m3_y")
        m3_out = counter("m3_out")
        m3_skip = counter("m3_skip")
        m3_res = counter("m3_res")
        f_h = counter("f_h", 4)
        f_g = counter("f_g", 4)
        f_acc = counter("f_acc", 2)
        f_out = counter("f_out")
        add_res = counter("add_res")
        e_h = counter("e_h", BLOCKS)
        e_s = counter("e_s", BLOCKS)
        e_t = counter("e_t", EXPERTS)
        e_m = counter("e_m", BLOCKS)
        e_w = counter("e_w", BLOCKS)
        e_xh = counter("e_xh")
        e_xl = counter("e_xl")
        e_out = counter("e_out")
        at_xs = counter("at_xs")
        at_proj = counter("at_proj", 2)
        at_hi = counter("at_hi", 2)
        at_lo = counter("at_lo", 3)
        at_spill = counter("at_spill", 16)
        at_scat = [sem(f"at_scat{r}") for r in range(3)]
        at_am = counter("at_am", 16)
        at_max = counter("at_max", 16)
        at_tp = counter("at_tp", 2)
        at_mh = counter("at_mh", 2)
        at_ml = counter("at_ml", 2)
        at_mx = [counter(f"at_mx{h}", 32) for h in range(2)]
        at_sc = counter("at_sc", 8)
        at_exp = counter("at_exp", 8)
        at_pv = counter("at_pv", 4)
        at_oev = counter("at_oev", 4)
        at_otp = counter("at_otp", 2)
        at_rec = counter("at_rec", 2)
        at_ot = counter("at_ot", 2)
        at_obp = counter("at_obp")
        at_ob = counter("at_ob")
        at_aop = counter("at_aop")
        at_ao = counter("at_ao")
        at_xm = counter("at_xm")
        at_vmp = counter("at_vmp")
        at_vm = counter("at_vm")
        at_sel = counter("at_sel")
        at_mask = counter("at_mask", 16)
        b_kbd = counter("b_kbd")
        b_q = counter("b_q")
        b_qf = counter("b_qf")
        b_s = counter("b_s", 2)
        b_mx = counter("b_mx", 2)
        b_m = counter("b_m", 2)

        def nth(s, c, k=0):
            n = counted[s.name][1]
            return n * c + (n * CREDIT + k + 1)

        def every(s, c):
            n = counted[s.name][1]
            return n * c + n * (CREDIT + 1)

        (SETUP, LN0, SPLIT, STAGE_A, LN_F1, GATE_F1, EXP_F1, LN_B, CHOOSE, ATT_B, LN_F2, GATE_F2, EXP_F2) = range(13)

        def passed(eng, n):
            eng.wait_ge(phase_done, 4 * n + 4)

        def gate(eng, n):
            eng.drain().then_inc(phase_done, 1)
            passed(eng, n)

        CLEARED = 5

        NR = [(BATCH + 2 - r) // 3 for r in range(3)]

        SPREAD = 16 * 5

        def scattered(e, third, r):
            return e * (NR[r] * SPREAD) + third * SPREAD + SPREAD

        def sequences(eng, step, last):
            step(0, 0, 0, first=True)
            with eng.Fori(0, 4) as i:
                for k in range(3):
                    step(i * 3 + (1 + k), i + (1 + k) // 3, (1 + k) % 3)
            step(13, 4, 1)
            step(14, 4, 2, proj=False)
            step(15, 5, 0, nxt=False, proj=False)
            last()

        pe_steps = {0: 1, 1: 5, "samples": 3, "rows": 4}
        act_steps = {0: 3, 1: 4}

        block = ctx.enter_context(nc.Block())

        @block.sync
        def _(sp):
            for s, n in counted.values():
                sp.sem_inc(s, CREDIT * n)
            for c in range(NC):
                sp.dma_start(res[:, c * CH:(c + 1) * CH], x_d[:, c * CH:(c + 1) * CH]).then_inc(load_x[c], 16)

            def load_layer(l):
                sp.dma_start(mw[:, 0:MSPLIT], mw_d[ds(l, 1), :, 0:MSPLIT].rearrange("o p n -> (o p) n"))\
                  .then_inc(load_m, 16)
                for hb in range(2):
                    sp.dma_start(wxp[:, hb, :, hb * STATES:(hb + 1) * STATES],
                                 xp_d[ds(l, 1)].rearrange("o p k n -> (o p) k n")).then_inc(load_m, 16)

            def load_network(l):
                sp.dma_start(mw[:, MSPLIT:MCOLS], mw_d[ds(l, 1), :, MSPLIT:MCOLS].rearrange("o p n -> (o p) n"))\
                  .then_inc(load_f, 16)

            def load_attention(l):
                sp.dma_start(tw[:], tw_d[ds(l, 1)].rearrange("o p n -> (o p) n")).then_inc(load_t, 16)

            sp.dma_start(w12raw[:], w12_d).then_inc(load_g, 16)
            sp.wait_ge(setup_done, 1)
            load_layer(0)
            load_attention(0)
            load_network(0)
            sp.dma_start(gw[:], gw_d).then_inc(load_g, 16)

            def attention(e, probsparse):
                def send_max(b, half, r):
                    B = e * BATCH + b
                    for row, part, ready in ((96, mh, at_mh), (97, ml, at_ml)):
                        sp.wait_ge(ready, nth(ready, B, half))
                        sp.dma_start(qv[r][row:row + 1, 8 * half:8 * half + 8, :].bitcast(F32),
                                     part[0:8, half, :].bitcast(F32)).then_inc(at_mx[half], 16)

                def spill_qk(b, third, r, first=False):
                    B = e * BATCH + b
                    if not first:
                        before, rb = third + (r + 2) // 3 - 1, (r + 2) % 3
                        sp.wait_ge(at_scat[rb], scattered(e, before, rb))
                    sp.wait_ge(at_lo, nth(at_lo, B, 1))
                    sp.dma_start(qk_d.rearrange("a p t n -> p a t n"), qks[:].bitcast(F32)).then_inc(at_spill, 16)

                def spread_qk(b, r):
                    B = e * BATCH + b
                    sp.wait_ge(at_spill, every(at_spill, B))
                    sp.wait_ge(at_sc, nth(at_sc, B - 3, 7))
                    rows = qk_d.rearrange("a (j x) t n -> a (x t) j n", j=4)
                    sp.dma_start(k4[r][0:96].bitcast(F32), rows[1])\
                      .then_inc(at_scat[r], 16)
                    for g in range(4):
                        sp.dma_start(qv[r][24 * g:24 * g + 24].bitcast(F32)
                                     .rearrange("p (j g) n -> p j g n", g=4)[:, :, g, :],
                                     rows[0, 24 * g:24 * g + 24])\
                          .then_inc(at_scat[r], 16)

                def send_mask(b):
                    sp.wait_ge(at_sel, nth(at_sel, b - 1))
                    sp.dma_start(maskb[:], mask_d[ds(b * P, P), :]).then_inc(at_mask, 16)

                def step(b, third, r, nxt=True, proj=True, first=False):
                    r2 = (r + 2) % 3
                    if proj:
                        spill_qk(b + 2, third + (r + 2) // 3, r2)
                    send_max(b, 1, r)
                    if probsparse and not first:
                        send_mask(b - 1)
                    if proj:
                        spread_qk(b + 2, r2)
                    if nxt:
                        send_max(b + 1, 0, (r + 1) % 3)

                for b in (0, 1):
                    spill_qk(b, 0, b, first=b == 0)
                    spread_qk(b, b)
                send_max(0, 0, 0)
                sequences(sp, step, (lambda: send_mask(15)) if probsparse else (lambda: None))

            with sp.Fori(0, LAYERS) as l:
                sp.wait_ge(m3_res, every(m3_res, l * NC + (NC - 1)))
                sp.sem_inc(waited, 1)
                load_layer(l + 1)
                sp.wait_ge(pool_step, l * 3 + CLEARED)
                sp.sem_inc(waited, 1)
                attention(l, False)
                sp.wait_ge(at_ao, every(at_ao, l * BATCH + (BATCH - 1)))
                sp.sem_inc(waited, 1)
                load_attention(l + 1)
                sp.wait_ge(f_out, every(f_out, l * NC + (NC - 1)))
                sp.sem_inc(waited, 1)
                load_network(l + 1)
            passed(sp, LN_B)
            sp.dma_start(idx_i[:], idx_d).then_inc(load_i, 16)
            sp.wait_ge(mask_ready, 1)
            for h in range(2):
                for d in range(DH):
                    sp.dma_start(mask_d.rearrange("(g r d) n -> g r d n", g=2, d=DH)[h, :, d, :],
                                 mwork[:, h, :]).then_inc(mask_stored, 16)
            sp.wait_ge(mask_stored, 16 * 2 * DH)
            passed(sp, CHOOSE)
            attention(LAYERS, True)
            for c in range(NC):
                sp.wait_ge(e_out, nth(e_out, NC + c))
                sp.dma_start(out_d[:, c * CH:(c + 1) * CH], res[:, c * CH:(c + 1) * CH]).then_inc(stored, 16)
            sp.wait_ge(load_m, 48 * (LAYERS + 1))
            sp.wait_ge(load_f, 16 * (LAYERS + 1))
            sp.wait_ge(stored, 16 * NC)

        @block.tensor
        def _(pe):
            mm = nc.tensor.matmul

            def norm(n, src, ready=None, hooks=None):
                def quad(q):
                    def centered(k):
                        c = q * 4 + k
                        if ready:
                            ready(c)
                        pe.wait_ge(ln_unit, nth(ln_unit, n * NC + c - 4))
                        mm(ps[:, k, :], center[:], src[:, ds(c * CH, CH)], start=True, stop=True).then_inc(ln_cen, 1)

                    def variance(k):
                        C = n * NC + q * 4 + k
                        pe.wait_ge(ln_sq, nth(ln_sq, C))
                        pe.wait_ge(ln_log, nth(ln_log, C - 2))
                        mm(ps[:, 4 + k % 2, :], average[:], sq[:, k % 2, :], start=True, stop=True).then_inc(ln_var, 1)
                        if hooks and (q, k) in hooks:
                            hooks[q, k]()

                    centered(0)
                    centered(1)
                    centered(2)
                    variance(0)
                    centered(3)
                    for k in range(1, 4):
                        variance(k)

                if hooks:
                    quad(0)
                    quad(1)
                else:
                    with pe.Fori(0, 2) as q:
                        quad(q)

            def m1(l):
                with pe.Fori(0, NC // 2) as i:
                    for u in range(2):
                        C = l * NC + i * 2 + u
                        if u == 0:
                            pe.wait_ge(f_out, every(f_out, l * NC - 1))
                        for o in range(4):
                            pe.wait_ge(m1_evac, nth(m1_evac, C - 2, o))
                            mm(ps[:, 4 * u + o, :], M("win", o * P, P), xa[:, ds((i * 2 + u) * CH, CH)],
                               start=True, stop=True).then_inc(m1_psum, 1)

            def m2(l):
                with pe.Fori(0, NC // 2) as i:
                    for u in range(2):
                        C = l * NC + i * 2 + u
                        if u == 0:
                            pe.wait_ge(m1_evac, every(m1_evac, l * NC + (NC - 1)))
                        pe.wait_ge(m2_abs, nth(m2_abs, C - 2))
                        pe.wait_ge(m2_pos, nth(m2_pos, C - 2))
                        for kb in range(2):
                            last = mm(ps[:, u, :], M("wdt", kb * P, P), xi[:, kb, ds((i * 2 + u) * CH, CH)],
                                      start=kb == 0, stop=kb == 1)
                        last.then_inc(m2_dt, 1)
                        pe.wait_ge(m2_uin, nth(m2_uin, C - 2))
                        for hb in range(2):
                            for kb in range(2):
                                last = mm(ps[:, 4 + u, 0:SEQ], wxp[:, hb, kb, :],
                                          xi[:, kb, ds((i * 2 + u) * CH + hb * SEQ, SEQ)],
                                          start=hb + kb == 0, stop=hb + kb == 2)
                        last.then_inc(m2_u, 1)
                    for u in range(2):
                        C = l * NC + i * 2 + u
                        pe.wait_ge(m2_delta, nth(m2_delta, C))
                        pe.wait_ge(m2_adisc, nth(m2_adisc, C - 2))
                        for hb in range(2):
                            last = mm(ps[:, 2 + u, 0:SEQ], halfavg[:, hb, :], delta[:, u, hb * SEQ:(hb + 1) * SEQ],
                                      start=hb == 0, stop=hb == 1)
                        last.then_inc(m2_mean, 1)

            def m3(l):
                with pe.Fori(0, NC // 2) as i:
                    for u in range(2):
                        C = l * NC + i * 2 + u
                        if u == 0:
                            pe.wait_ge(m2_uin, every(m2_uin, l * NC + (NC - 1)))
                        pe.wait_ge(m2_scan, nth(m2_scan, C))
                        pe.wait_ge(m3_y, nth(m3_y, C - 2))
                        for hb in range(2):
                            last = mm(ps[:, 4 + u, hb * SEQ:(hb + 1) * SEQ], halfsum[:, hb, :],
                                      st[:, ds((i * 2 + u) * SEQ, SEQ)], start=True, stop=True)
                        last.then_inc(m3_sum, 1)
                    for u in range(2):
                        C = l * NC + i * 2 + u
                        pe.wait_ge(m3_y, nth(m3_y, C))
                        pe.wait_ge(m3_res, nth(m3_res, C - 2))
                        for kb in range(2):
                            last = mm(ps[:, 6 + u, :], M("wout", kb * P, P), y[:, u, kb, :], start=kb == 0, stop=kb == 1)
                        last.then_inc(m3_out, 1)

            def f(l):
                with pe.Fori(0, NC // 2) as i:
                    def up(u, half):
                        C = l * NC + i * 2 + u
                        if u == 0 and half == 0:
                            pe.wait_ge(ln_unit, every(ln_unit, l * (2 * NC) + (3 * NC - 1)))
                            pe.wait_ge(ln_aff, nth(ln_aff, l * (2 * NC) + NC + i * 2 + 1))
                        pe.wait_ge(f_g, nth(f_g, C - 1, 2 * half + 1))
                        for q in range(2):
                            mm(ps[:, 2 * half + q, :], M("wf1", (2 * half + q) * P, P),
                               xa[:, ds((i * 2 + u) * CH, CH)], start=True, stop=True).then_inc(f_h, 1)

                    def down(u, half):
                        C = l * NC + i * 2 + u
                        pe.wait_ge(f_g, nth(f_g, C, 2 * half + 1))
                        if half == 0:
                            pe.wait_ge(f_out, nth(f_out, C - 2))
                        for q in range(2):
                            last = mm(ps[:, 4 + u, :], M("wf2", (2 * half + q) * P, P), hid[:, half, q, :],
                                      start=half + q == 0, stop=half + q == 2)
                        last.then_inc(f_acc, 1)

                    up(0, 0)
                    up(0, 1)
                    down(0, 0)
                    up(1, 0)
                    down(0, 1)
                    up(1, 1)
                    down(1, 0)
                    down(1, 1)

            def attention(e, probsparse, part="middle"):
                def project_qk(b):
                    B = e * BATCH + b
                    pe.wait_ge(at_xs, nth(at_xs, B))
                    pe.wait_ge(at_lo, nth(at_lo, B - 1, 2))
                    pe.wait_ge(at_ml, nth(at_ml, B - 2, 0))
                    mm(ps[:, 7, 0:SEQ], T("wq"), xs[:], start=True, stop=True)
                    mm(ps[:, 7, SEQ:CH], T("wk"), xs[:], start=True, stop=True).then_inc(at_proj, 1)

                def project_v(b):
                    B = e * BATCH + b
                    pe.wait_ge(at_lo, nth(at_lo, B, 1))
                    pe.wait_ge(at_ot, nth(at_ot, B - 3, 1))
                    if probsparse:
                        pe.wait_ge(at_xm, nth(at_xm, b))
                    for t in range(2):
                        last = mm(ps[:, 7, t * P:(t + 1) * P], xs[:, t * P:(t + 1) * P], T("wv"),
                                  start=True, stop=True)
                    last.then_inc(at_proj, 1)

                def rows(b, h, r):
                    B = e * BATCH + b
                    pe.wait_ge(at_max, nth(at_max, B, h - 2))
                    for qt in range(2):
                        last = mm(ps[:, h % 2, qt * SEQ:(qt + 1) * SEQ], qv[r][0:96, h, qt * P:(qt + 1) * P],
                                  k4[r][0:96, h // 4, :], start=True, stop=True)
                    last.then_inc(at_am, 1)

                def maxima(b, half, r):
                    B = e * BATCH + b
                    pe.wait_ge(at_max, nth(at_max, B, 8 * half + 7))
                    for qt in range(2):
                        last = nc.tensor.transpose(ps[0:8, 7, qt * P:(qt + 1) * P],
                                                   mxs[:, r, 8 * half:8 * half + 8, qt], ident[:])
                    last.then_inc(at_tp, 1)

                def scores(b, p, r):
                    B = e * BATCH + b
                    if p % 4 == 0:
                        pe.wait_ge(at_mx[p // 4], every(at_mx[p // 4], B))
                    pe.wait_ge(at_exp, nth(at_exp, B, p - 2))
                    for hh_ in range(2):
                        h = 2 * p + hh_
                        for kt in range(2):
                            last = mm(ps[:, 2 + 2 * (p % 2) + hh_, kt * SEQ:(kt + 1) * SEQ],
                                      k4[r][0:98, h // 4, kt * P:(kt + 1) * P], qv[r][0:98, h, :],
                                      start=True, stop=True)
                    last.then_inc(at_sc, 1)

                def values(b, j, r):
                    B = e * BATCH + b
                    pe.wait_ge(at_exp, nth(at_exp, B, 2 * j + 1))
                    pe.wait_ge(at_oev, nth(at_oev, B, j - 1))
                    if j == 0:
                        pe.wait_ge(at_lo, nth(at_lo, B, 2))
                    for kt in range(2):
                        for g in range(4):
                            last = mm(ps[32 * g:32 * g + 32, 6, (j % 2) * SEQ:(j % 2 + 1) * SEQ],
                                      vx[r][:, kt, 4 * j + g, :], pt[:, j % 2, g, kt, :], start=kt == 0, stop=kt == 1)
                    last.then_inc(at_pv, 1)

                def to_rows(b, qt):
                    B = e * BATCH + b
                    if qt == 0:
                        pe.wait_ge(at_oev, nth(at_oev, B, 3))
                    else:
                        pe.wait_ge(at_ot, nth(at_ot, B, 0))
                    for j in range(4):
                        last = nc.tensor.transpose(ps[:, 7, j * P:(j + 1) * P], oraw[:, j, qt * P:(qt + 1) * P],
                                                   ident[:])
                    last.then_inc(at_otp, 1)

                def to_columns(b):
                    pe.wait_ge(at_ot, nth(at_ot, e * BATCH + b, 1))
                    for qt in range(2):
                        last = nc.tensor.transpose(ps[:, 7, qt * P:(qt + 1) * P], ontok[:, qt, :], ident[:])
                    last.then_inc(at_obp, 1)

                def out(b):
                    pe.wait_ge(at_ob, nth(at_ob, e * BATCH + b))
                    mm(ps[:, 7, 0:SEQ], T("wo"), onT[:], start=True, stop=True).then_inc(at_aop, 1)

                def mean_v(b, r):
                    mm(ps[:, 7, SEQ:SEQ + 1], T("wv"), xsum[:, r:r + 1], start=True, stop=True).then_inc(at_vmp, 1)

                def step(b, third, r, nxt=True, proj=True, first=False):
                    B = e * BATCH + b
                    t, rn = third + (r + 1) // 3, (r + 1) % 3
                    for p in range(8):
                        scores(b, p, r)
                        if nxt:
                            if p == 0:
                                pe.wait_ge(at_scat[rn], scattered(e, t, rn))
                            rows(b + 1, 2 * p, rn)
                            rows(b + 1, 2 * p + 1, rn)
                        if p == 0:
                            pe.wait_ge(at_ao, nth(at_ao, B - 2))
                            if proj:
                                project_qk(b + 2)
                        if p == 1:
                            if not first:
                                values(b - 1, 3, (r + 2) % 3)
                            if proj:
                                pe.wait_ge(at_lo, nth(at_lo, B + 2, 1))
                            maxima(b, 1, r)
                        if p == 2:
                            values(b, 0, r)
                            if not first:
                                pe.wait_ge(at_ml, nth(at_ml, B, 1))
                                to_rows(b - 1, 0)
                        if p == 3 and not first:
                            to_rows(b - 1, 1)
                        if p == 4:
                            values(b, 1, r)
                            if proj:
                                if first:
                                    pe.wait_ge(at_ml, nth(at_ml, B, 1))
                                project_v(b + 2)
                        if p == 5:
                            if proj:
                                pe.wait_ge(at_lo, nth(at_lo, B + 2, 2))
                            else:
                                pe.wait_ge(at_ot, nth(at_ot, B - 1, 1))
                            if probsparse:
                                mean_v(b, r)
                            if nxt:
                                maxima(b + 1, 0, rn)
                        if p == 6:
                            values(b, 2, r)
                            if not first:
                                if nxt:
                                    pe.wait_ge(at_ml, nth(at_ml, B + 1, 0))
                                if probsparse:
                                    pe.wait_ge(at_vm, nth(at_vm, b))
                                to_columns(b - 1)
                        if p == 7 and not first:
                            out(b - 1)

                def last_rows():
                    pe.wait_ge(at_ao, nth(at_ao, e * BATCH + 14))
                    to_rows(15, 0)

                if part == "begin":
                    return [lambda: project_qk(0), lambda: project_v(0), lambda: project_qk(1), lambda: project_v(1)]
                if part == "end":
                    return [last_rows, lambda: to_rows(15, 1), lambda: to_columns(15), lambda: out(15)]

                def last():
                    values(15, 3, 0)

                pe.wait_ge(at_scat[0], scattered(e, 0, 0))
                for h in range(HEADS):
                    rows(0, h, 0)
                pe.wait_ge(at_lo, nth(at_lo, e * BATCH + 1, 2))
                maxima(0, 0, 0)
                sequences(pe, step, last)

            def all_of(steps):
                for step in steps:
                    step()

            def gates(n):
                for t in range(ntile):
                    last = mm(ps[:, 0, t * EXPERTS:(t + 1) * EXPERTS], xa[:, t * P:(t + 1) * P], G("router"),
                              start=True, stop=True)
                last.then_inc(pe_step, 1)
                pe.wait_ge(gates_ready, n + 1)
                for t in range(ntile):
                    last = nc.tensor.transpose(ps[0:EXPERTS, t // 4, (t % 4) * P:(t % 4 + 1) * P], sg[:, t, :],
                                               ident[:])
                last.then_inc(pe_step, 1)

            def experts(n):
                with pe.Fori(0, NC // 2) as i:
                    def up(u, k):
                        C = n * NC + i * 2 + u
                        if k == 0:
                            pe.wait_ge(e_xh, nth(e_xh, C))
                            pe.wait_ge(e_xl, nth(e_xl, C))
                        s = k % 2
                        if k == 0:
                            pe.wait_ge(e_m, nth(e_m, C - 1, BLOCKS - 2))
                        elif k == 1:
                            pe.wait_ge(e_m, nth(e_m, C - 1, BLOCKS - 1))
                        if k >= SHARED:
                            mm(ps[:, 4 + s, :], esel[:, k - SHARED, :], gateT[:, ds((i * 2 + u) * CH, CH)],
                               start=True, stop=True)
                        for bank, wh, wl in ((0, w1h, w1l), (2, w2h, w2l)):
                            o = ps[:, bank + s, :]
                            mm(o, wh[:, k, :], xh[:, u, :], start=True, stop=False)
                            mm(o, wh[:, k, :], xl[:, u, :], start=False, stop=False)
                            last = mm(o, wl[:, k, :], xh[:, u, :], start=False, stop=True)
                        last.then_inc(e_h, 1)

                    def down(u, k):
                        C = n * NC + i * 2 + u
                        pe.wait_ge(e_m, nth(e_m, C, k))
                        if k == 0:
                            pe.wait_ge(e_out, nth(e_out, C - 2))
                        mm(ps[:, 6 + u, :], G("w3", k * P, P), hh[:, k % 2, :], start=k == 0, stop=k == BLOCKS - 1)\
                            .then_inc(e_w, 1)

                    todo = [(u, k) for u in range(2) for k in range(BLOCKS)]
                    up(*todo[0])
                    for before_, now in zip(todo, todo[1:]):
                        up(*now)
                        down(*before_)
                    down(*todo[-1])

            def choose():
                pe.wait_ge(gathered, 1)
                for g in range(2):
                    last = mm(ps[:, g, 0:8 * SC], T("wk"), xg[:, 8 * g:8 * g + 8, :], start=True, stop=True)
                last.then_inc(pe_step, 1)
                pe.wait_ge(sampled, 2)
                with pe.Fori(0, BATCH // 2) as i:
                    for u in range(2):
                        b = i * 2 + u
                        pe.wait_ge(b_qf, nth(b_qf, b - 2))
                        mm(ps[:, u, 0:SEQ], T("wq"), xa[:, ds(b * SEQ, SEQ)], start=True, stop=True).then_inc(b_q, 1)
                    for u in range(2):
                        b = i * 2 + u
                        pe.wait_ge(b_qf, nth(b_qf, b))
                        pe.wait_ge(b_kbd, nth(b_kbd, b))
                        for qt in range(2):
                            pe.wait_ge(b_m, nth(b_m, b - 1, qt))
                            for g in range(2):
                                last = mm(ps[:, 2 + 2 * qt + g, 0:8 * SC], qf[:, u, qt * P:(qt + 1) * P],
                                          kbd[:, u, 8 * g:8 * g + 8, :], start=True, stop=True)
                            last.then_inc(b_s, 1)
                pe.wait_ge(b_m, every(b_m, BATCH - 1))
                for g in range(2):
                    for qt in range(2):
                        last = nc.tensor.transpose(ps[:, 6, (2 * g + qt) * P:(2 * g + qt + 1) * P],
                                                   mall[:, qt, 8 * g:8 * g + 8, :], ident[:])
                last.then_inc(pe_step, 1)

            gate(pe, SETUP)
            for c in range(NC):
                pe.wait_ge(load_x[c], 16)
            norm(0, res)
            gate(pe, LN0)
            gate(pe, SPLIT)
            with pe.Fori(0, LAYERS) as l:
                pe.wait_ge(load_m, l * 48 + 48)
                pe.sem_inc(waited, 1)
                m1(l)
                m2(l)
                m3(l)
                pe.wait_ge(load_t, l * 16 + 16)
                project = attention(l, False, "begin")

                def first_project():
                    pe.wait_ge(m3_res, every(m3_res, l * NC + (NC - 1)))
                    project[0]()

                norm(l * 2 + 1, xa, ready=lambda c: pe.wait_ge(m3_res, nth(m3_res, l * NC + c)),
                     hooks={(0, 3): first_project, (1, 0): project[1], (1, 1): project[2], (1, 3): project[3]})
                pe.wait_ge(ln_unit, every(ln_unit, l * (2 * NC) + (2 * NC - 1)))
                attention(l, False)
                norm(l * 2 + 2, xa, ready=lambda c: pe.wait_ge(at_ao, nth(at_ao, l * BATCH + c * 2 + 1)),
                     hooks={(0, k): step for k, step in enumerate(attention(l, False, "end"))})
                pe.wait_ge(load_f, l * 16 + 16)
                pe.sem_inc(waited, 1)
                f(l)
            gate(pe, STAGE_A)
            norm(9, res, ready=lambda c: pe.wait_ge(add_res, nth(add_res, c)))
            gate(pe, LN_F1)
            pe.wait_ge(load_g, 32)
            gates(0)
            gate(pe, GATE_F1)
            experts(0)
            gate(pe, EXP_F1)
            norm(10, res)
            gate(pe, LN_B)
            pe.wait_ge(load_t, (LAYERS + 1) * 16)
            choose()
            gate(pe, CHOOSE)
            all_of(attention(LAYERS, True, "begin"))
            attention(LAYERS, True)
            all_of(attention(LAYERS, True, "end"))
            gate(pe, ATT_B)
            norm(11, res)
            gate(pe, LN_F2)
            gates(1)
            gate(pe, GATE_F2)
            experts(1)
            gate(pe, EXP_F2)

        @block.scalar
        def _(act):
            A = nc.scalar.activation

            def norm(n, hooks=None):
                def quad(q):
                    def square(k):
                        C = n * NC + q * 4 + k
                        act.wait_ge(ln_cen, nth(ln_cen, C))
                        act.wait_ge(ln_var, nth(ln_var, C - 2))
                        A(sq[:, k % 2, :], ps[:, k, :], ACT.Square).then_inc(ln_sq, 1)

                    square(0)
                    square(1)
                    for k in range(4):
                        C = n * NC + q * 4 + k
                        act.wait_ge(ln_var, nth(ln_var, C))
                        act.wait_ge(ln_rstd, nth(ln_rstd, C - 2))
                        A(logv[:, k % 2, :], ps[:, 4 + k % 2, :], ACT.Ln, bias=acol[:, 3:4]).then_inc(ln_log, 1)
                        if k < 2:
                            square(k + 2)
                        act.wait_ge(ln_log, nth(ln_log, C))
                        act.wait_ge(ln_unit, nth(ln_unit, C - 2))
                        A(rstd[:, k % 2, :], logv[:, k % 2, :], ACT.Exp, scale=-0.5).then_inc(ln_rstd, 1)
                        if hooks and (q, k) in hooks:
                            hooks[q, k]()

                if hooks:
                    quad(0)
                    quad(1)
                else:
                    with act.Fori(0, 2) as q:
                        quad(q)

            def m1(l):
                act.preload_act_table(ACT.Silu)
                with act.Fori(0, NC // 2) as i:
                    for u in range(2):
                        C = l * NC + i * 2 + u
                        for o in range(4):
                            act.wait_ge(m1_psum, nth(m1_psum, C, o))
                            if o == 2:
                                act.wait_ge(m1_gate, nth(m1_gate, C - 2))
                            dst = xi[:, o, ds((i * 2 + u) * CH, CH)] if o < 2 else sres[:, u, o - 2, :]
                            A(dst, ps[:, 4 * u + o, :], ACT.Silu, bias=M("b_in", o, 1)).then_inc(m1_evac, 1)

            def m2(l):
                A(acol[:, 0:1], M("A_log"), ACT.Exp).then_inc(acol_exp, 1)
                act.wait_ge(acol_neg, l + CREDIT + 1)
                act.sem_inc(waited, 1)
                with act.Fori(0, NC // 2) as i:
                    for u in range(2):
                        C = l * NC + i * 2 + u
                        act.wait_ge(m2_dt, nth(m2_dt, C))
                        act.wait_ge(m2_log, nth(m2_log, C - 2))
                        A(absd[:, u, :], ps[:, u, :], ACT.Abs, bias=M("b_dt")).then_inc(m2_abs, 1)
                        act.wait_ge(m2_abs, nth(m2_abs, C))
                        A(absd[:, u, :], absd[:, u, :], ACT.Exp, scale=-1.0).then_inc(m2_exp, 1)
                        act.wait_ge(m2_exp, nth(m2_exp, C))
                        act.wait_ge(m2_delta, nth(m2_delta, C - 2))
                        A(logd[:, u, :], absd[:, u, :], ACT.Ln, bias=1.0).then_inc(m2_log, 1)
                    for u in range(2):
                        C = l * NC + i * 2 + u
                        act.wait_ge(m2_mean, nth(m2_mean, C))
                        act.wait_ge(m2_scan, nth(m2_scan, C - 2))
                        A(adisc[:, u, :], ps[:, 2 + u, 0:SEQ], ACT.Exp, scale=acol[:, 1:2]).then_inc(m2_adisc, 1)

            def m3(l):
                A(acol[:, 2:3], M("Dp"), ACT.Identity, bias=1.0).then_inc(acol_skip, 1)
                act.wait_ge(acol_skip, l + CREDIT + 1)
                act.sem_inc(waited, 1)
                with act.Fori(0, NC // 2) as i:
                    for u in range(2):
                        act.wait_ge(m3_res, nth(m3_res, l * NC + i * 2 + u - 2))
                        A(xd[:, u, :], xa[:, ds((i * 2 + u) * CH, CH)], ACT.Identity, scale=acol[:, 2:3],
                          bias=M("b_out")).then_inc(m3_skip, 1)

            def f(l):
                act.preload_act_table(ACT.Gelu)
                with act.Fori(0, NC // 2) as i:
                    for u in range(2):
                        C = l * NC + i * 2 + u
                        for o in range(4):
                            act.wait_ge(f_h, nth(f_h, C, o))
                            if o % 2 == 0:
                                act.wait_ge(f_acc, nth(f_acc, C - 1, o // 2))
                            A(hid[:, o // 2, o % 2, :], ps[:, o, :], ACT.Gelu, bias=M("b_f1", o, 1)).then_inc(f_g, 1)

            def attention(e, probsparse, part="middle"):
                def high(b):
                    B = e * BATCH + b
                    act.wait_ge(at_proj, nth(at_proj, B, 0))
                    act.wait_ge(at_spill, every(at_spill, B - 1))
                    for dst, bias, at_ in ((qks[:, 0, 0:2, :], "bq", 0), (qks[:, 1, 0:3:2, :], "bk", SEQ)):
                        A(dst, ps[:, 7, at_:at_ + SEQ].unsqueeze(1).broadcast_to([P, 2, SEQ]), ACT.Identity,
                          bias=T(bias)).then_inc(at_hi, 1)

                def minus_max(b, half):
                    B = e * BATCH + b
                    act.wait_ge(at_tp, nth(at_tp, B, half))
                    act.wait_ge(at_mx[half], every(at_mx[half], B - 1))
                    A(mh[:, half, :], ps[0:8, 7, 0:SEQ], ACT.Identity, scale=-1.0).then_inc(at_mh, 1)

                def exps(b, p):
                    B = e * BATCH + b
                    j = p // 2
                    act.wait_ge(at_sc, nth(at_sc, B, p))
                    act.wait_ge(at_pv, nth(at_pv, B, j - 2))
                    A(pt[:, j % 2, 2 * (p % 2):2 * (p % 2) + 2, :, :],
                      ps[:, 2 + 2 * (p % 2):4 + 2 * (p % 2), :], ACT.Exp, scale=QSCALE).then_inc(at_exp, 1)

                def evac(b, j):
                    B = e * BATCH + b
                    act.wait_ge(at_pv, nth(at_pv, B, j))
                    act.wait_ge(at_otp, nth(at_otp, B - 1, 1))
                    A(oraw[:, j, :], ps[:, 6, (j % 2) * SEQ:(j % 2 + 1) * SEQ], ACT.Copy).then_inc(at_oev, 1)

                def columns(b, r):
                    B = e * BATCH + b
                    act.wait_ge(at_aop, nth(at_aop, B - 1))
                    if probsparse:
                        act.wait_ge(at_sel, nth(at_sel, b))
                        A(onT[:], selo[:], ACT.Identity, bias=vmean[:, r:r + 1]).then_inc(at_ob, 1)
                    else:
                        act.wait_ge(at_obp, nth(at_obp, B))
                        A(onT[:], ps[:, 7, 0:SEQ], ACT.Copy).then_inc(at_ob, 1)

                def step(b, third, r, nxt=True, proj=True, first=False):
                    for p in range(8):
                        if p == 7 and not first:
                            columns(b - 1, (r + 2) % 3)
                        exps(b, p)
                        if p == 0 and proj:
                            high(b + 2)
                        if p == 1:
                            if not first:
                                evac(b - 1, 3)
                            minus_max(b, 1)
                        if p in (3, 5, 7):
                            evac(b, p // 2 - 1)
                        if p == 5 and nxt:
                            minus_max(b + 1, 0)

                if part == "begin":
                    return [lambda: high(0), lambda: high(1)]
                if part == "end":
                    return [lambda: columns(15, 0)]

                def last():
                    evac(15, 3)

                minus_max(0, 0)
                sequences(act, step, last)

            def gates(n):
                act.wait_ge(pe_step, pe_steps[n])
                A(sg[:].rearrange("p t e -> p (t e)"), ps[:, 0, :], ACT.Sigmoid).then_inc(act_step, 1)

            def experts(n):
                act.preload_act_table(ACT.Silu)
                with act.Fori(0, NC // 2) as i:
                    def split(u):
                        C = n * NC + i * 2 + u
                        act.wait_ge(e_w, nth(e_w, C - 2, BLOCKS - 1))
                        A(xh[:, u, :], xa[:, ds((i * 2 + u) * CH, CH)], ACT.Copy).then_inc(e_xh, 1)
                    split(0)
                    for u in range(2):
                        C = n * NC + i * 2 + u
                        for k in range(BLOCKS):
                            if u == 0 and k == BLOCKS // 2:
                                split(1)
                            act.wait_ge(e_h, nth(e_h, C, k))
                            act.wait_ge(e_m, nth(e_m, C, k - 2))
                            A(sil[:, k % 2, :], ps[:, k % 2, :], ACT.Silu).then_inc(e_s, 1)

            gate(act, SETUP)
            act.preload_act_table_set("natural_log_exp_and_others")
            norm(0)
            gate(act, LN0)
            act.wait_ge(load_g, 32)
            for n, (h_, l_) in enumerate(((w1h, w1l), (w2h, w2l))):
                A(h_[:].rearrange("p k n -> p (k n)"), w12raw[:, n, :], ACT.Copy).then_inc(act_step, 1)
            gate(act, SPLIT)
            with act.Fori(0, LAYERS) as l:
                act.wait_ge(load_m, l * 48 + 48)
                act.sem_inc(waited, 1)
                m1(l)
                act.preload_act_table_set("natural_log_exp_and_others")
                m2(l)
                m3(l)
                act.wait_ge(load_t, l * 16 + 16)
                high = attention(l, False, "begin")
                norm(l * 2 + 1, hooks={(0, 3): high[0], (1, 2): high[1]})
                attention(l, False)
                norm(l * 2 + 2, hooks={(0, 2): attention(l, False, "end")[0]})
                act.wait_ge(load_f, l * 16 + 16)
                act.sem_inc(waited, 1)
                f(l)
            gate(act, STAGE_A)
            act.preload_act_table_set("natural_log_exp_and_others")
            norm(9)
            gate(act, LN_F1)
            gates(0)
            gate(act, GATE_F1)
            experts(0)
            gate(act, EXP_F1)
            act.preload_act_table_set("natural_log_exp_and_others")
            norm(10)
            gate(act, LN_B)
            act.wait_ge(load_t, (LAYERS + 1) * 16)
            act.wait_ge(pe_step, pe_steps["samples"])
            for g in range(2):
                A(ksg[:, 8 * g:8 * g + 8, :], ps[:, g, 0:8 * SC].rearrange("p (b s) -> p b s", s=SC), ACT.Identity,
                  bias=T("bk")).then_inc(sampled, 1)
            with act.Fori(0, BATCH // 2) as i:
                for u in range(2):
                    b = i * 2 + u
                    act.wait_ge(b_q, nth(b_q, b))
                    act.wait_ge(b_s, nth(b_s, b - 2, 1))
                    A(qf[:, u, :], ps[:, u, 0:SEQ], ACT.Identity, bias=T("bq")).then_inc(b_qf, 1)
            gate(act, CHOOSE)
            for step in attention(LAYERS, True, "begin"):
                step()
            attention(LAYERS, True)
            for step in attention(LAYERS, True, "end"):
                step()
            gate(act, ATT_B)
            norm(11)
            gate(act, LN_F2)
            gates(1)
            gate(act, GATE_F2)
            experts(1)
            gate(act, EXP_F2)

        @block.vector
        def _(dve):
            V = nc.vector
            chain = [0]

            def link(ins):
                chain[0] += 1
                ins.then_inc(dve_step, 1)
                dve.wait_ge(dve_step, chain[0])

            def norm(n, dst=None, added=False, gain=None, hooks=None):
                if added:
                    with dve.Fori(0, NC) as c:
                        V.tensor_tensor(res[:, ds(c * CH, CH)], res[:, ds(c * CH, CH)], xa[:, ds(c * CH, CH)],
                                        ALU.add).then_inc(add_res, 1)
                def quad(q):
                    def multiply(k):
                        C = n * NC + q * 4 + k
                        dve.wait_ge(ln_rstd, nth(ln_rstd, C))
                        if dst is None:
                            dve.wait_ge(ln_aff, nth(ln_aff, C - NC - 2))
                            o = unit[:, k % 2, :]
                        else:
                            o = dst[:, ds((q * 4 + k) * CH, CH)]
                        V.tensor_tensor(o, ps[:, k, :], rstd[:, k % 2, :], ALU.mult).then_inc(ln_unit, 1)

                    def affine(k):
                        if dst is None:
                            dve.wait_ge(ln_unit, nth(ln_unit, n * NC + q * 4 + k))
                            V.tensor_scalar(xa[:, ds((q * 4 + k) * CH, CH)], unit[:, k % 2, :], M(gain[0]), M(gain[1]),
                                            ALU.mult, ALU.add).then_inc(ln_aff, 1)
                        if hooks and (q, k) in hooks:
                            hooks[q, k]()

                    multiply(0)
                    for k in range(4):
                        if k < 3:
                            multiply(k + 1)
                        affine(k)

                if hooks:
                    quad(0)
                    quad(1)
                else:
                    with dve.Fori(0, 2) as q:
                        quad(q)

            def m1(l):
                with dve.Fori(0, NC // 2) as i:
                    for u in range(2):
                        C = l * NC + i * 2 + u
                        dve.wait_ge(m1_evac, nth(m1_evac, C, 3))
                        c = i * 2 + u
                        V.tensor_tensor(zz[:, :, ds(c * CH, CH)], xi[:, :, ds(c * CH, CH)], sres[:, u, :, :],
                                        ALU.mult).then_inc(m1_gate, 1)

            def m2(l):
                dve.wait_ge(acol_exp, nth(acol_exp, l))
                V.tensor_scalar(acol[:, 1:2], acol[:, 0:1], -1.0, None, ALU.mult).then_inc(acol_neg, 1)
                with dve.Fori(0, NC // 2) as i:
                    for u in range(2):
                        C = l * NC + i * 2 + u
                        dve.wait_ge(m2_abs, nth(m2_abs, C))
                        dve.wait_ge(m2_delta, nth(m2_delta, C - 2))
                        V.tensor_scalar(posd[:, u, :], ps[:, u, :], M("b_dt"), 0.0, ALU.add, ALU.max)\
                            .then_inc(m2_pos, 1)
                        dve.wait_ge(m2_u, nth(m2_u, C))
                        dve.wait_ge(m2_scan, nth(m2_scan, C - 2))
                        V.tensor_scalar(uin[:, u, :], ps[:, 4 + u, 0:SEQ], M("b_xp"), None, ALU.add)\
                            .then_inc(m2_uin, 1)
                        dve.wait_ge(m2_pos, nth(m2_pos, C))
                        dve.wait_ge(m2_log, nth(m2_log, C))
                        dve.wait_ge(m2_mean, nth(m2_mean, C - 2))
                        V.tensor_tensor(delta[:, u, :], posd[:, u, :], logd[:, u, :], ALU.add).then_inc(m2_delta, 1)
                    for u in range(2):
                        C = l * NC + i * 2 + u
                        dve.wait_ge(m2_adisc, nth(m2_adisc, C))
                        dve.wait_ge(m2_uin, nth(m2_uin, C))
                        V.tensor_tensor_scan(st[:, ds((i * 2 + u) * SEQ, SEQ)], adisc[:, u, :], uin[:, u, :], 0.0,
                                             ALU.mult, ALU.add).then_inc(m2_scan, 1)

            def m3(l):
                with dve.Fori(0, NC // 2) as i:
                    for u in range(2):
                        C = l * NC + i * 2 + u
                        c = i * 2 + u
                        dve.wait_ge(m3_sum, nth(m3_sum, C))
                        dve.wait_ge(m3_out, nth(m3_out, C - 2))
                        V.tensor_tensor(y[:, u, :, :], zz[:, :, ds(c * CH, CH)],
                                        ps[:, 4 + u, :].unsqueeze(1).broadcast_to([P, 2, CH]), ALU.mult)\
                            .then_inc(m3_y, 1)
                    for u in range(2):
                        C = l * NC + i * 2 + u
                        dve.wait_ge(m3_out, nth(m3_out, C))
                        dve.wait_ge(m3_skip, nth(m3_skip, C))
                        V.tensor_tensor(xa[:, ds((i * 2 + u) * CH, CH)], ps[:, 6 + u, :], xd[:, u, :], ALU.add)\
                            .then_inc(m3_res, 1)

            def f(l):
                with dve.Fori(0, NC // 2) as i:
                    for u in range(2):
                        C = l * NC + i * 2 + u
                        c = i * 2 + u
                        dve.wait_ge(f_acc, nth(f_acc, C, 1))
                        V.scalar_tensor_tensor(xa[:, ds(c * CH, CH)], ps[:, 4 + u, :], M("b_f2"),
                                               xa[:, ds(c * CH, CH)], ALU.add, ALU.add).then_inc(f_out, 1)

            def attention(e, probsparse, part="middle"):
                stream = res if probsparse else xa

                def low(b, n):
                    B = e * BATCH + b
                    term, bias, at_ = ((2, "bq", 0), (1, "bk", SEQ))[n]
                    dve.wait_ge(at_hi, nth(at_hi, B, 1))
                    V.scalar_tensor_tensor(qks[:, n, term, :], ps[:, 7, at_:at_ + SEQ], T(bias),
                                           qks[:, n, 0, :].bitcast(F32),
                                           ALU.add, ALU.subtract).then_inc(at_lo, 1)

                def lay_v(b, r):
                    B = e * BATCH + b
                    dve.wait_ge(at_proj, nth(at_proj, B, 1))
                    dve.wait_ge(at_pv, nth(at_pv, B - 3, 3))
                    V.tensor_tensor(vx[r][:, :, :, 0:DH],
                                    ps[:, 7, 0:SEQ].rearrange("p (t h d) -> p t h d", t=2, d=DH),
                                    T("bvb").rearrange("p (h d) -> p h d", d=DH).unsqueeze(1)
                                    .broadcast_to([P, 2, HEADS, DH]), ALU.add).then_inc(at_lo, 1)

                def minus_max_low(b, half):
                    B = e * BATCH + b
                    dve.wait_ge(at_mh, nth(at_mh, B, half))
                    V.scalar_tensor_tensor(ml[:, half, :], ps[0:8, 7, 0:SEQ], -1.0, mh[:, half, :].bitcast(F32),
                                           ALU.mult, ALU.subtract).then_inc(at_ml, 1)

                def maxima(b, h, r):
                    B = e * BATCH + b
                    dve.wait_ge(at_am, nth(at_am, B, h))
                    V.tensor_reduce(mxs[:, r, h, :], ps[:, h % 2, :].rearrange("p (t k) -> p t k", t=2), AX.X, ALU.max)\
                        .then_inc(at_max, 1)

                def divide(b, qt):
                    B = e * BATCH + b
                    o = ps[:, 7, :].rearrange("p (h c) -> p h c", c=32)
                    dve.wait_ge(at_otp, nth(at_otp, B, qt))
                    dve.wait_ge(at_ot, nth(at_ot, B, qt - 1))
                    V.reciprocal(rec[:].unsqueeze(2), o[:, :, DH:DH + 1]).then_inc(at_rec, 1)
                    dve.wait_ge(at_rec, nth(at_rec, B, qt))
                    dve.wait_ge(at_obp, nth(at_obp, B - 1))
                    V.tensor_tensor(ontok[:, qt, :].rearrange("p (h d) -> p h d", d=DH), o[:, :, 0:DH],
                                    rec[:].unsqueeze(2).broadcast_to([P, HEADS, DH]), ALU.mult)\
                        .then_inc(at_ot, 1)

                def select(b, r):
                    dve.wait_ge(at_obp, nth(at_obp, e * BATCH + b))
                    dve.wait_ge(at_mask, every(at_mask, b))
                    dve.wait_ge(at_ob, nth(at_ob, e * BATCH + b - 1))
                    V.scalar_tensor_tensor(selo[:], ps[:, 7, 0:SEQ], vmean[:, r:r + 1], maskb[:],
                                           ALU.subtract, ALU.mult).then_inc(at_sel, 1)

                def add_out(b):
                    B = e * BATCH + b
                    dve.wait_ge(at_aop, nth(at_aop, B))
                    V.scalar_tensor_tensor(stream[:, ds(b * SEQ, SEQ)], ps[:, 7, 0:SEQ], T("bo"),
                                           stream[:, ds(b * SEQ, SEQ)], ALU.add, ALU.add).then_inc(at_ao, 1)

                def step(b, third, r, nxt=True, proj=True, first=False):
                    rn = (r + 1) % 3
                    for p in range(8):
                        if p == 0 and probsparse and proj:
                            sum_x(b + 2, (r + 2) % 3)
                        if nxt:
                            maxima(b + 1, 2 * p, rn)
                            maxima(b + 1, 2 * p + 1, rn)
                        if p == 0 and proj:
                            low(b + 2, 0)
                            low(b + 2, 1)
                        if p == 1:
                            minus_max_low(b, 1)
                        if p in (2, 3) and not first:
                            divide(b - 1, p - 2)
                        if p == 4 and proj:
                            lay_v(b + 2, (r + 2) % 3)
                        if p == 5:
                            if nxt:
                                minus_max_low(b + 1, 0)
                            if probsparse:
                                dve.wait_ge(at_vmp, nth(at_vmp, b))
                                dve.wait_ge(at_ob, nth(at_ob, e * BATCH + b - 3))
                                V.tensor_scalar(vmean[:, r:r + 1], ps[:, 7, SEQ:SEQ + 1], 1.0 / SEQ, T("bv"),
                                                ALU.mult, ALU.add).then_inc(at_vm, 1)
                        if p == 6 and probsparse and not first:
                            select(b - 1, (r + 2) % 3)
                        if p == 7 and not first:
                            add_out(b - 1)

                def sum_x(b, r):
                    dve.wait_ge(at_xs, nth(at_xs, e * BATCH + b))
                    V.tensor_reduce(xsum[:, r:r + 1], xs[:], AX.X, ALU.add).then_inc(at_xm, 1)

                def first_low(b):
                    if probsparse:
                        sum_x(b, b)
                    low(b, 0)
                    low(b, 1)

                def last_add():
                    if probsparse:
                        select(15, 0)
                    add_out(15)

                if part == "begin":
                    return [lambda: first_low(0), lambda: lay_v(0, 0), lambda: first_low(1), lambda: lay_v(1, 1)]
                if part == "end":
                    return [lambda: divide(15, 0), lambda: divide(15, 1), last_add]

                for h in range(HEADS):
                    maxima(0, h, 0)
                minus_max_low(0, 0)
                sequences(dve, step, lambda: None)

            def gates(n):
                dve.wait_ge(act_step, act_steps[n])
                link(V.tensor_tensor(se[:], sg[:], G("ebias").unsqueeze(1).broadcast_to([P, ntile, EXPERTS]), ALU.add))
                for t in range(ntile):
                    last = V.max(m8[:, t, :], se[:, t, :])
                link(last)
                second = m8[:, :, 1:2].broadcast_to([P, ntile, EXPERTS])
                V.tensor_tensor(gt[:], se[:], second, ALU.is_gt)
                link(V.tensor_tensor(eq[:], se[:], second, ALU.is_equal))
                flat = "p t e -> p (t e)"
                link(V.tensor_tensor_scan(cum[:].rearrange(flat), eq[:].rearrange(flat), eq[:].rearrange(flat), 0.0,
                                          ALU.add, ALU.max))
                V.memset(before[:, 0:1], 0.0)
                V.tensor_copy(before[:, 1:ntile], cum[:, 0:ntile - 1, EXPERTS - 1])
                link(V.tensor_reduce(cnt[:], gt[:], AX.X, ALU.add))
                link(V.tensor_tensor(before[:], before[:], cnt[:], ALU.subtract))
                link(V.tensor_tensor(cum[:], cum[:], before[:].unsqueeze(2).broadcast_to([P, ntile, EXPERTS]),
                                     ALU.subtract))
                link(V.scalar_tensor_tensor(eq[:], cum[:], 2.0, eq[:], ALU.is_le, ALU.mult))
                link(V.tensor_tensor(gt[:], gt[:], eq[:], ALU.add))
                V.tensor_tensor(sg[:], sg[:], gt[:], ALU.mult).then_inc(gates_ready, 1)
                dve.wait_ge(pe_step, pe_steps[n] + 1)
                for c in range(NC):
                    last = V.tensor_copy(gateT[0:EXPERTS, c * CH:(c + 1) * CH], ps[0:EXPERTS, c, :])
                link(last)
                for c in range(NC):
                    V.tensor_tensor(gateT[32:32 + EXPERTS, c * CH:(c + 1) * CH], ps[0:EXPERTS, c, :],
                                    gateT[0:EXPERTS, c * CH:(c + 1) * CH].bitcast(F32), ALU.subtract)
                for row in (0, 32):
                    V.tensor_copy(esel[row:row + EXPERTS], ident[0:EXPERTS, 0:EXPERTS].unsqueeze(2)
                                  .broadcast_to([EXPERTS, EXPERTS, P]))

            def experts(n):
                with dve.Fori(0, NC // 2) as i:
                    def split(u):
                        dve.wait_ge(e_xh, nth(e_xh, n * NC + i * 2 + u))
                        V.tensor_tensor(xl[:, u, :], xa[:, ds((i * 2 + u) * CH, CH)], xh[:, u, :].bitcast(F32),
                                        ALU.subtract).then_inc(e_xl, 1)
                    split(0)
                    for u in range(2):
                        C = n * NC + i * 2 + u
                        c = i * 2 + u
                        for k in range(BLOCKS):
                            if u == 0 and k == BLOCKS // 2:
                                split(1)
                            s = k % 2
                            dve.wait_ge(e_s, nth(e_s, C, k))
                            dve.wait_ge(e_w, nth(e_w, C, k - 2))
                            if k < SHARED:
                                V.tensor_tensor(hh[:, s, :], ps[:, 2 + s, :], sil[:, s, :], ALU.mult)\
                                    .then_inc(e_m, 1)
                            else:
                                dve.wait_ge(e_m, nth(e_m, C, k - 2))
                                V.tensor_tensor(su[:, s, :], ps[:, 2 + s, :], sil[:, s, :], ALU.mult)\
                                    .then_inc(e_t, 1)
                                dve.wait_ge(e_t, nth(e_t, C, k - SHARED))
                                V.tensor_tensor(hh[:, s, :], ps[:, 4 + s, :], su[:, s, :], ALU.mult)\
                                    .then_inc(e_m, 1)
                        dve.wait_ge(e_w, nth(e_w, C, BLOCKS - 1))
                        V.tensor_tensor(res[:, ds(c * CH, CH)], ps[:, 6 + u, :], res[:, ds(c * CH, CH)], ALU.add)\
                            .then_inc(e_out, 1)

            def choose():
                dve.wait_ge(load_i, 16)
                link(V.tensor_copy(idx_f[:], idx_i[:]))
                link(V.tensor_scalar(idx_n[:], idx_f[:], 0.0, float(SEQ), ALU.is_lt, ALU.mult))
                link(V.tensor_tensor(idx_f[:], idx_f[:], idx_n[:], ALU.add))
                link(V.tensor_scalar(idx_n[:], idx_f[:], 0.0, float(SEQ - 1), ALU.max, ALU.min))
                V.tensor_copy(idx_c[:], idx_n[:]).then_inc(idx_ready, 1)
                dve.wait_ge(taken, 1)
                link(V.tensor_reduce(mxq[:, 0, 0, :].rearrange("p (b o) -> p b o", o=1), xg[:, :, 0:SAMPLES], AX.X,
                                     ALU.add))
                V.tensor_scalar(xg[:, :, SAMPLES], mxq[:, 0, 0, :], 1.0 / SAMPLES, None, ALU.mult)\
                    .then_inc(gathered, 1)
                dve.wait_ge(sampled, 2)
                with dve.Fori(0, BATCH // 2) as i:
                    for u in range(2):
                        b = i * 2 + u
                        dve.wait_ge(b_s, nth(b_s, b - 2, 1))
                        V.tensor_tensor(kbd[:, u], ksg[:, ds(b, 1), :].broadcast_to([P, HEADS, SC]),
                                        headmask[:].unsqueeze(2).broadcast_to([P, HEADS, SC]), ALU.mult)\
                            .then_inc(b_kbd, 1)
                    for u in range(2):
                        b = i * 2 + u
                        for qt in range(2):
                            s = ps[:, 2 + 2 * qt:4 + 2 * qt, 0:8 * SC].rearrange("p g (h s) -> p g h s", s=SC)
                            dve.wait_ge(b_s, nth(b_s, b, qt))
                            dve.wait_ge(b_m, nth(b_m, b - 1, qt))
                            V.tensor_reduce(mxq[:, u, qt, :].rearrange("p (g h) -> p g h", g=2), s[:, :, :, 0:SAMPLES],
                                            AX.X, ALU.max).then_inc(b_mx, 1)
                            dve.wait_ge(b_mx, nth(b_mx, b, qt))
                            V.tensor_tensor(mall[:, qt, ds(b, 1), :].rearrange("p o (g h) -> p (o g) h", g=2),
                                            mxq[:, u, qt, :].rearrange("p (g h) -> p g h", g=2),
                                            s[:, :, :, SAMPLES], ALU.subtract).then_inc(b_m, 1)
                dve.wait_ge(pe_step, pe_steps["rows"])
                V.tensor_copy(mwork[:], ps[:, 6, :].rearrange("p (g q) -> p g q", g=2))
                link(V.tensor_copy(mrow[:], ps[:, 6, :].rearrange("p (g q) -> p g q", g=2)))
                for rnd in range((TOP + 7) // 8):
                    for g in range(2):
                        last = V.max(mtop[:, g, :], mwork[:, g, :])
                    link(last)
                    if 8 * rnd + 8 < TOP:
                        for g in range(2):
                            last = V.match_replace(mwork[:, g, :], mtop[:, g, :], mwork[:, g, :], -3.0e38)
                        link(last)
                least = (TOP - 1) % 8
                for g in range(2):
                    V.tensor_scalar(mgt[:, g, :], mrow[:, g, :], mtop[:, g, least:least + 1], None, ALU.is_gt)
                    last = V.tensor_scalar(meq[:, g, :], mrow[:, g, :], mtop[:, g, least:least + 1], None, ALU.is_equal)
                link(last)
                V.tensor_reduce(mneed[:].unsqueeze(2), mgt[:], AX.X, ALU.add)
                for g in range(2):
                    last = V.tensor_tensor_scan(mcum[:, g, :], meq[:, g, :], meq[:, g, :], 0.0, ALU.add, ALU.max)
                link(last)
                link(V.tensor_scalar(mneed[:], mneed[:], -1.0, float(TOP), ALU.mult, ALU.add))
                for g in range(2):
                    last = V.scalar_tensor_tensor(mcum[:, g, :], mcum[:, g, :], mneed[:, g:g + 1], meq[:, g, :],
                                                  ALU.is_le, ALU.mult)
                link(last)
                V.tensor_tensor(mwork[:], mgt[:], mcum[:], ALU.add).then_inc(mask_ready, 1)

            V.memset(acol[:, 3:4], EPS)
            V.memset(acol[:, 4:5], 0.0)
            gate(dve, SETUP)
            norm(0, xa)
            gate(dve, LN0)
            for n, (h_, l_) in enumerate(((w1h, w1l), (w2h, w2l))):
                dve.wait_ge(act_step, n + 1)
                V.tensor_tensor(l_[:].rearrange("p k n -> p (k n)"), w12raw[:, n, :],
                                h_[:].rearrange("p k n -> p (k n)").bitcast(F32), ALU.subtract)
            gate(dve, SPLIT)
            with dve.Fori(0, LAYERS) as l:
                dve.wait_ge(load_m, l * 48 + 48)
                dve.sem_inc(waited, 1)
                m1(l)
                m2(l)
                m3(l)
                dve.wait_ge(load_f, l * 16 + 16)
                dve.sem_inc(waited, 1)
                dve.wait_ge(load_t, l * 16 + 16)
                dve.sem_inc(waited, 1)
                dve.wait_ge(pool_step, l * 3 + CLEARED)
                begin = attention(l, False, "begin")
                norm(l * 2 + 1, gain=("g1", "be1"),
                     hooks={(0, 3): begin[0], (1, 0): begin[1], (1, 2): begin[2], (1, 3): begin[3]})
                attention(l, False)
                end = attention(l, False, "end")
                norm(l * 2 + 2, gain=("g2", "be2"), hooks={(0, 0): end[0], (0, 1): end[1], (0, 3): end[2]})
                f(l)
            gate(dve, STAGE_A)
            norm(9, xa, added=True)
            gate(dve, LN_F1)
            dve.wait_ge(load_g, 32)
            gates(0)
            gate(dve, GATE_F1)
            experts(0)
            gate(dve, EXP_F1)
            norm(10, xa)
            gate(dve, LN_B)
            dve.wait_ge(load_t, (LAYERS + 1) * 16)
            choose()
            gate(dve, CHOOSE)
            for step in attention(LAYERS, True, "begin"):
                step()
            attention(LAYERS, True)
            for step in attention(LAYERS, True, "end"):
                step()
            gate(dve, ATT_B)
            norm(11, xa)
            gate(dve, LN_F2)
            gates(1)
            gate(dve, GATE_F2)
            experts(1)
            gate(dve, EXP_F2)

        @block.gpsimd
        def _(pool):
            G_ = nc.gpsimd

            def clear_queries():
                for r in range(2):
                    G_.memset(qv[r][:].bitcast(F32), 0.0)

            def clear_operands(n):
                for r in range(3):
                    G_.memset(vx[r][:], 0.0)
                G_.memset(qv[2][:].bitcast(F32), 0.0).then_inc(pool_step, 1)
                pool.wait_ge(pool_step, n * 3 + 3)
                pool.sem_inc(waited, 1)
                for r in range(3):
                    last = G_.memset(vx[r][:, :, :, DH:DH + 1], 1.0)
                last.then_inc(pool_step, 1)
                pool.wait_ge(pool_step, n * 3 + 4)
                pool.sem_inc(waited, 1)
                for r in range(3):
                    last = G_.memset(k4[r][96:P].bitcast(F32), 1.0)
                last.then_inc(pool_step, 1)
                pool.wait_ge(pool_step, n * 3 + 5)
                pool.sem_inc(waited, 1)

            def attention(e, probsparse):
                with pool.Fori(0, BATCH // 2) as i:
                    for u in range(2):
                        b = i * 2 + u
                        if not probsparse and u == 0:
                            pool.wait_ge(ln_aff, nth(ln_aff, e * (2 * NC) + i))
                        pool.wait_ge(at_proj, nth(at_proj, e * BATCH + b - 1, 1))
                        G_.tensor_copy(xs[:], xa[:, ds(b * SEQ, SEQ)]).then_inc(at_xs, 1)

            def clear_gates():
                G_.memset(gateT[:].bitcast(F32), 0.0)
                G_.memset(esel[:].bitcast(F32), 0.0)

            def diagonal(t, value):
                G_.affine_select(out=t, in_=t, compare_op=ALU.not_equal, fill=value, base=0, pattern=[[-1, P]],
                                 channel_multiplier=1)

            G_.memset(wxp[:], 0.0)
            G_.memset(ident[:], 0.0)
            G_.memset(center[:], -1.0 / P)
            G_.memset(average[:], 1.0 / P)
            G_.memset(halfavg[:], 0.0)
            G_.memset(halfsum[:], 0.0).then_inc(setup_done, 1)
            pool.wait_ge(setup_done, 1)
            diagonal(ident[:], 1.0)
            diagonal(center[:], 1.0 - 1.0 / P)
            for hb in range(2):
                G_.memset(halfavg[:, hb, hb * STATES:(hb + 1) * STATES], 1.0 / P)
            for hb in range(2):
                pool.drain().then_inc(pool_step, 1)
                pool.wait_ge(pool_step, hb + 1)
                G_.memset(halfsum[hb * STATES:(hb + 1) * STATES, hb, :], 1.0)
            gate(pool, SETUP)
            gate(pool, LN0)
            gate(pool, SPLIT)
            with pool.Fori(0, LAYERS) as l:
                pool.wait_ge(m2_u, every(m2_u, l * NC + (NC - 1)))
                pool.sem_inc(waited, 1)
                clear_queries()
                pool.wait_ge(m3_y, every(m3_y, l * NC + (NC - 1)))
                pool.sem_inc(waited, 1)
                clear_operands(l)
                attention(l, False)
            gate(pool, STAGE_A)
            clear_gates()
            gate(pool, LN_F1)
            gate(pool, GATE_F1)
            gate(pool, EXP_F1)
            clear_queries()
            clear_operands(LAYERS)
            gate(pool, LN_B)
            G_.memset(headmask[:], 1.0).then_inc(pool_step, 1)
            pool.wait_ge(pool_step, 3 * LAYERS + 6)
            G_.affine_select(out=headmask[:], in_=headmask[:], compare_op=ALU.is_ge, fill=0.0, base=0,
                             pattern=[[-DH, HEADS]], channel_multiplier=1).then_inc(pool_step, 1)
            pool.wait_ge(pool_step, 3 * LAYERS + 7)
            G_.affine_select(out=headmask[:], in_=headmask[:], compare_op=ALU.is_ge, fill=0.0, base=DH - 1,
                             pattern=[[DH, HEADS]], channel_multiplier=-1)
            pool.wait_ge(idx_ready, 1)
            xn = xa[:].rearrange("p (b s) -> p b s", s=SEQ)
            with pool.Fori(0, SAMPLES) as s:
                at_ = pool.value_load(idx_c[0:1, ds(s, 1)], min_val=0, max_val=SEQ - 1)
                G_.tensor_copy(xg[:, :, ds(s, 1)], xn[:, :, ds(at_, 1)]).then_inc(column_taken, 1)
            pool.wait_ge(column_taken, SAMPLES)
            pool.sem_inc(taken, 1)
            gate(pool, CHOOSE)
            attention(LAYERS, True)
            gate(pool, ATT_B)
            clear_gates()
            gate(pool, LN_F2)
            gate(pool, GATE_F2)
            gate(pool, EXP_F2)


def kernel(**inputs):
    import numpy as np
    import concourse.bacc as bacc
    from concourse.bass_utils import run_bass_kernel_spmd

    a = {k[len("L0_"):]: np.asarray(v) for k, v in inputs.items()}
    m = {k[len("attn_a_"):]: v for k, v in a.items() if k.startswith("attn_a_")}
    b = {k[len("attn_b_"):]: v for k, v in a.items() if k.startswith("attn_b_")}
    g = {k[len("ffn_"):]: v for k, v in a.items() if k.startswith("ffn_")}

    def fill(out, table, **parts):
        for name, part in parts.items():
            at, n = table[name]
            out[:, at:at + n] = np.asarray(part).reshape(P, n)

    def blocks(w):
        return w.T.reshape(-1, P, w.shape[0]).transpose(1, 0, 2)

    def columns(v):
        return v.reshape(-1, P).T

    mws = np.zeros((LAYERS + 1, P, MCOLS), np.float32)
    xps = np.zeros((LAYERS + 1, P, 2, STATES), np.float32)
    tws = np.zeros((LAYERS + 1, P, TCOLS), np.float32)
    for l in range(LAYERS):
        fill(mws[l], MW, win=m["W_in"][l].T, wdt=blocks(m["W_dt"][l]), wout=blocks(m["W_out"][l]), wf1=m["W_f1"][l].T,
             wf2=blocks(m["W_f2"][l]), b_in=columns(m["b_in"][l]), b_dt=m["b_dt"][l], b_xp=np.tile(m["b_xp"][l], 2),
             b_out=m["b_out"][l], Dp=m["Dp"][l], A_log=np.tile(m["A_log"][l], 2), g1=m["g1"][l], be1=m["be1"][l],
             g2=m["g2"][l], be2=m["be2"][l], b_f1=columns(m["b_f1"][l]), b_f2=m["b_f2"][l])
        xps[l] = blocks(m["W_xp"][l])
        wq, wk, wv = (m["W_qkv"][l][k * D:(k + 1) * D].T for k in range(3))
        bq, bk, bv = (m["b_qkv"][l][k * D:(k + 1) * D] for k in range(3))
        fill(tws[l], TW, wq=wq, wk=wk, wv=wv, wo=m["W_ao"][l].T, bq=bq, bk=bk, bo=m["b_ao"][l], bv=bv,
             bvb=np.broadcast_to(bv, (P, D)))
    mws[LAYERS], xps[LAYERS] = mws[LAYERS - 1], xps[LAYERS - 1]
    fill(tws[LAYERS], TW, wq=b["Wq"].T, wk=b["Wk"].T, wv=b["Wv"].T, wo=b["Wo"].T, bq=b["bq"], bk=b["bk"], bo=b["bo"], bv=b["bv"],
         bvb=np.broadcast_to(b["bv"], (P, D)))
    w12 = np.stack([np.concatenate([g[f"shared_w{k}"][0], g[f"routed_w{k}"].transpose(1, 0, 2).reshape(P, -1)], 1)
                    for k in (1, 2)], 1)
    gws = np.zeros((P, GCOLS), np.float32)
    w3 = np.concatenate([g["shared_w3"][0].reshape(SHARED, P, D), g["routed_w3"]], 0).transpose(1, 0, 2)
    fill(gws, GW, w3=w3, router=g["router_w"], ebias=np.broadcast_to(g["expert_bias"], (P, EXPERTS)))
    arrays = {
        "x_in": np.ascontiguousarray(m["x"].reshape(TOK, D).T), "mw_in": mws, "xp_in": xps, "tw_in": tws,
        "w12_in": np.ascontiguousarray(w12), "gw_in": gws,
        "idx_in": np.ascontiguousarray(np.broadcast_to(b["sample_idx"], (P, SAMPLES))),
    }
    nc = bacc.Bacc("TRN2", target_bir_lowering=False, num_devices=1)
    args = [nc.dram_tensor(n, v.shape, mybir.dt.from_np(v.dtype), kind="ExternalInput").ap() for n, v in arrays.items()]
    args.append(nc.dram_tensor("out", (P, TOK), F32, kind="ExternalOutput").ap())
    build_program(nc, *args)
    r = run_bass_kernel_spmd(nc, [arrays], core_ids=[0])
    return r.results[0]["out"].T.reshape(BATCH, SEQ, D)
```

```python
from contextlib import ExitStack

import concourse.bass as bass
from concourse import mybir

F32 = mybir.dt.float32
F32R = mybir.dt.float32r
I32 = mybir.dt.int32
ALU = mybir.AluOpType
ACT = mybir.ActivationFunctionType
AX = mybir.AxisListType
ds = bass.ds

P = 128
BATCH, SEQ, D = 16, 256, 128
TOK = BATCH * SEQ
CH = 512
NC = TOK // CH
LAYERS, STATES, HEADS, DH = 4, 64, 16, 8
DI, DF = 2 * D, 4 * D
EXPERTS, SHARED = 16, 4
BLOCKS = EXPERTS + SHARED
SAMPLES = TOP = 35
POOL_FIVES = 4
SC = SAMPLES + 1
EPS = 1e-5
QSCALE = 1.0 / DH ** 0.5
CREDIT = 4

MW = {}
for _name, _n in (("win", 2 * DI), ("wdt", 2 * D), ("wout", 2 * D), ("b_in", 4), ("b_dt", 1), ("b_xp", 1),
                  ("b_out", 1), ("Dp", 1), ("A_log", 1), ("wf1", DF), ("wf2", DF), ("g1", 1), ("be1", 1), ("g2", 1),
                  ("be2", 1), ("b_f1", 4), ("b_f2", 1)):
    MW[_name] = (sum(n for _, n in MW.values()), _n)
MCOLS = sum(n for _, n in MW.values())
MSPLIT = MW["wf1"][0]
TW = {}
for _name, _n in (("wq", D), ("wk", D), ("wv", D), ("wo", D), ("bvb", D), ("bq", 1), ("bk", 1), ("bo", 1), ("bv", 1)):
    TW[_name] = (sum(n for _, n in TW.values()), _n)
TCOLS = sum(n for _, n in TW.values())
GW = {}
for _name, _n in (("w3", BLOCKS * D), ("router", EXPERTS), ("ebias", EXPERTS)):
    GW[_name] = (sum(n for _, n in GW.values()), _n)
GCOLS = sum(n for _, n in GW.values())


def build_program(nc, x_d, mw_d, xp_d, tw_d, w12_d, gw_d, idx_d, out_d):
    ctx = ExitStack()
    with ctx:
        def sem(name):
            return ctx.enter_context(nc.semaphore(name))

        base = (nc.sbuf_base + 63) // 64 * 64
        top = [base]

        def at(name, shape, dt=F32, where=None):
            where = top if where is None else where
            n = 4
            for s in shape[1:]:
                n *= s
            t = nc.alloc_sbuf_tensor_at(name, shape, dt, offset=where[0])
            where[0] += (n + 63) // 64 * 64
            return t

        streams = at("streams", [P, 2 * TOK])
        xa = streams[:, 0:TOK]
        res = streams[:, TOK:2 * TOK]
        mw = at("mw", [P, MCOLS])
        tw = at("tw", [P, TCOLS])
        wxp = at("wxp", [P, 2, 2, P])
        w1h = at("w1h", [P, BLOCKS, D], F32R)
        w1l = at("w1l", [P, BLOCKS, D], F32R)
        w2h = at("w2h", [P, BLOCKS, D], F32R)
        w2l = at("w2l", [P, BLOCKS, D], F32R)
        gw = at("gw", [P, GCOLS])
        ident = at("ident", [P, P])
        center = at("center", [P, P])
        average = at("average", [P, P])
        halfavg = at("halfavg", [P, 2, P])
        halfsum = at("halfsum", [P, 2, P])
        acol = at("acol", [P, 5])
        work = top[0]
        end = nc.sbuf_usable_end

        def M(name, k=0, n=None):
            a, m = MW[name]
            return mw[:, a + k:a + k + (m if n is None else n)]

        def T(name, k=0, n=None):
            a, m = TW[name]
            return tw[:, a + k:a + k + (m if n is None else n)]

        def G(name, k=0, n=None):
            a, m = GW[name]
            return gw[:, a + k:a + k + (m if n is None else n)]

        w = [work + (3 * 16 + 3 * 4 + 3 * 4) * 1024]
        sq = at("sq", [P, 2, CH], where=w)
        logv = at("logv", [P, 2, CH], where=w)
        rstd = at("rstd", [P, 2, CH], where=w)
        unit = at("unit", [P, 2, CH], where=w)
        w = [work]
        xi = at("xi", [P, 2, TOK], where=w)
        zz = at("zz", [P, 2, TOK], where=w)
        st = at("st", [P, NC * SEQ], where=w)
        scan_at = w[0]
        absd = at("absd", [P, 2, CH], where=w)
        logd = at("logd", [P, 2, CH], where=w)
        posd = at("posd", [P, 2, CH], where=w)
        delta = at("delta", [P, 2, CH], where=w)
        shared_at = w[0]
        sres = at("sres", [P, 2, 2, CH], where=w)
        w = [shared_at]
        y = at("y", [P, 2, 2, CH], where=w)
        xd = at("xd", [P, 2, CH], where=w)
        adisc = at("adisc", [P, 2, SEQ], where=w)
        uin = at("uin", [P, 2, SEQ], where=w)
        winh = at("winh", [P, 2 * DI], F32R, where=w)
        winl = at("winl", [P, 2 * DI], F32R, where=w)
        assert w[0] <= end
        w = [scan_at]
        mxh = at("mxh", [P, 2, CH], F32R, where=w)
        mxl = at("mxl", [P, 2, CH], F32R, where=w)
        w = [work]
        hid = at("hid", [P, 2, 2, CH], where=w)
        fxh = at("fxh", [P, 2, CH], F32R, where=w)
        fxl = at("fxl", [P, 2, CH], F32R, where=w)
        wf1h = at("wf1h", [P, DF], F32R, where=w)
        wf1l = at("wf1l", [P, DF], F32R, where=w)
        w = [work]
        w12raw = at("w12raw", [P, 2, BLOCKS * D], where=w)
        w = [work]
        gateT = at("gateT", [64, TOK], F32R, where=w)
        esel = at("esel", [64, EXPERTS, P], F32R, where=w)
        xh = at("xh", [P, 2, CH], F32R, where=w)
        xl = at("xl", [P, 2, CH], F32R, where=w)
        sil = at("sil", [P, 2, CH], where=w)
        su = at("su", [P, 2, CH], where=w)
        hh = at("hh", [P, 2, CH], where=w)
        hhh = at("hhh", [P, 4, CH], F32R, where=w)
        hhl = at("hhl", [P, 4, CH], F32R, where=w)
        ntile = TOK // P
        sg = at("sg", [P, ntile, EXPERTS], where=w)
        se = at("se", [P, ntile, EXPERTS], where=w)
        m8 = at("m8", [P, ntile, 8], where=w)
        gt = at("gt", [P, ntile, EXPERTS], where=w)
        eq = at("eq", [P, ntile, EXPERTS], where=w)
        cum = at("cum", [P, ntile, EXPERTS], where=w)
        cnt = at("cnt", [P, ntile], where=w)
        before = at("before", [P, ntile], where=w)
        w3h = at("w3h", [P, BLOCKS * D], F32R, where=w)
        w3l = at("w3l", [P, BLOCKS * D], F32R, where=w)
        assert w[0] <= end
        w = [work]
        qv = [at(f"qv{r}", [P, HEADS, SEQ], F32R, where=w) for r in range(3)]
        k4 = [at(f"k4{r}", [P, 4, SEQ], F32R, where=w) for r in range(3)]
        vx = [at(f"vx{r}", [P, 2, HEADS, 32], where=w) for r in range(3)]
        pt = at("pt", [P, 2, 4, 2, SEQ], where=w)
        oraw = at("oraw", [P, 4, SEQ], where=w)
        xs = at("xs", [P, SEQ], where=w)
        qks = at("qks", [P, 2, 3, SEQ], F32R, where=w)
        mh = at("mh", [8, 2, SEQ], F32R, where=w)
        ml = at("ml", [8, 2, SEQ], F32R, where=w)
        mxs = at("mxs", [P, 3, HEADS, 2], where=w)
        rec = at("rec", [P, HEADS], where=w)
        ontok = at("ontok", [P, 2, P], where=w)
        onT = at("onT", [P, SEQ], where=w)
        maskb = at("maskb", [P, SEQ], where=w)
        selo = at("selo", [P, SEQ], where=w)
        vmean = at("vmean", [P, 3], where=w)
        xsum = at("xsum", [P, 3], where=w)
        assert w[0] <= end, (w[0], end)
        w = [work + (3 * 16 + 3 * 4 + 3 * 4) * 1024]
        idx_i = at("idx_i", [P, SAMPLES], I32, where=w)
        idx_f = at("idx_f", [P, SAMPLES], where=w)
        idx_n = at("idx_n", [P, SAMPLES], where=w)
        idx_c = at("idx_c", [P, SAMPLES], I32, where=w)
        xg = at("xg", [P, BATCH, SC], where=w)
        ksg = at("ksg", [P, BATCH, SC], where=w)
        headmask = at("headmask", [P, HEADS], where=w)
        kbd = at("kbd", [P, 2, HEADS, SC], where=w)
        qf = at("qf", [P, 2, SEQ], where=w)
        mxq = at("mxq", [P, 2, 2, HEADS], where=w)
        mall = at("mall", [P, 2, BATCH, HEADS], where=w)
        mrow = at("mrow", [P, 2, SEQ], where=w)
        mwork = at("mwork", [P, 2, SEQ], where=w)
        mtop = at("mtop", [P, 2, 8], where=w)
        mgt = at("mgt", [P, 2, SEQ], where=w)
        meq = at("meq", [P, 2, SEQ], where=w)
        mcum = at("mcum", [P, 2, SEQ], where=w)
        mneed = at("mneed", [P, 2], where=w)

        ps = ctx.enter_context(nc.psum_tensor("ps", [P, 8, CH], F32))
        qk_d = nc.dram_tensor("qk_scratch", (2, P, 3, SEQ), F32, kind="Internal").ap()
        mask_d = nc.dram_tensor("mask_scratch", (BATCH * P, SEQ), F32, kind="Internal").ap()

        counted = {}

        def counter(name, n=1):
            s = sem(name)
            counted[s.name] = (s, n)
            return s

        phase_done = sem("phase_done")
        load_x = [sem(f"load_x{c}") for c in range(NC)]
        load_m = sem("load_m")
        load_f = sem("load_f")
        load_t = sem("load_t")
        load_g = sem("load_g")
        load_i = sem("load_i")
        stored = sem("stored")
        gates_clear = sem("gates_clear")
        gates_ready = sem("gates_ready")
        gates_rows = sem("gates_rows")
        gates_high = sem("gates_high")
        gates_set = sem("gates_set")
        w3_high = sem("w3_high")
        w3_set = sem("w3_set")
        idx_ready = sem("idx_ready")
        column_taken = sem("column_taken")
        column_copied = sem("column_copied")
        taken = sem("taken")
        gathered = sem("gathered")
        sampled = sem("sampled")
        mask_ready = sem("mask_ready")
        mask_stored = sem("mask_stored")
        setup_done = sem("setup_done")
        waited = sem("waited")
        dve_step = sem("dve_step")
        act_step = sem("act_step")
        pool_step = sem("pool_step")
        pe_step = sem("pe_step")

        ln_cen = counter("ln_cen")
        ln_sq = counter("ln_sq")
        ln_var = counter("ln_var")
        ln_log = counter("ln_log")
        ln_rstd = counter("ln_rstd")
        ln_unit = counter("ln_unit")
        ln_aff = counter("ln_aff")
        acol_exp = counter("acol_exp")
        acol_neg = counter("acol_neg")
        acol_skip = counter("acol_skip")
        split_step = sem("split_step")
        win_set = sem("win_set")
        wf1_set = sem("wf1_set")
        m1_xh = counter("m1_xh")
        m1_xl = counter("m1_xl")
        f_xh = counter("f_xh")
        f_xl = counter("f_xl")
        m1_psum = counter("m1_psum", 4)
        m1_evac = counter("m1_evac", 4)
        m1_gate = counter("m1_gate")
        m2_dt = counter("m2_dt")
        m2_u = counter("m2_u")
        m2_mean = counter("m2_mean")
        m2_abs = counter("m2_abs")
        m2_exp = counter("m2_exp")
        m2_log = counter("m2_log")
        m2_pos = counter("m2_pos")
        m2_delta = counter("m2_delta")
        m2_uin = counter("m2_uin")
        m2_adisc = counter("m2_adisc")
        m2_scan = counter("m2_scan")
        m3_sum = counter("m3_sum")
        m3_y = counter("m3_y")
        m3_out = counter("m3_out")
        m3_skip = counter("m3_skip")
        m3_res = counter("m3_res")
        f_h = counter("f_h", 4)
        f_g = counter("f_g", 4)
        f_acc = counter("f_acc", 2)
        f_out = counter("f_out")
        add_res = counter("add_res")
        e_h = counter("e_h", BLOCKS)
        e_g = counter("e_g", BLOCKS)
        e_s = counter("e_s", BLOCKS)
        e_t = counter("e_t", EXPERTS)
        e_m = counter("e_m", BLOCKS)
        e_w = counter("e_w", BLOCKS)
        e_hi = counter("e_hi", BLOCKS)
        e_lo = counter("e_lo", BLOCKS)
        e_xh = counter("e_xh")
        e_xl = counter("e_xl")
        e_out = counter("e_out")
        at_xs = counter("at_xs")
        at_proj = counter("at_proj", 2)
        at_hi = counter("at_hi", 2)
        at_lo = counter("at_lo", 3)
        at_spill = counter("at_spill", 16)
        at_scat = [sem(f"at_scat{r}") for r in range(3)]
        at_am = counter("at_am", 16)
        at_max = counter("at_max", 16)
        at_tp = counter("at_tp", 2)
        at_mh = counter("at_mh", 2)
        at_ml = counter("at_ml", 2)
        at_mx = [counter(f"at_mx{h}", 32) for h in range(2)]
        at_sc = counter("at_sc", 8)
        at_exp = counter("at_exp", 8)
        at_pv = counter("at_pv", 4)
        at_oev = counter("at_oev", 4)
        at_otp = counter("at_otp", 2)
        at_rec = counter("at_rec", 2)
        at_ot = counter("at_ot", 2)
        at_obp = counter("at_obp")
        at_ob = counter("at_ob")
        at_aop = counter("at_aop")
        at_ao = counter("at_ao")
        at_xm = counter("at_xm")
        at_vmp = counter("at_vmp")
        at_vm = counter("at_vm")
        at_sel = counter("at_sel")
        at_mask = counter("at_mask", 16)
        b_kbd = counter("b_kbd")
        b_q = counter("b_q")
        b_qf = counter("b_qf")
        b_s = counter("b_s", 2)
        b_mx = counter("b_mx", 2)
        b_m = counter("b_m", 2)

        def nth(s, c, k=0):
            n = counted[s.name][1]
            return n * c + (n * CREDIT + k + 1)

        def every(s, c):
            n = counted[s.name][1]
            return n * c + n * (CREDIT + 1)

        SETUP, LN0, SPLIT, STAGE_A, EXP_F1, LN_B, CHOOSE, EXP_F2 = range(8)

        def passed(eng, n):
            eng.wait_ge(phase_done, 4 * n + 4)

        def gate(eng, n):
            eng.drain().then_inc(phase_done, 1)
            passed(eng, n)

        CLEARED = 5

        NR = [(BATCH + 2 - r) // 3 for r in range(3)]

        SPREAD = 16 * 5

        def scattered(e, third, r):
            return e * (NR[r] * SPREAD) + third * SPREAD + SPREAD

        def sequences(eng, step, last):
            step(0, 0, 0, first=True)
            with eng.Fori(0, 4) as i:
                for k in range(3):
                    step(i * 3 + (1 + k), i + (1 + k) // 3, (1 + k) % 3)
            step(13, 4, 1)
            step(14, 4, 2, proj=False)
            step(15, 5, 0, nxt=False, proj=False)
            last()

        pe_steps = {0: 1, 1: 4, "samples": 2, "rows": 3}
        act_steps = {0: 3, 1: 4}

        block = ctx.enter_context(nc.Block())

        @block.sync
        def _(sp):
            for c in range(NC):
                sp.dma_start(res[:, c * CH:(c + 1) * CH], x_d[:, c * CH:(c + 1) * CH]).then_inc(load_x[c], 16)
            for s, n in counted.values():
                sp.sem_inc(s, CREDIT * n)

            def load_layer(l):
                sp.dma_start(mw[:, 0:MSPLIT], mw_d[ds(l, 1), :, 0:MSPLIT].rearrange("o p n -> (o p) n"))\
                  .then_inc(load_m, 16)
                for hb in range(2):
                    sp.dma_start(wxp[:, hb, :, hb * STATES:(hb + 1) * STATES],
                                 xp_d[ds(l, 1)].rearrange("o p k n -> (o p) k n")).then_inc(load_m, 16)

            def load_network(l):
                sp.dma_start(mw[:, MSPLIT:MCOLS], mw_d[ds(l, 1), :, MSPLIT:MCOLS].rearrange("o p n -> (o p) n"))\
                  .then_inc(load_f, 16)

            def load_attention(l):
                sp.dma_start(tw[:], tw_d[ds(l, 1)].rearrange("o p n -> (o p) n")).then_inc(load_t, 16)

            sp.dma_start(w12raw[:], w12_d).then_inc(load_g, 16)
            sp.wait_ge(setup_done, 1)
            load_layer(0)
            load_attention(0)
            load_network(0)
            sp.dma_start(gw[:], gw_d).then_inc(load_g, 16)

            def attention(e, probsparse):
                def send_max(b, half, r):
                    B = e * BATCH + b
                    for row, part, ready in ((96, mh, at_mh), (97, ml, at_ml)):
                        sp.wait_ge(ready, nth(ready, B, half))
                        sp.dma_start(qv[r][row:row + 1, 8 * half:8 * half + 8, :].bitcast(F32),
                                     part[0:8, half, :].bitcast(F32)).then_inc(at_mx[half], 16)

                def spill_qk(b, third, r, first=False):
                    B = e * BATCH + b
                    if not first:
                        before, rb = third + (r + 2) // 3 - 1, (r + 2) % 3
                        sp.wait_ge(at_scat[rb], scattered(e, before, rb))
                    sp.wait_ge(at_lo, nth(at_lo, B, 1))
                    sp.dma_start(qk_d.rearrange("a p t n -> p a t n"), qks[:].bitcast(F32)).then_inc(at_spill, 16)

                def spread_qk(b, r):
                    B = e * BATCH + b
                    sp.wait_ge(at_spill, every(at_spill, B))
                    sp.wait_ge(at_sc, nth(at_sc, B - 3, 7))
                    rows = qk_d.rearrange("a (j x) t n -> a (x t) j n", j=4)
                    sp.dma_start(k4[r][0:96].bitcast(F32), rows[1])\
                      .then_inc(at_scat[r], 16)
                    for g in range(4):
                        sp.dma_start(qv[r][24 * g:24 * g + 24].bitcast(F32)
                                     .rearrange("p (j g) n -> p j g n", g=4)[:, :, g, :],
                                     rows[0, 24 * g:24 * g + 24])\
                          .then_inc(at_scat[r], 16)

                def send_mask(b):
                    sp.wait_ge(at_sel, nth(at_sel, b - 1))
                    sp.dma_start(maskb[:], mask_d[ds(b * P, P), :]).then_inc(at_mask, 16)

                def step(b, third, r, nxt=True, proj=True, first=False):
                    r2 = (r + 2) % 3
                    if proj:
                        spill_qk(b + 2, third + (r + 2) // 3, r2)
                    send_max(b, 1, r)
                    if probsparse and not first:
                        send_mask(b - 1)
                    if proj:
                        spread_qk(b + 2, r2)
                    if nxt:
                        send_max(b + 1, 0, (r + 1) % 3)

                for b in (0, 1):
                    spill_qk(b, 0, b, first=b == 0)
                    spread_qk(b, b)
                send_max(0, 0, 0)
                sequences(sp, step, (lambda: send_mask(15)) if probsparse else (lambda: None))

            with sp.Fori(0, LAYERS) as l:
                sp.wait_ge(m3_res, every(m3_res, l * NC + (NC - 1)))
                sp.sem_inc(waited, 1)
                load_layer(l + 1)
                sp.wait_ge(pool_step, l * 3 + CLEARED)
                sp.sem_inc(waited, 1)
                attention(l, False)
                sp.wait_ge(at_ao, every(at_ao, l * BATCH + (BATCH - 1)))
                sp.sem_inc(waited, 1)
                load_attention(l + 1)
                sp.wait_ge(f_out, every(f_out, l * NC + (NC - 1)))
                sp.sem_inc(waited, 1)
                load_network(l + 1)
            passed(sp, LN_B)
            sp.dma_start(idx_i[:], idx_d).then_inc(load_i, 16)
            sp.wait_ge(mask_ready, 1)
            for h in range(2):
                sp.dma_start(mask_d.rearrange("(g r d) n -> g r d n", g=2, d=DH)[h],
                             mwork[:, h, :].unsqueeze(1).broadcast_to([P, DH, SEQ])).then_inc(mask_stored, 16)
            sp.wait_ge(mask_stored, 16 * 2)
            passed(sp, CHOOSE)
            attention(LAYERS, True)
            for c in range(NC):
                sp.wait_ge(e_out, nth(e_out, NC + c))
                sp.dma_start(out_d[:, c * CH:(c + 1) * CH], res[:, c * CH:(c + 1) * CH]).then_inc(stored, 16)
            sp.wait_ge(load_m, 48 * (LAYERS + 1))
            sp.wait_ge(load_f, 16 * (LAYERS + 1))
            sp.wait_ge(stored, 16 * NC)

        @block.tensor
        def _(pe):
            mm = nc.tensor.matmul

            def norm(n, src, ready=None, hooks=None):
                def quad(q):
                    def centered(k):
                        c = q * 4 + k
                        if ready:
                            ready(c)
                        pe.wait_ge(ln_unit, nth(ln_unit, n * NC + c - 4))
                        mm(ps[:, k, :], center[:], src[:, ds(c * CH, CH)], start=True, stop=True).then_inc(ln_cen, 1)

                    def variance(k):
                        C = n * NC + q * 4 + k
                        pe.wait_ge(ln_sq, nth(ln_sq, C))
                        pe.wait_ge(ln_log, nth(ln_log, C - 2))
                        mm(ps[:, 4 + k % 2, :], average[:], sq[:, k % 2, :], start=True, stop=True).then_inc(ln_var, 1)
                        if hooks and (q, k) in hooks:
                            hooks[q, k]()

                    centered(0)
                    centered(1)
                    centered(2)
                    variance(0)
                    centered(3)
                    for k in range(1, 4):
                        variance(k)

                if hooks:
                    quad(0)
                    quad(1)
                else:
                    with pe.Fori(0, 2) as q:
                        quad(q)

            def m1(l):
                with pe.Fori(0, NC // 2) as i:
                    for u in range(2):
                        C = l * NC + i * 2 + u
                        if u == 0:
                            pe.wait_ge(f_out, every(f_out, l * NC - 1))
                            pe.wait_ge(win_set, l + 1)
                        pe.wait_ge(m1_xl, nth(m1_xl, l * (NC + 2) + (i * 2 + u)))
                        for o in range(4):
                            pe.wait_ge(m1_evac, nth(m1_evac, C - 2, o))
                            out, wh, wl = ps[:, 4 * u + o, :], winh[:, o * P:(o + 1) * P], winl[:, o * P:(o + 1) * P]
                            mm(out, wh, mxh[:, u, :], start=True, stop=False)
                            mm(out, wh, mxl[:, u, :], start=False, stop=False)
                            mm(out, wl, mxh[:, u, :], start=False, stop=True).then_inc(m1_psum, 1)

            def m2(l):
                with pe.Fori(0, NC // 2) as i:
                    for u in range(2):
                        C = l * NC + i * 2 + u
                        if u == 0:
                            pe.wait_ge(m1_evac, every(m1_evac, l * NC + (NC - 1)))
                        pe.wait_ge(m2_abs, nth(m2_abs, C - 2))
                        pe.wait_ge(m2_pos, nth(m2_pos, C - 2))
                        for kb in range(2):
                            last = mm(ps[:, u, :], M("wdt", kb * P, P), xi[:, kb, ds((i * 2 + u) * CH, CH)],
                                      start=kb == 0, stop=kb == 1)
                        last.then_inc(m2_dt, 1)
                        pe.wait_ge(m2_uin, nth(m2_uin, C - 2))
                        for hb in range(2):
                            for kb in range(2):
                                last = mm(ps[:, 4 + u, 0:SEQ], wxp[:, hb, kb, :],
                                          xi[:, kb, ds((i * 2 + u) * CH + hb * SEQ, SEQ)],
                                          start=hb + kb == 0, stop=hb + kb == 2)
                        last.then_inc(m2_u, 1)
                    for u in range(2):
                        C = l * NC + i * 2 + u
                        pe.wait_ge(m2_delta, nth(m2_delta, C))
                        pe.wait_ge(m2_adisc, nth(m2_adisc, C - 2))
                        for hb in range(2):
                            last = mm(ps[:, 2 + u, 0:SEQ], halfavg[:, hb, :], delta[:, u, hb * SEQ:(hb + 1) * SEQ],
                                      start=hb == 0, stop=hb == 1)
                        last.then_inc(m2_mean, 1)

            def m3(l):
                with pe.Fori(0, NC // 4) as i:
                    def states(k):
                        C = l * NC + i * 4 + k
                        pe.wait_ge(m2_scan, nth(m2_scan, C))
                        pe.wait_ge(m3_y, nth(m3_y, C - 2))
                        for hb in range(2):
                            last = mm(ps[:, 4 + k % 2, hb * SEQ:(hb + 1) * SEQ], halfsum[:, hb, :],
                                      st[:, ds((i * 4 + k) * SEQ, SEQ)], start=True, stop=True)
                        last.then_inc(m3_sum, 1)

                    def out(k):
                        C = l * NC + i * 4 + k
                        pe.wait_ge(m3_y, nth(m3_y, C))
                        pe.wait_ge(m3_res, nth(m3_res, C - 2))
                        for kb in range(2):
                            last = mm(ps[:, 6 + k % 2, :], M("wout", kb * P, P), y[:, k % 2, kb, :],
                                      start=kb == 0, stop=kb == 1)
                        last.then_inc(m3_out, 1)

                    pe.wait_ge(m2_uin, every(m2_uin, l * NC + (NC - 1)))
                    states(0)
                    states(1)
                    out(0)
                    states(2)
                    out(1)
                    states(3)
                    out(2)
                    out(3)

            def f(l):
                with pe.Fori(0, NC // 2) as i:
                    def up(u, half):
                        C = l * NC + i * 2 + u
                        if u == 0:
                            pe.wait_ge(ln_unit, nth(ln_unit, l * (2 * NC) + (2 * NC + 5 + 2 * half)))
                        if u == 0 and half == 0:
                            pe.wait_ge(wf1_set, l + 1)
                        if half == 0:
                            pe.wait_ge(f_xl, nth(f_xl, l * (NC + 2) + (i * 2 + u)))
                        pe.wait_ge(f_g, nth(f_g, C - 1, 2 * half + 1))
                        for o in (2 * half, 2 * half + 1):
                            out, wh, wl = ps[:, o, :], wf1h[:, o * P:(o + 1) * P], wf1l[:, o * P:(o + 1) * P]
                            mm(out, wh, fxh[:, u, :], start=True, stop=False)
                            mm(out, wh, fxl[:, u, :], start=False, stop=False)
                            mm(out, wl, fxh[:, u, :], start=False, stop=True).then_inc(f_h, 1)

                    def down(u, half):
                        C = l * NC + i * 2 + u
                        pe.wait_ge(f_g, nth(f_g, C, 2 * half + 1))
                        if half == 0:
                            pe.wait_ge(f_out, nth(f_out, C - 2))
                        for q in range(2):
                            last = mm(ps[:, 4 + u, :], M("wf2", (2 * half + q) * P, P), hid[:, half, q, :],
                                      start=half + q == 0, stop=half + q == 2)
                        last.then_inc(f_acc, 1)

                    up(0, 0)
                    up(0, 1)
                    down(0, 0)
                    up(1, 0)
                    down(0, 1)
                    up(1, 1)
                    down(1, 0)
                    down(1, 1)

            def attention(e, probsparse, part="middle"):
                def project_qk(b):
                    B = e * BATCH + b
                    pe.wait_ge(at_xs, nth(at_xs, B))
                    pe.wait_ge(at_lo, nth(at_lo, B - 1, 2))
                    pe.wait_ge(at_ml, nth(at_ml, B - 2, 0))
                    mm(ps[:, 7, 0:SEQ], T("wq"), xs[:], start=True, stop=True)
                    mm(ps[:, 7, SEQ:CH], T("wk"), xs[:], start=True, stop=True).then_inc(at_proj, 1)

                def project_v(b):
                    B = e * BATCH + b
                    pe.wait_ge(at_lo, nth(at_lo, B, 1))
                    pe.wait_ge(at_ot, nth(at_ot, B - 3, 1))
                    if probsparse:
                        pe.wait_ge(at_xm, nth(at_xm, b))
                    for t in range(2):
                        last = mm(ps[:, 7, t * P:(t + 1) * P], xs[:, t * P:(t + 1) * P], T("wv"),
                                  start=True, stop=True)
                    last.then_inc(at_proj, 1)

                def rows(b, h, r):
                    B = e * BATCH + b
                    pe.wait_ge(at_max, nth(at_max, B, h - 2))
                    for qt in range(2):
                        last = mm(ps[:, h % 2, qt * SEQ:(qt + 1) * SEQ], qv[r][0:96, h, qt * P:(qt + 1) * P],
                                  k4[r][0:96, h // 4, :], start=True, stop=True)
                    last.then_inc(at_am, 1)

                def maxima(b, half, r):
                    B = e * BATCH + b
                    pe.wait_ge(at_max, nth(at_max, B, 8 * half + 7))
                    for qt in range(2):
                        last = nc.tensor.transpose(ps[0:8, 7, qt * P:(qt + 1) * P],
                                                   mxs[:, r, 8 * half:8 * half + 8, qt], ident[:])
                    last.then_inc(at_tp, 1)

                def scores(b, p, r):
                    B = e * BATCH + b
                    if p % 4 == 0:
                        pe.wait_ge(at_mx[p // 4], every(at_mx[p // 4], B))
                    pe.wait_ge(at_exp, nth(at_exp, B, p - 2))
                    for hh_ in range(2):
                        h = 2 * p + hh_
                        for kt in range(2):
                            last = mm(ps[:, 2 + 2 * (p % 2) + hh_, kt * SEQ:(kt + 1) * SEQ],
                                      k4[r][0:98, h // 4, kt * P:(kt + 1) * P], qv[r][0:98, h, :],
                                      start=True, stop=True)
                    last.then_inc(at_sc, 1)

                def values(b, j, r):
                    B = e * BATCH + b
                    pe.wait_ge(at_exp, nth(at_exp, B, 2 * j + 1))
                    pe.wait_ge(at_oev, nth(at_oev, B, j - 1))
                    if j == 0:
                        pe.wait_ge(at_lo, nth(at_lo, B, 2))
                    for kt in range(2):
                        for g in range(4):
                            last = mm(ps[32 * g:32 * g + 32, 6, (j % 2) * SEQ:(j % 2 + 1) * SEQ],
                                      vx[r][:, kt, 4 * j + g, :], pt[:, j % 2, g, kt, :], start=kt == 0, stop=kt == 1)
                    last.then_inc(at_pv, 1)

                def to_rows(b, qt):
                    B = e * BATCH + b
                    if qt == 0:
                        pe.wait_ge(at_oev, nth(at_oev, B, 3))
                    else:
                        pe.wait_ge(at_ot, nth(at_ot, B, 0))
                    for j in range(4):
                        last = nc.tensor.transpose(ps[:, 7, j * P:(j + 1) * P], oraw[:, j, qt * P:(qt + 1) * P],
                                                   ident[:])
                    last.then_inc(at_otp, 1)

                def to_columns(b):
                    pe.wait_ge(at_ot, nth(at_ot, e * BATCH + b, 1))
                    for qt in range(2):
                        last = nc.tensor.transpose(ps[:, 7, qt * P:(qt + 1) * P], ontok[:, qt, :], ident[:])
                    last.then_inc(at_obp, 1)

                def out(b):
                    pe.wait_ge(at_ob, nth(at_ob, e * BATCH + b))
                    mm(ps[:, 7, 0:SEQ], T("wo"), onT[:], start=True, stop=True).then_inc(at_aop, 1)

                def mean_v(b, r):
                    mm(ps[:, 7, SEQ:SEQ + 1], T("wv"), xsum[:, r:r + 1], start=True, stop=True).then_inc(at_vmp, 1)

                def step(b, third, r, nxt=True, proj=True, first=False):
                    B = e * BATCH + b
                    t, rn = third + (r + 1) // 3, (r + 1) % 3
                    for p in range(8):
                        scores(b, p, r)
                        if nxt:
                            if p == 0:
                                pe.wait_ge(at_scat[rn], scattered(e, t, rn))
                            rows(b + 1, 2 * p, rn)
                            rows(b + 1, 2 * p + 1, rn)
                        if p == 0:
                            pe.wait_ge(at_ao, nth(at_ao, B - 2))
                            if proj:
                                project_qk(b + 2)
                        if p == 1:
                            if not first:
                                values(b - 1, 3, (r + 2) % 3)
                            if proj:
                                pe.wait_ge(at_lo, nth(at_lo, B + 2, 1))
                            maxima(b, 1, r)
                        if p == 2:
                            values(b, 0, r)
                            if not first:
                                pe.wait_ge(at_ml, nth(at_ml, B, 1))
                                to_rows(b - 1, 0)
                        if p == 3 and not first:
                            to_rows(b - 1, 1)
                        if p == 4:
                            values(b, 1, r)
                            if proj:
                                if first:
                                    pe.wait_ge(at_ml, nth(at_ml, B, 1))
                                project_v(b + 2)
                        if p == 5:
                            if proj:
                                pe.wait_ge(at_lo, nth(at_lo, B + 2, 2))
                            else:
                                pe.wait_ge(at_ot, nth(at_ot, B - 1, 1))
                            if probsparse:
                                mean_v(b, r)
                            if nxt:
                                maxima(b + 1, 0, rn)
                        if p == 6:
                            values(b, 2, r)
                            if not first:
                                if nxt:
                                    pe.wait_ge(at_ml, nth(at_ml, B + 1, 0))
                                if probsparse:
                                    pe.wait_ge(at_vm, nth(at_vm, b))
                                to_columns(b - 1)
                        if p == 7 and not first:
                            out(b - 1)

                def last_rows():
                    pe.wait_ge(at_ao, nth(at_ao, e * BATCH + 14))
                    to_rows(15, 0)

                if part == "begin":
                    return [lambda: project_qk(0), lambda: project_v(0), lambda: project_qk(1), lambda: project_v(1)]
                if part == "end":
                    return [last_rows, lambda: to_rows(15, 1), lambda: to_columns(15), lambda: out(15)]

                def last():
                    values(15, 3, 0)

                pe.wait_ge(at_scat[0], scattered(e, 0, 0))
                for h in range(HEADS):
                    if h == HEADS // 2 + 2:
                        pe.wait_ge(at_lo, nth(at_lo, e * BATCH + 1, 2))
                        maxima(0, 0, 0)
                    rows(0, h, 0)
                sequences(pe, step, last)

            def all_of(steps):
                for step in steps:
                    step()

            def router(n, c):
                def step():
                    pe.wait_ge(ln_unit, nth(ln_unit, n * NC + c))
                    for t in range(4 * c, 4 * c + 4):
                        last = mm(ps[:, 6, t * EXPERTS:(t + 1) * EXPERTS], xa[:, t * P:(t + 1) * P], G("router"),
                                  start=True, stop=True)
                    if c == NC - 1:
                        last.then_inc(pe_step, 1)
                return step

            def routers(n):
                return {((c + 2) // 4, (c + 2) % 4): router(n, c) for c in range(NC - 2)}

            def gates(n):
                pe.wait_ge(gates_ready, n + 1)
                for c in range(NC):
                    for t in range(4):
                        last = nc.tensor.transpose(ps[0:EXPERTS, c, t * P:(t + 1) * P], sg[:, 4 * c + t, :], ident[:])
                    last.then_inc(gates_rows, 1)

            def experts(n):
                pe.wait_ge(gates_set, n + 1)
                pe.wait_ge(w3_set, n + 1)

                def up(c, u, k):
                    C = n * NC + c
                    s = k % 2
                    if k == 0:
                        pe.wait_ge(e_xl, nth(e_xl, C, n))
                    if k < 2:
                        pe.wait_ge(e_m, nth(e_m, C - 1, BLOCKS - 2 + k))
                    else:
                        pe.wait_ge(e_m, nth(e_m, C, k - 2))
                    for bank, wh, wl in ((0, w1h, w1l), (2, w2h, w2l)):
                        o = ps[:, bank + s, :]
                        mm(o, wh[:, k, :], xh[:, u, :], start=True, stop=False)
                        mm(o, wh[:, k, :], xl[:, u, :], start=False, stop=False)
                        last = mm(o, wl[:, k, :], xh[:, u, :], start=False, stop=True)
                        last.then_inc(e_h if bank == 0 else e_g, 1)
                        if bank == 0 and k >= SHARED:
                            mm(ps[:, 4 + s, :], esel[:, k - SHARED, :], gateT[:, ds(c * CH, CH)], start=True, stop=True)

                def down(c, u, k):
                    C = n * NC + c
                    pe.wait_ge(e_lo, nth(e_lo, C, k))
                    if k == 0:
                        pe.wait_ge(e_out, nth(e_out, C - 2))
                    o, wh, wl = ps[:, 6 + u, :], w3h[:, k * P:(k + 1) * P], w3l[:, k * P:(k + 1) * P]
                    mm(o, wh, hhh[:, k % 4, :], start=k == 0, stop=False)
                    mm(o, wh, hhl[:, k % 4, :], start=False, stop=False)
                    mm(o, wl, hhh[:, k % 4, :], start=False, stop=k == BLOCKS - 1).then_inc(e_w, 1)

                up(0, 0, 0)
                up(0, 0, 1)
                with pe.Fori(0, NC // 2) as i:
                    for j in range(2 * BLOCKS):
                        ahead = j + 2
                        up(i * 2 + ahead // BLOCKS, ahead // BLOCKS % 2, ahead % BLOCKS)
                        down(i * 2 + j // BLOCKS, j // BLOCKS, j % BLOCKS)

            def choose():
                pe.wait_ge(gathered, 1)
                for g in range(2):
                    last = mm(ps[:, g, 0:8 * SC], T("wk"), xg[:, 8 * g:8 * g + 8, :], start=True, stop=True)
                last.then_inc(pe_step, 1)
                pe.wait_ge(sampled, 2)

                def project(b, u):
                    pe.wait_ge(b_qf, nth(b_qf, b - 2))
                    mm(ps[:, u, 0:SEQ], T("wq"), streams[:, ds(b * SEQ, SEQ)], start=True, stop=True).then_inc(b_q, 1)

                project(0, 0)
                project(1, 1)
                with pe.Fori(0, BATCH // 2) as i:
                    for u in range(2):
                        b = i * 2 + u
                        pe.wait_ge(b_qf, nth(b_qf, b))
                        pe.wait_ge(b_kbd, nth(b_kbd, b))
                        for qt in range(2):
                            pe.wait_ge(b_m, nth(b_m, b - 1, qt))
                            for g in range(2):
                                last = mm(ps[:, 2 + 2 * qt + g, 0:8 * SC], qf[:, u, qt * P:(qt + 1) * P],
                                          kbd[:, u, 8 * g:8 * g + 8, :], start=True, stop=True)
                            last.then_inc(b_s, 1)
                        project(b + 2, u)
                pe.wait_ge(b_m, every(b_m, BATCH - 1))
                for g in range(2):
                    for qt in range(2):
                        last = nc.tensor.transpose(ps[:, 6, (2 * g + qt) * P:(2 * g + qt + 1) * P],
                                                   mall[:, qt, 8 * g:8 * g + 8, :], ident[:])
                last.then_inc(pe_step, 1)

            gate(pe, SETUP)
            norm(0, res, ready=lambda c: pe.wait_ge(load_x[c], 16), hooks={"apart": None})
            gate(pe, LN0)
            gate(pe, SPLIT)
            with pe.Fori(0, LAYERS) as l:
                pe.wait_ge(load_m, l * 48 + 48)
                pe.sem_inc(waited, 1)
                m1(l)
                m2(l)
                m3(l)
                pe.wait_ge(load_t, l * 16 + 16)
                project = attention(l, False, "begin")

                def first_project():
                    pe.wait_ge(m3_res, every(m3_res, l * NC + (NC - 1)))
                    project[0]()

                norm(l * 2 + 1, xa, ready=lambda c: pe.wait_ge(m3_res, nth(m3_res, l * NC + c)),
                     hooks={(0, 2): first_project, (1, 0): project[1], (1, 1): project[2], (1, 3): project[3]})
                pe.wait_ge(ln_unit, every(ln_unit, l * (2 * NC) + (2 * NC - 1)))
                attention(l, False)
                norm(l * 2 + 2, xa, ready=lambda c: pe.wait_ge(at_ao, nth(at_ao, l * BATCH + c * 2 + 1)),
                     hooks={(0, k): step for k, step in enumerate(attention(l, False, "end"))})
                pe.wait_ge(load_f, l * 16 + 16)
                pe.sem_inc(waited, 1)
                f(l)
            gate(pe, STAGE_A)
            pe.wait_ge(load_g, 32)
            norm(9, res, ready=lambda c: pe.wait_ge(add_res, nth(add_res, c)), hooks=routers(9))
            router(9, NC - 2)()
            router(9, NC - 1)()
            gates(0)
            experts(0)
            gate(pe, EXP_F1)
            norm(10, res)
            gate(pe, LN_B)
            pe.wait_ge(load_t, (LAYERS + 1) * 16)
            choose()
            gate(pe, CHOOSE)
            all_of(attention(LAYERS, True, "begin"))
            attention(LAYERS, True)
            last = attention(LAYERS, True, "end")
            norm(11, res, ready=lambda c: pe.wait_ge(at_ao, nth(at_ao, LAYERS * BATCH + c * 2 + 1)),
                 hooks={**routers(11), (0, 0): last[0], (0, 1): last[1], (0, 2): last[2], (0, 3): last[3],
                        (1, 0): lambda: (router(11, 0)(), router(11, 1)(), router(11, 2)())})
            router(11, NC - 2)()
            router(11, NC - 1)()
            gates(1)
            experts(1)
            gate(pe, EXP_F2)

        @block.scalar
        def _(act):
            A = nc.scalar.activation

            def norm(n, hooks=None):
                def quad(q):
                    def square(k):
                        C = n * NC + q * 4 + k
                        act.wait_ge(ln_cen, nth(ln_cen, C))
                        act.wait_ge(ln_var, nth(ln_var, C - 2))
                        A(sq[:, k % 2, :], ps[:, k, :], ACT.Square).then_inc(ln_sq, 1)

                    square(0)
                    square(1)
                    for k in range(4):
                        C = n * NC + q * 4 + k
                        act.wait_ge(ln_var, nth(ln_var, C))
                        act.wait_ge(ln_rstd, nth(ln_rstd, C - 2))
                        A(logv[:, k % 2, :], ps[:, 4 + k % 2, :], ACT.Ln, bias=acol[:, 3:4]).then_inc(ln_log, 1)
                        if k < 2:
                            square(k + 2)
                        act.wait_ge(ln_log, nth(ln_log, C))
                        act.wait_ge(ln_unit, nth(ln_unit, C - 2))
                        A(rstd[:, k % 2, :], logv[:, k % 2, :], ACT.Exp, scale=-0.5).then_inc(ln_rstd, 1)
                        if hooks and (q, k) in hooks:
                            hooks[q, k]()

                if hooks:
                    quad(0)
                    quad(1)
                else:
                    with act.Fori(0, 2) as q:
                        quad(q)

            def m1(l):
                act.preload_act_table(ACT.Silu)
                with act.Fori(0, NC // 2) as i:
                    for u in range(2):
                        C = l * NC + i * 2 + u
                        for o in range(4):
                            act.wait_ge(m1_psum, nth(m1_psum, C, o))
                            if o == 2:
                                act.wait_ge(m1_gate, nth(m1_gate, C - 2))
                            dst = xi[:, o, ds((i * 2 + u) * CH, CH)] if o < 2 else sres[:, u, o - 2, :]
                            A(dst, ps[:, 4 * u + o, :], ACT.Silu, bias=M("b_in", o, 1)).then_inc(m1_evac, 1)

            def m2(l):
                A(acol[:, 0:1], M("A_log"), ACT.Exp).then_inc(acol_exp, 1)
                act.wait_ge(acol_neg, l + CREDIT + 1)
                act.sem_inc(waited, 1)
                with act.Fori(0, NC // 2) as i:
                    for u in range(2):
                        C = l * NC + i * 2 + u
                        act.wait_ge(m2_dt, nth(m2_dt, C))
                        act.wait_ge(m2_log, nth(m2_log, C - 2))
                        A(absd[:, u, :], ps[:, u, :], ACT.Abs, bias=M("b_dt")).then_inc(m2_abs, 1)
                        act.wait_ge(m2_abs, nth(m2_abs, C))
                        A(absd[:, u, :], absd[:, u, :], ACT.Exp, scale=-1.0).then_inc(m2_exp, 1)
                        act.wait_ge(m2_exp, nth(m2_exp, C))
                        act.wait_ge(m2_delta, nth(m2_delta, C - 2))
                        A(logd[:, u, :], absd[:, u, :], ACT.Ln, bias=1.0).then_inc(m2_log, 1)
                    for u in range(2):
                        C = l * NC + i * 2 + u
                        act.wait_ge(m2_mean, nth(m2_mean, C))
                        act.wait_ge(m2_scan, nth(m2_scan, C - 2))
                        A(adisc[:, u, :], ps[:, 2 + u, 0:SEQ], ACT.Exp, scale=acol[:, 1:2]).then_inc(m2_adisc, 1)

            def m3(l):
                A(acol[:, 2:3], M("Dp"), ACT.Identity, bias=1.0).then_inc(acol_skip, 1)
                act.wait_ge(acol_skip, l + CREDIT + 1)
                act.sem_inc(waited, 1)
                with act.Fori(0, NC // 2) as i:
                    for u in range(2):
                        act.wait_ge(m3_res, nth(m3_res, l * NC + i * 2 + u - 2))
                        A(xd[:, u, :], xa[:, ds((i * 2 + u) * CH, CH)], ACT.Identity, scale=acol[:, 2:3],
                          bias=M("b_out")).then_inc(m3_skip, 1)

            def f(l):
                act.preload_act_table(ACT.Gelu)
                with act.Fori(0, NC // 2) as i:
                    for u in range(2):
                        C = l * NC + i * 2 + u
                        for o in range(4):
                            act.wait_ge(f_h, nth(f_h, C, o))
                            if o % 2 == 0:
                                act.wait_ge(f_acc, nth(f_acc, C - 1, o // 2))
                            A(hid[:, o // 2, o % 2, :], ps[:, o, :], ACT.Gelu, bias=M("b_f1", o, 1)).then_inc(f_g, 1)

            def attention(e, probsparse, part="middle"):
                def high(b):
                    B = e * BATCH + b
                    act.wait_ge(at_proj, nth(at_proj, B, 0))
                    act.wait_ge(at_spill, every(at_spill, B - 1))
                    for dst, bias, at_ in ((qks[:, 0, 0:2, :], "bq", 0), (qks[:, 1, 0:3:2, :], "bk", SEQ)):
                        A(dst, ps[:, 7, at_:at_ + SEQ].unsqueeze(1).broadcast_to([P, 2, SEQ]), ACT.Identity,
                          bias=T(bias)).then_inc(at_hi, 1)

                def minus_max(b, half):
                    B = e * BATCH + b
                    act.wait_ge(at_tp, nth(at_tp, B, half))
                    act.wait_ge(at_mx[half], every(at_mx[half], B - 1))
                    A(mh[:, half, :], ps[0:8, 7, 0:SEQ], ACT.Identity, scale=-1.0).then_inc(at_mh, 1)

                def exps(b, p):
                    B = e * BATCH + b
                    j = p // 2
                    act.wait_ge(at_sc, nth(at_sc, B, p))
                    act.wait_ge(at_pv, nth(at_pv, B, j - 2))
                    A(pt[:, j % 2, 2 * (p % 2):2 * (p % 2) + 2, :, :],
                      ps[:, 2 + 2 * (p % 2):4 + 2 * (p % 2), :], ACT.Exp, scale=QSCALE).then_inc(at_exp, 1)

                def evac(b, j):
                    B = e * BATCH + b
                    act.wait_ge(at_pv, nth(at_pv, B, j))
                    act.wait_ge(at_otp, nth(at_otp, B - 1, 1))
                    A(oraw[:, j, :], ps[:, 6, (j % 2) * SEQ:(j % 2 + 1) * SEQ], ACT.Copy).then_inc(at_oev, 1)

                def columns(b, r):
                    B = e * BATCH + b
                    act.wait_ge(at_aop, nth(at_aop, B - 1))
                    if probsparse:
                        act.wait_ge(at_sel, nth(at_sel, b))
                        A(onT[:], selo[:], ACT.Identity, bias=vmean[:, r:r + 1]).then_inc(at_ob, 1)
                    else:
                        act.wait_ge(at_obp, nth(at_obp, B))
                        A(onT[:], ps[:, 7, 0:SEQ], ACT.Copy).then_inc(at_ob, 1)

                def step(b, third, r, nxt=True, proj=True, first=False):
                    for p in range(8):
                        if p == 7 and not first:
                            columns(b - 1, (r + 2) % 3)
                        exps(b, p)
                        if p == 0 and proj:
                            high(b + 2)
                        if p == 1:
                            if not first:
                                evac(b - 1, 3)
                            minus_max(b, 1)
                        if p in (3, 5, 7):
                            evac(b, p // 2 - 1)
                        if p == 5 and nxt:
                            minus_max(b + 1, 0)

                if part == "begin":
                    return [lambda: high(0), lambda: high(1)]
                if part == "end":
                    return [lambda: columns(15, 0)]

                def last():
                    evac(15, 3)

                minus_max(0, 0)
                sequences(act, step, last)

            def gates(n):
                act.wait_ge(gates_clear, n + 1)
                for row in (0, 32):
                    A(esel[row:row + EXPERTS], ident[0:EXPERTS, 0:EXPERTS].unsqueeze(2)
                      .broadcast_to([EXPERTS, EXPERTS, P]), ACT.Copy)
                act.wait_ge(pe_step, pe_steps[n])
                A(sg[:].rearrange("p t e -> p (t e)"), ps[:, 6, :], ACT.Sigmoid).then_inc(act_step, 1)
                A(w3h[:], G("w3"), ACT.Copy).then_inc(w3_high, 1)
                act.preload_act_table(ACT.Silu)
                split(n, 0, 0)
                for c in range(NC):
                    act.wait_ge(gates_rows, n * NC + c + 1)
                    A(gateT[0:EXPERTS, c * CH:(c + 1) * CH], ps[0:EXPERTS, c, :], ACT.Copy).then_inc(gates_high, 1)

            def split(n, c, u):
                act.wait_ge(e_w, nth(e_w, n * NC + c - 2, BLOCKS - 1))
                A(xh[:, u, :], streams[:, ds(c * CH, CH)], ACT.Copy).then_inc(e_xh, 1)

            def experts(n):
                with act.Fori(0, NC // 2) as i:
                    for u in range(2):
                        C = n * NC + i * 2 + u
                        for k in range(BLOCKS):
                            if k == BLOCKS // 2:
                                split(n, i * 2 + (u + 1), 1 - u)
                            act.wait_ge(e_h, nth(e_h, C, k + 2 * n))
                            act.wait_ge(e_m, nth(e_m, C, k - 2))
                            A(sil[:, k % 2, :], ps[:, k % 2, :], ACT.Silu).then_inc(e_s, 1)
                            for b in {0: (), BLOCKS - 1: (k - 1, k)}.get(k, (k - 1,)):
                                act.wait_ge(e_m, nth(e_m, C, b))
                                act.wait_ge(e_w, nth(e_w, C, b - 4))
                                A(hhh[:, b % 4, :], hh[:, b % 2, :], ACT.Copy).then_inc(e_hi, 1)

            gate(act, SETUP)
            act.preload_act_table_set("natural_log_exp_and_others")
            norm(0)
            gate(act, LN0)
            act.wait_ge(load_g, 32)
            for n, (h_, l_) in enumerate(((w1h, w1l), (w2h, w2l))):
                A(h_[:].rearrange("p k n -> p (k n)"), w12raw[:, n, :], ACT.Copy).then_inc(act_step, 1)
            gate(act, SPLIT)
            with act.Fori(0, LAYERS) as l:
                act.wait_ge(load_m, l * 48 + 48)
                act.sem_inc(waited, 1)
                m1(l)
                act.preload_act_table_set("natural_log_exp_and_others")
                m2(l)
                m3(l)
                act.wait_ge(load_t, l * 16 + 16)
                high = attention(l, False, "begin")
                norm(l * 2 + 1, hooks={(0, 3): high[0], (1, 1): high[1]})
                attention(l, False)
                norm(l * 2 + 2, hooks={(0, 1): attention(l, False, "end")[0]})
                act.wait_ge(load_f, l * 16 + 16)
                act.sem_inc(waited, 1)
                f(l)
            gate(act, STAGE_A)
            act.preload_act_table_set("natural_log_exp_and_others")
            norm(9)
            gates(0)
            experts(0)
            gate(act, EXP_F1)
            act.preload_act_table_set("natural_log_exp_and_others")
            norm(10)
            gate(act, LN_B)
            act.wait_ge(load_t, (LAYERS + 1) * 16)
            act.wait_ge(pe_step, pe_steps["samples"])
            for g in range(2):
                A(ksg[:, 8 * g:8 * g + 8, :], ps[:, g, 0:8 * SC].rearrange("p (b s) -> p b s", s=SC), ACT.Identity,
                  bias=T("bk")).then_inc(sampled, 1)
            with act.Fori(0, BATCH // 2) as i:
                for u in range(2):
                    b = i * 2 + u
                    act.wait_ge(b_q, nth(b_q, b))
                    act.wait_ge(b_s, nth(b_s, b - 2, 1))
                    A(qf[:, u, :], ps[:, u, 0:SEQ], ACT.Identity, bias=T("bq")).then_inc(b_qf, 1)
            gate(act, CHOOSE)
            for step in attention(LAYERS, True, "begin"):
                step()
            attention(LAYERS, True)
            norm(11, hooks={(0, 1): attention(LAYERS, True, "end")[0]})
            gates(1)
            experts(1)
            gate(act, EXP_F2)

        @block.vector
        def _(dve):
            V = nc.vector
            chain = [0]

            def link(ins):
                chain[0] += 1
                ins.then_inc(dve_step, 1)
                dve.wait_ge(dve_step, chain[0])

            def norm(n, dst=None, added=False, gain=None, hooks=None):
                if added:
                    with dve.Fori(0, NC) as c:
                        V.tensor_tensor(res[:, ds(c * CH, CH)], res[:, ds(c * CH, CH)], xa[:, ds(c * CH, CH)],
                                        ALU.add).then_inc(add_res, 1)
                def quad(q):
                    def multiply(k):
                        C = n * NC + q * 4 + k
                        dve.wait_ge(ln_rstd, nth(ln_rstd, C))
                        if dst is None:
                            dve.wait_ge(ln_aff, nth(ln_aff, C - NC - 2))
                            o = unit[:, k % 2, :]
                        else:
                            o = dst[:, ds((q * 4 + k) * CH, CH)]
                        V.tensor_tensor(o, ps[:, k, :], rstd[:, k % 2, :], ALU.mult).then_inc(ln_unit, 1)

                    def affine(k):
                        if dst is None:
                            dve.wait_ge(ln_unit, nth(ln_unit, n * NC + q * 4 + k))
                            V.tensor_scalar(xa[:, ds((q * 4 + k) * CH, CH)], unit[:, k % 2, :], M(gain[0]), M(gain[1]),
                                            ALU.mult, ALU.add).then_inc(ln_aff, 1)
                        if hooks and (q, k) in hooks:
                            hooks[q, k]()

                    def ahead(k):
                        if hooks and ("before", q, k) in hooks:
                            hooks["before", q, k]()
                        multiply(k)

                    ahead(0)
                    for k in range(4):
                        if k < 3:
                            ahead(k + 1)
                        affine(k)

                if hooks:
                    quad(0)
                    quad(1)
                else:
                    with dve.Fori(0, 2) as q:
                        quad(q)

            def parts(c, u, xh_, xl_, high, low, count):
                x = streams[:, ds(c * CH, CH)]
                V.tensor_copy(xh_[:, u, :], x).then_inc(high, 1)
                dve.wait_ge(high, nth(high, count))
                V.tensor_tensor(xl_[:, u, :], x, xh_[:, u, :].bitcast(F32), ALU.subtract).then_inc(low, 1)

            def m1(l):
                with dve.Fori(0, NC // 2) as i:
                    for u in range(2):
                        C = l * NC + i * 2 + u
                        c = i * 2 + u
                        dve.wait_ge(m1_psum, nth(m1_psum, C, 3))
                        parts(c + 2, u, mxh, mxl, m1_xh, m1_xl, l * (NC + 2) + c + 2)
                        dve.wait_ge(m1_evac, nth(m1_evac, C, 3))
                        V.tensor_tensor(zz[:, :, ds(c * CH, CH)], xi[:, :, ds(c * CH, CH)], sres[:, u, :, :],
                                        ALU.mult).then_inc(m1_gate, 1)

            def m2(l):
                dve.wait_ge(acol_exp, nth(acol_exp, l))
                V.tensor_scalar(acol[:, 1:2], acol[:, 0:1], -1.0, None, ALU.mult).then_inc(acol_neg, 1)
                with dve.Fori(0, NC // 2) as i:
                    for u in range(2):
                        C = l * NC + i * 2 + u
                        dve.wait_ge(m2_abs, nth(m2_abs, C))
                        dve.wait_ge(m2_delta, nth(m2_delta, C - 2))
                        V.tensor_scalar(posd[:, u, :], ps[:, u, :], M("b_dt"), 0.0, ALU.add, ALU.max)\
                            .then_inc(m2_pos, 1)
                        dve.wait_ge(m2_u, nth(m2_u, C))
                        dve.wait_ge(m2_scan, nth(m2_scan, C - 2))
                        V.tensor_scalar(uin[:, u, :], ps[:, 4 + u, 0:SEQ], M("b_xp"), None, ALU.add)\
                            .then_inc(m2_uin, 1)
                        dve.wait_ge(m2_pos, nth(m2_pos, C))
                        dve.wait_ge(m2_log, nth(m2_log, C))
                        dve.wait_ge(m2_mean, nth(m2_mean, C - 2))
                        V.tensor_tensor(delta[:, u, :], posd[:, u, :], logd[:, u, :], ALU.add).then_inc(m2_delta, 1)
                    for u in range(2):
                        C = l * NC + i * 2 + u
                        dve.wait_ge(m2_adisc, nth(m2_adisc, C))
                        dve.wait_ge(m2_uin, nth(m2_uin, C))
                        V.tensor_tensor_scan(st[:, ds((i * 2 + u) * SEQ, SEQ)], adisc[:, u, :], uin[:, u, :], 0.0,
                                             ALU.mult, ALU.add).then_inc(m2_scan, 1)

            def m3(l):
                with dve.Fori(0, NC // 4) as i:
                    def gated(k):
                        C = l * NC + i * 4 + k
                        dve.wait_ge(m3_sum, nth(m3_sum, C))
                        dve.wait_ge(m3_out, nth(m3_out, C - 2))
                        V.tensor_tensor(y[:, k % 2, :, :], zz[:, :, ds((i * 4 + k) * CH, CH)],
                                        ps[:, 4 + k % 2, :].unsqueeze(1).broadcast_to([P, 2, CH]), ALU.mult)\
                            .then_inc(m3_y, 1)

                    def add(k):
                        C = l * NC + i * 4 + k
                        dve.wait_ge(m3_out, nth(m3_out, C))
                        dve.wait_ge(m3_skip, nth(m3_skip, C))
                        V.tensor_tensor(xa[:, ds((i * 4 + k) * CH, CH)], ps[:, 6 + k % 2, :], xd[:, k % 2, :], ALU.add)\
                            .then_inc(m3_res, 1)

                    gated(0)
                    gated(1)
                    add(0)
                    gated(2)
                    add(1)
                    gated(3)
                    add(2)
                    add(3)

            def f_parts(l, c):
                dve.wait_ge(ln_aff, nth(ln_aff, l * (2 * NC) + NC + c))
                parts(c, c, fxh, fxl, f_xh, f_xl, l * (NC + 2) + c)

            def f(l):
                def pair(i):
                    for u in range(2):
                        C = l * NC + i * 2 + u
                        c = i * 2 + u
                        dve.wait_ge(f_h, nth(f_h, C, 3))
                        parts(c + 2, u, fxh, fxl, f_xh, f_xl, l * (NC + 2) + c + 2)
                        dve.wait_ge(f_acc, nth(f_acc, C, 1))
                        V.scalar_tensor_tensor(xa[:, ds(c * CH, CH)], ps[:, 4 + u, :], M("b_f2"),
                                               xa[:, ds(c * CH, CH)], ALU.add, ALU.add).then_inc(f_out, 1)

                dve.wait_ge(ln_aff, every(ln_aff, l * (2 * NC) + (2 * NC - 1)))
                pair(0)
                for u in range(2):
                    dve.wait_ge(f_out, nth(f_out, l * NC + u))
                    parts(u, u, mxh, mxl, m1_xh, m1_xl, l * (NC + 2) + (NC + 2 + u))
                with dve.Fori(1, NC // 2) as i:
                    pair(i)

            def attention(e, probsparse, part="middle"):
                stream = res if probsparse else xa

                def low(b, n):
                    B = e * BATCH + b
                    term, bias, at_ = ((2, "bq", 0), (1, "bk", SEQ))[n]
                    dve.wait_ge(at_hi, nth(at_hi, B, 1))
                    V.scalar_tensor_tensor(qks[:, n, term, :], ps[:, 7, at_:at_ + SEQ], T(bias),
                                           qks[:, n, 0, :].bitcast(F32),
                                           ALU.add, ALU.subtract).then_inc(at_lo, 1)

                def lay_v(b, r):
                    B = e * BATCH + b
                    dve.wait_ge(at_proj, nth(at_proj, B, 1))
                    dve.wait_ge(at_pv, nth(at_pv, B - 3, 3))
                    V.tensor_tensor(vx[r][:, :, :, 0:DH],
                                    ps[:, 7, 0:SEQ].rearrange("p (t h d) -> p t h d", t=2, d=DH),
                                    T("bvb").rearrange("p (h d) -> p h d", d=DH).unsqueeze(1)
                                    .broadcast_to([P, 2, HEADS, DH]), ALU.add).then_inc(at_lo, 1)

                def minus_max_low(b, half):
                    B = e * BATCH + b
                    dve.wait_ge(at_mh, nth(at_mh, B, half))
                    V.scalar_tensor_tensor(ml[:, half, :], ps[0:8, 7, 0:SEQ], -1.0, mh[:, half, :].bitcast(F32),
                                           ALU.mult, ALU.subtract).then_inc(at_ml, 1)

                def maxima(b, h, r):
                    B = e * BATCH + b
                    dve.wait_ge(at_am, nth(at_am, B, h))
                    V.tensor_reduce(mxs[:, r, h, :], ps[:, h % 2, :].rearrange("p (t k) -> p t k", t=2), AX.X, ALU.max)\
                        .then_inc(at_max, 1)

                def divide(b, qt):
                    B = e * BATCH + b
                    o = ps[:, 7, :].rearrange("p (h c) -> p h c", c=32)
                    dve.wait_ge(at_otp, nth(at_otp, B, qt))
                    dve.wait_ge(at_ot, nth(at_ot, B, qt - 1))
                    V.reciprocal(rec[:].unsqueeze(2), o[:, :, DH:DH + 1]).then_inc(at_rec, 1)
                    dve.wait_ge(at_rec, nth(at_rec, B, qt))
                    dve.wait_ge(at_obp, nth(at_obp, B - 1))
                    V.tensor_tensor(ontok[:, qt, :].rearrange("p (h d) -> p h d", d=DH), o[:, :, 0:DH],
                                    rec[:].unsqueeze(2).broadcast_to([P, HEADS, DH]), ALU.mult)\
                        .then_inc(at_ot, 1)

                def select(b, r):
                    dve.wait_ge(at_obp, nth(at_obp, e * BATCH + b))
                    dve.wait_ge(at_mask, every(at_mask, b))
                    dve.wait_ge(at_ob, nth(at_ob, e * BATCH + b - 1))
                    V.scalar_tensor_tensor(selo[:], ps[:, 7, 0:SEQ], vmean[:, r:r + 1], maskb[:],
                                           ALU.subtract, ALU.mult).then_inc(at_sel, 1)

                def add_out(b):
                    B = e * BATCH + b
                    dve.wait_ge(at_aop, nth(at_aop, B))
                    V.scalar_tensor_tensor(stream[:, ds(b * SEQ, SEQ)], ps[:, 7, 0:SEQ], T("bo"),
                                           stream[:, ds(b * SEQ, SEQ)], ALU.add, ALU.add).then_inc(at_ao, 1)

                def step(b, third, r, nxt=True, proj=True, first=False):
                    rn = (r + 1) % 3
                    for p in range(8):
                        if p == 0 and probsparse and proj:
                            sum_x(b + 2, (r + 2) % 3)
                        if nxt:
                            maxima(b + 1, 2 * p, rn)
                            maxima(b + 1, 2 * p + 1, rn)
                        if p == 0 and proj:
                            low(b + 2, 0)
                            low(b + 2, 1)
                        if p == 1:
                            minus_max_low(b, 1)
                        if p in (2, 3) and not first:
                            divide(b - 1, p - 2)
                        if p == 4 and proj:
                            lay_v(b + 2, (r + 2) % 3)
                        if p == 5:
                            if nxt:
                                minus_max_low(b + 1, 0)
                            if probsparse:
                                dve.wait_ge(at_vmp, nth(at_vmp, b))
                                dve.wait_ge(at_ob, nth(at_ob, e * BATCH + b - 3))
                                V.tensor_scalar(vmean[:, r:r + 1], ps[:, 7, SEQ:SEQ + 1], 1.0 / SEQ, T("bv"),
                                                ALU.mult, ALU.add).then_inc(at_vm, 1)
                        if p == 6 and probsparse and not first:
                            select(b - 1, (r + 2) % 3)
                        if p == 7 and not first:
                            add_out(b - 1)

                def sum_x(b, r):
                    dve.wait_ge(at_xs, nth(at_xs, e * BATCH + b))
                    V.tensor_reduce(xsum[:, r:r + 1], xs[:], AX.X, ALU.add).then_inc(at_xm, 1)

                def first_low(b):
                    if probsparse:
                        sum_x(b, b)
                    low(b, 0)
                    low(b, 1)

                def last_add():
                    if probsparse:
                        select(15, 0)
                    add_out(15)

                if part == "begin":
                    return [lambda: first_low(0), lambda: lay_v(0, 0), lambda: first_low(1), lambda: lay_v(1, 1)]
                if part == "end":
                    return [lambda: divide(15, 0), lambda: divide(15, 1), last_add]

                for h in range(HEADS):
                    if h == HEADS // 2 + 3:
                        minus_max_low(0, 0)
                    maxima(0, h, 0)
                sequences(dve, step, lambda: None)

            def gates(n):
                dve.wait_ge(act_step, act_steps[n])
                link(V.tensor_tensor(se[:], sg[:], G("ebias").unsqueeze(1).broadcast_to([P, ntile, EXPERTS]), ALU.add))
                for t in range(ntile):
                    last = V.max(m8[:, t, :], se[:, t, :])
                link(last)
                second = m8[:, :, 1:2].broadcast_to([P, ntile, EXPERTS])
                V.tensor_tensor(gt[:], se[:], second, ALU.is_gt)
                link(V.tensor_tensor(eq[:], se[:], second, ALU.is_equal))
                flat = "p t e -> p (t e)"
                link(V.tensor_tensor_scan(cum[:].rearrange(flat), eq[:].rearrange(flat), eq[:].rearrange(flat), 0.0,
                                          ALU.add, ALU.max))
                V.memset(before[:, 0:1], 0.0)
                V.tensor_copy(before[:, 1:ntile], cum[:, 0:ntile - 1, EXPERTS - 1])
                link(V.tensor_reduce(cnt[:], gt[:], AX.X, ALU.add))
                link(V.tensor_tensor(before[:], before[:], cnt[:], ALU.subtract))
                link(V.tensor_tensor(cum[:], cum[:], before[:].unsqueeze(2).broadcast_to([P, ntile, EXPERTS]),
                                     ALU.subtract))
                link(V.scalar_tensor_tensor(eq[:], cum[:], 2.0, eq[:], ALU.is_le, ALU.mult))
                link(V.tensor_tensor(gt[:], gt[:], eq[:], ALU.add))
                V.tensor_tensor(sg[:], sg[:], gt[:], ALU.mult).then_inc(gates_ready, 1)
                dve.wait_ge(e_xh, nth(e_xh, n * NC, n))
                split(n, 0, 0)
                for c in range(NC):
                    dve.wait_ge(gates_high, n * NC + c + 1)
                    last = V.tensor_tensor(gateT[32:32 + EXPERTS, c * CH:(c + 1) * CH], ps[0:EXPERTS, c, :],
                                           gateT[0:EXPERTS, c * CH:(c + 1) * CH].bitcast(F32), ALU.subtract)
                last.then_inc(gates_set, 1)

            def split(n, c, u):
                dve.wait_ge(e_xh, nth(e_xh, n * NC + c, n))
                V.tensor_tensor(xl[:, u, :], streams[:, ds(c * CH, CH)], xh[:, u, :].bitcast(F32), ALU.subtract)\
                    .then_inc(e_xl, 1)

            def experts(n):
                with dve.Fori(0, NC // 2) as i:
                    for u in range(2):
                        C = n * NC + i * 2 + u
                        for k in range(BLOCKS):
                            if k == BLOCKS // 2:
                                split(n, i * 2 + (u + 1), 1 - u)
                            s = k % 2
                            dve.wait_ge(e_s, nth(e_s, C, k))
                            dve.wait_ge(e_g, nth(e_g, C, k + 2 * n))
                            if k < SHARED:
                                dve.wait_ge(e_lo, nth(e_lo, C, k - 2))
                                V.tensor_tensor(hh[:, s, :], ps[:, 2 + s, :], sil[:, s, :], ALU.mult).then_inc(e_m, 1)
                            else:
                                dve.wait_ge(e_m, nth(e_m, C, k - 2))
                                V.tensor_tensor(su[:, s, :], ps[:, 2 + s, :], sil[:, s, :], ALU.mult).then_inc(e_t, 1)
                                dve.wait_ge(e_t, nth(e_t, C, k - SHARED))
                                dve.wait_ge(e_lo, nth(e_lo, C, k - 2))
                                V.tensor_tensor(hh[:, s, :], ps[:, 4 + s, :], su[:, s, :], ALU.mult).then_inc(e_m, 1)
                            out = {(1, SHARED): 0, (1, BLOCKS - 1): 1}.get((u, k))
                            if out is not None:
                                c = i * 2 + out
                                dve.wait_ge(e_w, nth(e_w, n * NC + c, BLOCKS - 1))
                                V.tensor_tensor(res[:, ds(c * CH, CH)], ps[:, 6 + out, :], res[:, ds(c * CH, CH)],
                                                ALU.add).then_inc(e_out, 1)

            def choose():
                dve.wait_ge(load_i, 16)
                link(V.tensor_copy(idx_f[:], idx_i[:]))
                link(V.tensor_scalar(idx_n[:], idx_f[:], 0.0, float(SEQ), ALU.is_lt, ALU.mult))
                link(V.tensor_tensor(idx_f[:], idx_f[:], idx_n[:], ALU.add))
                link(V.tensor_scalar(idx_n[:], idx_f[:], 0.0, float(SEQ - 1), ALU.max, ALU.min))
                V.tensor_copy(idx_c[:], idx_n[:]).then_inc(idx_ready, 1)
                dve.wait_ge(idx_ready, 1)
                xn = xa[:].rearrange("p (b s) -> p b s", s=SEQ)
                with dve.Fori(POOL_FIVES, SAMPLES // 5) as g:
                    at_ = [dve.value_load(idx_c[0:1, ds(g * 5 + k, 1)], min_val=0, max_val=SEQ - 1) for k in range(5)]
                    for k in range(5):
                        V.tensor_copy(xg[:, :, ds(g * 5 + k, 1)], xn[:, :, ds(at_[k], 1)]).then_inc(column_copied, 1)
                dve.wait_ge(column_copied, SAMPLES - 5 * POOL_FIVES)
                dve.wait_ge(taken, 1)
                link(V.tensor_reduce(mxq[:, 0, 0, :].rearrange("p (b o) -> p b o", o=1), xg[:, :, 0:SAMPLES], AX.X,
                                     ALU.add))
                V.tensor_scalar(xg[:, :, SAMPLES], mxq[:, 0, 0, :], 1.0 / SAMPLES, None, ALU.mult)\
                    .then_inc(gathered, 1)
                with dve.Fori(0, BATCH // 2) as i:
                    for u in range(2):
                        b = i * 2 + u
                        for qt in range(2):
                            s = ps[:, 2 + 2 * qt:4 + 2 * qt, 0:8 * SC].rearrange("p g (h s) -> p g h s", s=SC)
                            dve.wait_ge(b_s, nth(b_s, b, qt))
                            dve.wait_ge(b_m, nth(b_m, b - 1, qt))
                            V.tensor_reduce(mxq[:, u, qt, :].rearrange("p (g h) -> p g h", g=2), s[:, :, :, 0:SAMPLES],
                                            AX.X, ALU.max).then_inc(b_mx, 1)
                            dve.wait_ge(b_mx, nth(b_mx, b, qt))
                            V.tensor_tensor(mall[:, qt, ds(b, 1), :].rearrange("p o (g h) -> p (o g) h", g=2),
                                            mxq[:, u, qt, :].rearrange("p (g h) -> p g h", g=2),
                                            s[:, :, :, SAMPLES], ALU.subtract).then_inc(b_m, 1)
                dve.wait_ge(pe_step, pe_steps["rows"])
                V.tensor_copy(mwork[:], ps[:, 6, :].rearrange("p (g q) -> p g q", g=2))
                link(V.tensor_copy(mrow[:], ps[:, 6, :].rearrange("p (g q) -> p g q", g=2)))
                for rnd in range((TOP + 7) // 8):
                    for g in range(2):
                        last = V.max(mtop[:, g, :], mwork[:, g, :])
                    link(last)
                    if 8 * rnd + 8 < TOP:
                        for g in range(2):
                            last = V.match_replace(mwork[:, g, :], mtop[:, g, :], mwork[:, g, :], -3.0e38)
                        link(last)
                least = (TOP - 1) % 8
                for g in range(2):
                    V.tensor_scalar(mgt[:, g, :], mrow[:, g, :], mtop[:, g, least:least + 1], None, ALU.is_gt)
                    last = V.tensor_scalar(meq[:, g, :], mrow[:, g, :], mtop[:, g, least:least + 1], None, ALU.is_equal)
                link(last)
                V.tensor_reduce(mneed[:].unsqueeze(2), mgt[:], AX.X, ALU.add)
                for g in range(2):
                    last = V.tensor_tensor_scan(mcum[:, g, :], meq[:, g, :], meq[:, g, :], 0.0, ALU.add, ALU.max)
                link(last)
                link(V.tensor_scalar(mneed[:], mneed[:], -1.0, float(TOP), ALU.mult, ALU.add))
                for g in range(2):
                    last = V.scalar_tensor_tensor(mcum[:, g, :], mcum[:, g, :], mneed[:, g:g + 1], meq[:, g, :],
                                                  ALU.is_le, ALU.mult)
                link(last)
                V.tensor_tensor(mwork[:], mgt[:], mcum[:], ALU.add).then_inc(mask_ready, 1)

            V.memset(acol[:, 3:4], EPS)
            V.memset(acol[:, 4:5], 0.0)
            gate(dve, SETUP)
            norm(0, xa)
            gate(dve, LN0)
            for n, (h_, l_) in enumerate(((w1h, w1l), (w2h, w2l))):
                dve.wait_ge(act_step, n + 1)
                V.tensor_tensor(l_[:].rearrange("p k n -> p (k n)"), w12raw[:, n, :],
                                h_[:].rearrange("p k n -> p (k n)").bitcast(F32), ALU.subtract)
            gate(dve, SPLIT)
            for u in range(2):
                parts(u, u, mxh, mxl, m1_xh, m1_xl, u)
            with dve.Fori(0, LAYERS) as l:
                dve.wait_ge(load_m, l * 48 + 48)
                dve.sem_inc(waited, 1)
                m1(l)
                m2(l)
                m3(l)
                dve.wait_ge(load_f, l * 16 + 16)
                dve.sem_inc(waited, 1)
                dve.wait_ge(load_t, l * 16 + 16)
                dve.sem_inc(waited, 1)
                dve.wait_ge(pool_step, l * 3 + CLEARED)
                begin = attention(l, False, "begin")
                norm(l * 2 + 1, gain=("g1", "be1"),
                     hooks={(0, 3): begin[0], ("before", 1, 1): begin[1], (1, 1): begin[2], (1, 2): begin[3]})
                attention(l, False)
                end = attention(l, False, "end")
                norm(l * 2 + 2, gain=("g2", "be2"),
                     hooks={("before", 0, 0): end[0], ("before", 0, 1): end[1], (0, 2): end[2],
                            (1, 0): lambda: f_parts(l, 0), (1, 1): lambda: f_parts(l, 1)})
                f(l)
            gate(dve, STAGE_A)
            norm(9, xa, added=True)
            dve.wait_ge(load_g, 32)
            gates(0)
            experts(0)
            gate(dve, EXP_F1)
            norm(10, xa)
            gate(dve, LN_B)
            dve.wait_ge(load_t, (LAYERS + 1) * 16)
            choose()
            gate(dve, CHOOSE)
            for step in attention(LAYERS, True, "begin"):
                step()
            attention(LAYERS, True)
            end = attention(LAYERS, True, "end")
            norm(11, xa, hooks={("before", 0, 0): end[0], ("before", 0, 1): end[1], (0, 0): end[2]})
            gates(1)
            experts(1)
            gate(dve, EXP_F2)

        @block.gpsimd
        def _(pool):
            G_ = nc.gpsimd

            def weight_parts(high, low, w, step, ready):
                G_.tensor_copy(high[:], w).then_inc(split_step, 1)
                pool.wait_ge(split_step, step)
                pool.sem_inc(waited, 1)
                G_.tensor_tensor(low[:], w, high[:].bitcast(F32), ALU.subtract).then_inc(ready, 1)

            def clear_queries():
                for r in range(2):
                    G_.memset(qv[r][:].bitcast(F32), 0.0)

            def clear_operands(n):
                for r in range(3):
                    G_.memset(vx[r][:], 0.0)
                G_.memset(qv[2][:].bitcast(F32), 0.0).then_inc(pool_step, 1)
                pool.wait_ge(pool_step, n * 3 + 3)
                pool.sem_inc(waited, 1)
                for r in range(3):
                    last = G_.memset(vx[r][:, :, :, DH:DH + 1], 1.0)
                last.then_inc(pool_step, 1)
                pool.wait_ge(pool_step, n * 3 + 4)
                pool.sem_inc(waited, 1)
                for r in range(3):
                    last = G_.memset(k4[r][96:P].bitcast(F32), 1.0)
                last.then_inc(pool_step, 1)
                pool.wait_ge(pool_step, n * 3 + 5)
                pool.sem_inc(waited, 1)

            def attention(e, probsparse):
                with pool.Fori(0, BATCH // 2) as i:
                    for u in range(2):
                        b = i * 2 + u
                        if not probsparse and u == 0:
                            pool.wait_ge(ln_aff, nth(ln_aff, e * (2 * NC) + i))
                        pool.wait_ge(at_proj, nth(at_proj, e * BATCH + b - 1, 1))
                        G_.tensor_copy(xs[:], xa[:, ds(b * SEQ, SEQ)]).then_inc(at_xs, 1)

            def clear_gates():
                G_.memset(gateT[:].bitcast(F32), 0.0)
                G_.memset(esel[:].bitcast(F32), 0.0).then_inc(gates_clear, 1)

            def experts(n):
                pool.wait_ge(w3_high, n + 1)
                G_.tensor_tensor(w3l[:], G("w3"), w3h[:].bitcast(F32), ALU.subtract).then_inc(w3_set, 1)
                with pool.Fori(0, NC // 2) as i:
                    for u in range(2):
                        for k in range(BLOCKS):
                            pool.wait_ge(e_hi, nth(e_hi, n * NC + i * 2 + u, k))
                            G_.tensor_tensor(hhl[:, k % 4, :], hh[:, k % 2, :], hhh[:, k % 4, :].bitcast(F32),
                                             ALU.subtract).then_inc(e_lo, 1)

            def diagonal(t, value):
                G_.affine_select(out=t, in_=t, compare_op=ALU.not_equal, fill=value, base=0, pattern=[[-1, P]],
                                 channel_multiplier=1)

            G_.memset(wxp[:], 0.0)
            G_.memset(ident[:], 0.0)
            G_.memset(center[:], -1.0 / P)
            G_.memset(average[:], 1.0 / P)
            G_.memset(halfavg[:], 0.0)
            G_.memset(halfsum[:], 0.0).then_inc(setup_done, 1)
            pool.wait_ge(setup_done, 1)
            diagonal(ident[:], 1.0)
            diagonal(center[:], 1.0 - 1.0 / P)
            for hb in range(2):
                G_.memset(halfavg[:, hb, hb * STATES:(hb + 1) * STATES], 1.0 / P)
            for hb in range(2):
                pool.drain().then_inc(pool_step, 1)
                pool.wait_ge(pool_step, hb + 1)
                G_.memset(halfsum[hb * STATES:(hb + 1) * STATES, hb, :], 1.0)
            gate(pool, SETUP)
            gate(pool, LN0)
            gate(pool, SPLIT)
            pool.wait_ge(load_m, 48)
            weight_parts(winh, winl, M("win"), 1, win_set)
            with pool.Fori(0, LAYERS) as l:
                pool.wait_ge(m2_u, every(m2_u, l * NC + (NC - 1)))
                pool.sem_inc(waited, 1)
                clear_queries()
                pool.wait_ge(m3_y, every(m3_y, l * NC + (NC - 1)))
                pool.sem_inc(waited, 1)
                clear_operands(l)
                attention(l, False)
                pool.wait_ge(load_f, l * 16 + 16)
                pool.sem_inc(waited, 1)
                pool.wait_ge(at_ao, every(at_ao, l * BATCH + (BATCH - 1)))
                pool.sem_inc(waited, 1)
                weight_parts(wf1h, wf1l, M("wf1"), l * 2 + 2, wf1_set)
                pool.wait_ge(load_m, l * 48 + 96)
                pool.sem_inc(waited, 1)
                weight_parts(winh, winl, M("win"), l * 2 + 3, win_set)
            gate(pool, STAGE_A)
            clear_gates()
            experts(0)
            gate(pool, EXP_F1)
            clear_queries()
            clear_operands(LAYERS)
            gate(pool, LN_B)
            G_.memset(headmask[:], 1.0).then_inc(pool_step, 1)
            pool.wait_ge(pool_step, 3 * LAYERS + 6)
            G_.affine_select(out=headmask[:], in_=headmask[:], compare_op=ALU.is_ge, fill=0.0, base=0,
                             pattern=[[-DH, HEADS]], channel_multiplier=1).then_inc(pool_step, 1)
            pool.wait_ge(pool_step, 3 * LAYERS + 7)
            G_.affine_select(out=headmask[:], in_=headmask[:], compare_op=ALU.is_ge, fill=0.0, base=DH - 1,
                             pattern=[[DH, HEADS]], channel_multiplier=-1)
            pool.wait_ge(idx_ready, 1)
            xn = xa[:].rearrange("p (b s) -> p b s", s=SEQ)
            with pool.Fori(0, POOL_FIVES) as g:
                at_ = [pool.value_load(idx_c[0:1, ds(g * 5 + k, 1)], min_val=0, max_val=SEQ - 1) for k in range(5)]
                for k in range(5):
                    G_.tensor_copy(xg[:, :, ds(g * 5 + k, 1)], xn[:, :, ds(at_[k], 1)]).then_inc(column_taken, 1)
            pool.wait_ge(column_taken, 5 * POOL_FIVES)
            pool.sem_inc(taken, 1)
            pool.wait_ge(sampled, 2)
            with pool.Fori(0, BATCH // 2) as i:
                for u in range(2):
                    b = i * 2 + u
                    pool.wait_ge(b_s, nth(b_s, b - 2, 1))
                    G_.tensor_tensor(kbd[:, u], ksg[:, ds(b, 1), :].broadcast_to([P, HEADS, SC]),
                                     headmask[:].unsqueeze(2).broadcast_to([P, HEADS, SC]), ALU.mult)\
                      .then_inc(b_kbd, 1)
            gate(pool, CHOOSE)
            attention(LAYERS, True)
            pool.wait_ge(at_ao, every(at_ao, LAYERS * BATCH + (BATCH - 1)))
            clear_gates()
            experts(1)
            gate(pool, EXP_F2)


def kernel(**inputs):
    import numpy as np
    import concourse.bacc as bacc
    from concourse.bass_utils import run_bass_kernel_spmd

    a = {k[len("L0_"):]: np.asarray(v) for k, v in inputs.items()}
    m = {k[len("attn_a_"):]: v for k, v in a.items() if k.startswith("attn_a_")}
    b = {k[len("attn_b_"):]: v for k, v in a.items() if k.startswith("attn_b_")}
    g = {k[len("ffn_"):]: v for k, v in a.items() if k.startswith("ffn_")}

    def fill(out, table, **parts):
        for name, part in parts.items():
            at, n = table[name]
            out[:, at:at + n] = np.asarray(part).reshape(P, n)

    def blocks(w):
        return w.T.reshape(-1, P, w.shape[0]).transpose(1, 0, 2)

    def columns(v):
        return v.reshape(-1, P).T

    mws = np.zeros((LAYERS + 1, P, MCOLS), np.float32)
    xps = np.zeros((LAYERS + 1, P, 2, STATES), np.float32)
    tws = np.zeros((LAYERS + 1, P, TCOLS), np.float32)
    for l in range(LAYERS):
        fill(mws[l], MW, win=m["W_in"][l].T, wdt=blocks(m["W_dt"][l]), wout=blocks(m["W_out"][l]), wf1=m["W_f1"][l].T,
             wf2=blocks(m["W_f2"][l]), b_in=columns(m["b_in"][l]), b_dt=m["b_dt"][l], b_xp=np.tile(m["b_xp"][l], 2),
             b_out=m["b_out"][l], Dp=m["Dp"][l], A_log=np.tile(m["A_log"][l], 2), g1=m["g1"][l], be1=m["be1"][l],
             g2=m["g2"][l], be2=m["be2"][l], b_f1=columns(m["b_f1"][l]), b_f2=m["b_f2"][l])
        xps[l] = blocks(m["W_xp"][l])
        wq, wk, wv = (m["W_qkv"][l][k * D:(k + 1) * D].T for k in range(3))
        bq, bk, bv = (m["b_qkv"][l][k * D:(k + 1) * D] for k in range(3))
        fill(tws[l], TW, wq=wq, wk=wk, wv=wv, wo=m["W_ao"][l].T, bq=bq, bk=bk, bo=m["b_ao"][l], bv=bv,
             bvb=np.broadcast_to(bv, (P, D)))
    mws[LAYERS], xps[LAYERS] = mws[LAYERS - 1], xps[LAYERS - 1]
    fill(tws[LAYERS], TW, wq=b["Wq"].T, wk=b["Wk"].T, wv=b["Wv"].T, wo=b["Wo"].T, bq=b["bq"], bk=b["bk"], bo=b["bo"],
         bv=b["bv"], bvb=np.broadcast_to(b["bv"], (P, D)))
    w12 = np.stack([np.concatenate([g[f"shared_w{k}"][0], g[f"routed_w{k}"].transpose(1, 0, 2).reshape(P, -1)], 1)
                    for k in (1, 2)], 1)
    gws = np.zeros((P, GCOLS), np.float32)
    w3 = np.concatenate([g["shared_w3"][0].reshape(SHARED, P, D), g["routed_w3"]], 0).transpose(1, 0, 2)
    fill(gws, GW, w3=w3, router=g["router_w"], ebias=np.broadcast_to(g["expert_bias"], (P, EXPERTS)))
    arrays = {
        "x_in": np.ascontiguousarray(m["x"].reshape(TOK, D).T), "mw_in": mws, "xp_in": xps, "tw_in": tws,
        "w12_in": np.ascontiguousarray(w12), "gw_in": gws,
        "idx_in": np.ascontiguousarray(np.broadcast_to(b["sample_idx"], (P, SAMPLES))),
    }
    nc = bacc.Bacc("TRN2", target_bir_lowering=False, num_devices=1)
    args = [nc.dram_tensor(n, v.shape, mybir.dt.from_np(v.dtype), kind="ExternalInput").ap() for n, v in arrays.items()]
    args.append(nc.dram_tensor("out", (P, TOK), F32, kind="ExternalOutput").ap())
    build_program(nc, *args)
    r = run_bass_kernel_spmd(nc, [arrays], core_ids=[0])
    return r.results[0]["out"].T.reshape(BATCH, SEQ, D)
```
